# Optimizing a Trainium2 kernel written in Bass

```python
import numpy as np
import jax
import jax.numpy as jnp

def _softmax(x, axis=-1):
    return jax.nn.softmax(x, axis=axis)

def _gelu(x):
    return jax.nn.gelu(x, approximate=True)

def _silu(x):
    return jax.nn.silu(x)

def _sigmoid(x):
    return jax.nn.sigmoid(x)

def _layernorm(x, axis=-1, eps=1e-05):
    m = jnp.mean(x, axis=axis, keepdims=True)
    v = jnp.var(x, axis=axis, keepdims=True)
    return (x - m) / jnp.sqrt(v + eps)

def _scatter_add(tgt, idx, src, axis=0):
    return tgt.at[idx].add(src)

def _segment_sum(src, seg, n):
    return jax.ops.segment_sum(src, seg, n)
kernel_name = 'mk_gnn_resnorm_d2_gnn_r32_663407'

def setup_inputs(seed: int=0):
    np.random.seed(seed)
    _w = jnp.asarray

    def _rec_inputs():
        import jax
        import jax.numpy as jnp
        _gk = jax.random.key(seed)
        x = -0.0002928 + 1 * jax.random.normal(jax.random.fold_in(_gk, 1), (3125, 256), jnp.float32)
        src = jax.random.randint(jax.random.fold_in(_gk, 2), (50000,), 0, 3125, jnp.int32)
        dst = jnp.minimum((3125 * jax.random.uniform(jax.random.fold_in(_gk, 3), (50000,)) ** 2.0).astype(jnp.int32), 99999)
        _o = jnp.argsort(dst, stable=True)
        src = src[_o]
        dst = dst[_o]
        edge_attr_128 = -1.52775e-05 + 0.999936 * jax.random.normal(jax.random.fold_in(_gk, 12), (50000, 128), jnp.float32)
        edge_weight = jax.random.uniform(jax.random.fold_in(_gk, 14), (50000,), jnp.float32, 0.0, 0.999998)
        return (x, src, dst, edge_attr_128, edge_weight)
    x, src, dst, edge_attr_128, edge_weight = _rec_inputs()

    def _L0_gnn_setup():
        import jax, jax.numpy as jnp
        import numpy as np
        N_NODES = 512
        N_EDGES = 8192
        D_NODE = 256
        D_EDGE = 128
        OUT_DIM = 256
        N_LAYERS = 3

        def _auto_mlp_dims(inp_dim, out_dim, n_layers):
            dims = np.logspace(np.log(inp_dim), np.log(out_dim), n_layers + 1, base=np.e)
            return [int(d) for d in np.round(dims)[1:]]

        def _segment_mean(data, seg, num_segments):
            s = jax.ops.segment_sum(data, seg, num_segments=num_segments, indices_are_sorted=True)
            c = jax.ops.segment_sum(jnp.ones((data.shape[0], 1), data.dtype), seg, num_segments=num_segments, indices_are_sorted=True)
            return s / jnp.maximum(c, 1.0)
        key = jax.random.key(seed)
        ks = jax.random.split(key, 12)
        n_embed = jax.random.normal(ks[0], (N_NODES, D_NODE), dtype=jnp.float32)
        e_embed = jax.random.normal(ks[1], (N_EDGES, D_EDGE), dtype=jnp.float32)
        senders = jnp.sort(jax.random.randint(ks[2], (N_EDGES,), 0, N_NODES))
        receivers = jax.random.randint(ks[3], (N_EDGES,), 0, N_NODES)
        dims = _auto_mlp_dims(2 * D_NODE, OUT_DIM, N_LAYERS)
        in_dims = [2 * D_NODE] + dims[:-1]
        params = {}
        for i, (di, do) in enumerate(zip(in_dims, dims)):
            params[f'W{i}'] = jax.random.normal(ks[4 + i], (di, do), dtype=jnp.float32) / np.sqrt(di)
            params[f'b{i}'] = jnp.zeros((do,), dtype=jnp.float32)
        params['Wg'] = jax.random.normal(ks[10], (D_EDGE, dims[-1]), dtype=jnp.float32) / np.sqrt(D_EDGE)
        return dict(n_embed=n_embed, e_embed=e_embed, senders=senders, receivers=receivers, **params)
    _L0_gnn_all = _L0_gnn_setup()
    _L0_gnn_in = {k: v for k, v in _L0_gnn_all.items() if k in ('W0', 'b0', 'W1', 'b1', 'W2', 'b2', 'Wg')}
    del _L0_gnn_all

    def _L1_gnn_setup():
        import jax, jax.numpy as jnp
        import numpy as np
        N_NODES = 50000
        N_EDGES = 25000
        IN_F = 256
        OUT_F = 64
        HEADS = 4
        NEG_SLOPE = 0.2
        key = jax.random.key(seed)
        ks = jax.random.split(key, 6)
        x = jax.random.normal(ks[0], (N_NODES, IN_F), dtype=jnp.float32)
        edge_index = jax.random.randint(ks[1], (2, N_EDGES), 0, N_NODES, dtype=jnp.int32)
        edge_weight = jax.random.uniform(ks[2], (N_EDGES,), dtype=jnp.float32)
        gain = float(np.sqrt(2.0 / (1.0 + NEG_SLOPE ** 2)))
        w_bound = gain * np.sqrt(6.0 / (IN_F + OUT_F))
        a_bound = gain * np.sqrt(6.0 / (OUT_F + 1))
        W = jax.random.uniform(ks[3], (HEADS, IN_F, OUT_F), minval=-w_bound, maxval=w_bound, dtype=jnp.float32)
        a_src = jax.random.uniform(ks[4], (HEADS, OUT_F, 1), minval=-a_bound, maxval=a_bound, dtype=jnp.float32)
        a_dst = jax.random.uniform(ks[5], (HEADS, OUT_F, 1), minval=-a_bound, maxval=a_bound, dtype=jnp.float32)
        return {'x': x, 'edge_index': edge_index, 'edge_weight': edge_weight, 'W': W, 'a_src': a_src, 'a_dst': a_dst}
    _L1_gnn_all = _L1_gnn_setup()
    _L1_gnn_in = {k: v for k, v in _L1_gnn_all.items() if k in ('W', 'a_src', 'a_dst')}
    del _L1_gnn_all
    return {'x': x, 'src': src, 'dst': dst, 'edge_attr_128': edge_attr_128, 'edge_weight': edge_weight, 'L0_gnn_W0': _L0_gnn_in['W0'], 'L0_gnn_b0': _L0_gnn_in['b0'], 'L0_gnn_W1': _L0_gnn_in['W1'], 'L0_gnn_b1': _L0_gnn_in['b1'], 'L0_gnn_W2': _L0_gnn_in['W2'], 'L0_gnn_b2': _L0_gnn_in['b2'], 'L0_gnn_Wg': _L0_gnn_in['Wg'], 'L1_gnn_W': _L1_gnn_in['W'], 'L1_gnn_a_src': _L1_gnn_in['a_src'], 'L1_gnn_a_dst': _L1_gnn_in['a_dst']}

def reference(x, src, dst, edge_attr_128, edge_weight, L0_gnn_W0, L0_gnn_b0, L0_gnn_W1, L0_gnn_b1, L0_gnn_W2, L0_gnn_b2, L0_gnn_Wg, L1_gnn_W, L1_gnn_a_src, L1_gnn_a_dst):
    import jax
    import jax.numpy as jnp

    def _L0_gnn_ref(n_embed, e_embed, senders, receivers, W0, b0, W1, b1, W2, b2, Wg):
        import jax, jax.numpy as jnp
        import numpy as np
        N_NODES = 512
        N_EDGES = 8192
        D_NODE = 256
        D_EDGE = 128
        OUT_DIM = 256
        N_LAYERS = 3

        def _auto_mlp_dims(inp_dim, out_dim, n_layers):
            dims = np.logspace(np.log(inp_dim), np.log(out_dim), n_layers + 1, base=np.e)
            return [int(d) for d in np.round(dims)[1:]]

        def _segment_mean(data, seg, num_segments):
            s = jax.ops.segment_sum(data, seg, num_segments=num_segments, indices_are_sorted=True)
            c = jax.ops.segment_sum(jnp.ones((data.shape[0], 1), data.dtype), seg, num_segments=num_segments, indices_are_sorted=True)
            return s / jnp.maximum(c, 1.0)
        h = jnp.concatenate([n_embed[senders], n_embed[receivers]], axis=-1)
        h = jnp.tanh(h @ W0 + b0)
        h = jnp.tanh(h @ W1 + b1)
        h = h @ W2 + b2
        h = h * (e_embed @ Wg)
        return _segment_mean(h, senders, n_embed.shape[0])

    def _L1_gnn_ref(x, edge_index, edge_weight, W, a_src, a_dst):
        import jax, jax.numpy as jnp
        import numpy as np
        N_NODES = 50000
        N_EDGES = 25000
        IN_F = 256
        OUT_F = 64
        HEADS = 4
        NEG_SLOPE = 0.2
        num_nodes = x.shape[0]
        h = jnp.einsum('ni,hio->hno', x, W)
        attn_src = jnp.einsum('hno,hod->hn', h, a_src)
        attn_dst = jnp.einsum('hno,hod->hn', h, a_dst)
        src_idx, dst_idx = (edge_index[0], edge_index[1])
        e = attn_src[:, src_idx] + attn_dst[:, dst_idx]
        e = jnp.where(e >= 0, e, NEG_SLOPE * e)
        e = e * edge_weight[None, :]
        e_exp = jnp.exp(e - jnp.max(e))
        denom = jax.ops.segment_sum(e_exp.T, dst_idx, num_segments=num_nodes).T
        alpha = e_exp / (denom[:, dst_idx] + 1e-10)
        msg = h[:, src_idx] * alpha[..., None]
        out = jax.vmap(lambda m: jax.ops.segment_sum(m, dst_idx, num_segments=num_nodes))(msg)
        return jnp.transpose(out, (1, 0, 2)).reshape(num_nodes, HEADS * OUT_F)
    edge_index = jnp.stack([src, dst])
    x = _layernorm(x + _L0_gnn_ref(x, edge_attr_128, src, dst, L0_gnn_W0, L0_gnn_b0, L0_gnn_W1, L0_gnn_b1, L0_gnn_W2, L0_gnn_b2, L0_gnn_Wg), axis=-1)
    x = _layernorm(x + _L1_gnn_ref(x, edge_index, edge_weight, L1_gnn_W, L1_gnn_a_src, L1_gnn_a_dst), axis=-1)
    return x

_drawn_inputs = setup_inputs


def setup_inputs(seed=0):
    import zlib

    import numpy as np

    out = dict(_drawn_inputs(seed))
    spreads = {'L0_gnn_b0': (0.0, 0.446), 'L0_gnn_b1': (0.0, 0.297), 'L0_gnn_b2': (0.0, 0.1)}
    factors = {}
    for name, (base, spread) in spreads.items():
        noise = np.random.default_rng([zlib.crc32(name.encode()), seed]).standard_normal(out[name].shape)
        drawn = base * np.exp(spread * noise) if base else spread * noise
        out[name] = jnp.asarray(drawn.astype(out[name].dtype))
    for name, factor in factors.items():
        out[name] = (out[name] * factor).astype(out[name].dtype)
    return out
```

```python
import numpy as np
import concourse.bass as bass
from concourse import mybir
from concourse.alu_op_type import AluOpType as ALU
from contextlib import ExitStack


P = 128
BLOCKS_PER_GROUP = 4
TABLES = 3
Y_RING = 2 * TABLES
NEG_SLOPE = 0.2
LN_EPS = 1e-5
DENOM_EPS = 1e-10
LOWEST = -3.0e38


def build_program(nc, xT, x, src_cols, dst_cols, src_row, dst_row, eT, w_cols,
                  W0, b0, W1, b1, W2, b2, Wg, Wcat, WcatT, a_src, a_dst, out):
    f32, f32r, bf16, i32 = mybir.dt.float32, mybir.dt.float32r, mybir.dt.bfloat16, mybir.dt.int32
    ACT, AX = mybir.ActivationFunctionType, mybir.AxisListType

    D, N = xT.shape
    E = src_row.shape[0]
    H0, H1, OUT = W0.shape[1], W1.shape[1], W2.shape[1]
    HEADS, HD = a_src.shape[0], a_src.shape[1]
    DK = D // P
    NT = -(-N // P)
    NB = -(-E // P)
    NG = -(-NB // BLOCKS_PER_GROUP)
    GE = BLOCKS_PER_GROUP * P
    NPAIR = -(-NB // 2)
    C1 = -(-H0 // P)
    K1 = -(-H0 // C1)
    C2 = -(-H1 // P)
    K2 = -(-H1 // C2)
    AW = OUT + 2
    BW = OUT + HEADS
    TR = (NT + 1) * P
    TQ = NT * HEADS
    RQ = 125
    QC = E // RQ
    assert D % P == 0 and N + P <= TR and E % RQ == 0 and TQ <= P and HEADS == 4

    def rows_of_tile(t):
        return min(P, N - t * P)

    def rows_of_block(b):
        return min(P, E - b * P)

    def blocks_of_group(g):
        return range(g * BLOCKS_PER_GROUP, min((g + 1) * BLOCKS_PER_GROUP, NB))

    def blocks_of_pair(q):
        return range(2 * q, min(2 * q + 2, NB))

    def pairs_of_group(g):
        return range(2 * g, min(2 * g + 2, NPAIR))

    def edges_of_group(g):
        return min(GE, E - g * GE)

    def k1(c):
        return min(K1, H0 - c * K1)

    def k2(m):
        return min(K2, H1 - m * K2)

    def same_rows(blocks):
        full = [b for b in blocks if rows_of_block(b) == P]
        return [r for r in (full, [b for b in blocks if rows_of_block(b) < P]) if r]

    ctx = ExitStack()
    with ctx:
        def sb(name, shape, dt=f32, scope=ctx):
            return scope.enter_context(nc.sbuf_tensor(name, shape, dt))

        def sem(name):
            return ctx.enter_context(nc.semaphore(name))

        TA = nc.dram_tensor("TA", [N, H0], f32).ap()
        TB = nc.dram_tensor("TB", [N, H0], f32).ap()
        HT = nc.dram_tensor("HT", [N, OUT], f32).ap()
        RQD = nc.dram_tensor("RQD", [4, E], bf16).ap()
        accA = [nc.dram_tensor(f"accA{k}", [TR, AW], f32).ap() for k in range(TABLES)]
        accB = [nc.dram_tensor(f"accB{k}", [TR, BW], f32).ap() for k in range(TABLES)]

        ident = sb("ident", [P, P])
        lower = sb("lower", [P, P])
        iota_row = sb("iota_row", [P, P])
        iota_i = sb("iota_i", [P, P], i32)
        p_i = sb("p_i", [P, 1], i32)
        p_f = sb("p_f", [P, 1])
        q_i = sb("q_i", [P, 1], i32)
        q_of_p = sb("q_of_p", [P, 1])
        h_i = sb("h_i", [P, 1], i32)
        h_of_p = sb("h_of_p", [P, 1])
        select = sb("select", [P, HEADS])
        trash = sb("trash", [P, 1])
        src_c = sb("src_c", [P, NB], i32)
        dst_c = sb("dst_c", [P, NB], i32)
        src_f = sb("src_f", [P, NB])
        dst_f = sb("dst_f", [P, NB])
        src_t = sb("src_t", [P, NB])
        dst_t = sb("dst_t", [P, NB])
        dup = sb("dup", [P, NB])
        to_a = sb("to_a", [P, NB], i32)
        to_b = sb("to_b", [P, NB], i32)
        to_f = sb("to_f", [P, BLOCKS_PER_GROUP])
        w_c = sb("w_c", [P, NB])
        xn = sb("xn", [P, NT, D])
        mv = sb("mv", [P, NT, 2])
        std = sb("std", [P, NT])
        rstd = sb("rstd", [P, NT])
        eps = sb("eps", [P, 1])
        zeros = sb("zeros", [P, BW])
        ystage = sb("ystage", [P, Y_RING, BW])
        bcast_i = sb("bcast_i", [P, 2, GE], i32)

        sa = ExitStack()
        W1h = sb("W1h", [K1, C1, H1], f32r, sa)
        W1l = sb("W1l", [K1, C1, H1], f32r, sa)
        W2h = sb("W2h", [K2, C2, OUT], f32r, sa)
        W2l = sb("W2l", [K2, C2, OUT], f32r, sa)
        Wgh = sb("Wgh", [P, OUT], f32r, sa)
        Wgl = sb("Wgl", [P, OUT], f32r, sa)
        b1c = sb("b1c", [K2, C2], f32, sa)
        GAR, GBR = 3, 2
        sn = ExitStack()
        xTf = sb("xTf", [P, DK, N], f32, sn)
        xTh = sb("xTh", [P, DK, N], f32r, sn)
        xTl = sb("xTl", [P, DK, N], f32r, sn)
        W0f = sb("W0f", [P, 2 * DK, H0], f32, sn)
        W0h = sb("W0h", [P, 2 * DK, H0], f32r, sn)
        W0l = sb("W0l", [P, 2 * DK, H0], f32r, sn)
        b0b = sb("b0b", [P, H0], f32, sn)
        N0R = 4
        stA = sb("stA", [P, N0R, H0], f32, sn)
        stB = sb("stB", [P, N0R, H0], f32, sn)
        idx_rows = sb("idx_rows", [RQ, 2, QC], i32, sn)
        rq_i = sb("rq_i", [RQ, 4, QC], i32, sn)
        rq_b = sb("rq_b", [RQ, 4, QC], bf16, sn)
        W1f = sb("W1f", [K1, C1, H1], f32, sn)
        W2f = sb("W2f", [K2, C2, OUT], f32, sn)
        Wgf = sb("Wgf", [P, OUT], f32, sn)
        sn.close()
        GA = sb("GA", [P, GAR * BLOCKS_PER_GROUP, H0], f32, sa)
        GB = sb("GB", [P, GBR * BLOCKS_PER_GROUP, H0], f32, sa)
        h1f = sb("h1f", [K1, C1, GE], f32, sa)
        h1h = sb("h1h", [K1, 2, C1, GE], f32r, sa)
        h1l = sb("h1l", [K1, 2, C1, GE], f32r, sa)
        h2f = sb("h2f", [K2, C2, GE], f32, sa)
        h2h = sb("h2h", [K2, 2, C2, GE], f32r, sa)
        h2l = sb("h2l", [K2, 2, C2, GE], f32r, sa)
        ef = sb("ef", [P, 2, GE], f32, sa)
        eh = sb("eh", [P, 2, GE], f32r, sa)
        el = sb("el", [P, 2, GE], f32r, sa)
        gate = sb("gate", [P, 2, 2, OUT], f32, sa)
        mf = sb("mf", [P, 2, 2, OUT], f32, sa)
        mh = sb("mh", [P, 2, 2, AW], f32r, sa)
        ml = sb("ml", [P, 2, 2, AW], f32r, sa)
        EQR = 2 * BLOCKS_PER_GROUP
        eqA = sb("eqA", [P, EQR, P], f32r, sa)
        eq_low = sb("eq_low", [P, 2, P], f32, sa)
        sa.close()

        sc = ExitStack()
        TSR = 4
        tab = sb("tab", [P, TSR, TABLES, BW], f32, sc)
        tsum = sb("tsum", [P, 2, 2, BW], f32, sc)
        cinv = sb("cinv", [P, NT, HEADS], f32, sc)
        cden = sb("cden", [P, NT, HEADS], f32, sc)
        att = sb("att", [P, 2, OUT], f32, sc)
        stats = sb("stats", [P, NT, 6], f32, sc)
        x1T = sb("x1T", [P, 2, DK, P], f32, sc)
        Wc = sb("Wc", [P, DK, OUT + 2 * HEADS], f32, sc)
        WcT = sb("WcT", [P, DK, OUT], f32, sc)
        ablk = sb("ablk", [P, DK, 2 * HEADS], f32, sc)
        hst = sb("hst", [P, 4, OUT], f32, sc)
        score_h = sb("score_h", [P, 2, NT, HEADS], f32r, sc)
        score_l = sb("score_l", [P, 2, NT, HEADS], f32r, sc)
        RQG = 4
        rqb = sb("rqb", [P, 2, 4, RQG * GE], bf16, sc)
        hot = sb("hot", [P, 2, 2, GE], f32r, sc)
        picked = sb("picked", [TQ, 2, 2, GE], f32, sc)
        score = sb("score", [P, NB, HEADS], f32, sc)
        score2 = sb("score2", [P, NB, HEADS], f32, sc)
        top = sb("top", [P, 1], f32, sc)
        top_all = sb("top_all", [P, 1], f32, sc)
        neg_top = sb("neg_top", [P, 1], f32, sc)
        HGR = 8
        Hg = sb("Hg", [P, HGR * BLOCKS_PER_GROUP, OUT], f32, sc)
        XBR = 4
        xb = sb("xb", [P, XBR, BW], f32, sc)
        eqB = sb("eqB", [P, XBR, P], f32, sc)
        eq_lowb = sb("eq_lowb", [P, 2, P], f32, sc)
        sc.close()

        bank = [ctx.enter_context(nc.psum_tensor(f"bank{i}", [P, 512], f32)) for i in range(8)]
        PT, PL1, PG, P2, PY = bank[0:2], bank[2:4], bank[4], bank[5], bank[6:8]

        s_const = sem("s_const")
        s_dc = sem("s_dc")
        s_ldw = sem("s_ldw")
        s_ldx = [sem(f"s_ldx{i}") for i in range(4)]
        s_ldi = sem("s_ldi")
        s_rqd = sem("s_rqd")
        s_zero = sem("s_zero")
        s_w0 = sem("s_w0")
        s_xh = sem("s_xh")
        s_xl = sem("s_xl")
        s_wh = sem("s_wh")
        s_wl = sem("s_wl")
        s_n0 = sem("s_n0")
        s_n0a = sem("s_n0a")
        s_n0b = sem("s_n0b")
        s_ta = [sem(f"s_ta{i}") for i in range(N0R)]
        s_tb = [sem(f"s_tb{i}") for i in range(N0R)]
        s_ga = [sem(f"s_ga{i}") for i in range(GAR)]
        s_gb = [sem(f"s_gb{i}") for i in range(GBR)]
        s_e = [sem(f"s_e{i}") for i in range(2)]
        s_bc = [sem(f"s_bc{i}") for i in range(2)]
        s_add = sem("s_add")
        s_T = sem("s_T")
        s_tanh1 = sem("s_tanh1")
        s_h1h = sem("s_h1h")
        s_h1l = sem("s_h1l")
        s_L1 = sem("s_L1")
        s_tanh2 = sem("s_tanh2")
        s_h2h = sem("s_h2h")
        s_h2l = sem("s_h2l")
        s_eh = sem("s_eh")
        s_el = sem("s_el")
        s_G = sem("s_G")
        s_gate = sem("s_gate")
        s_L2 = sem("s_L2")
        s_mul = sem("s_mul")
        s_mh = sem("s_mh")
        s_ml = sem("s_ml")
        s_eq = sem("s_eq")
        s_dup = sem("s_dup")
        s_tof = sem("s_tof")
        s_to = sem("s_to")
        s_Y = sem("s_Y")
        s_Yc = sem("s_Yc")
        s_scA = [sem(f"s_scA{i}") for i in range(TABLES)]
        s_scB = [sem(f"s_scB{i}") for i in range(TABLES)]
        s_xn = sem("s_xn")
        s_ldc = sem("s_ldc")
        s_tab = [sem(f"s_tab{i}") for i in range(TSR)]
        s_sum1 = sem("s_sum1")
        s_sum2 = sem("s_sum2")
        s_cden = sem("s_cden")
        s_cinv = sem("s_cinv")
        s_att = sem("s_att")
        s_res = sem("s_res")
        s_stat = sem("s_stat")
        s_mv = sem("s_mv")
        s_std = sem("s_std")
        s_rstd = sem("s_rstd")
        s_x1 = sem("s_x1")
        s_wa = sem("s_wa")
        s_wac = sem("s_wac")
        s_x1t = sem("s_x1t")
        s_x1c = sem("s_x1c")
        s_H = sem("s_H")
        s_hc = sem("s_hc")
        s_sh = sem("s_sh")
        s_sl = sem("s_sl")
        s_ht = [sem(f"s_ht{i}") for i in range(4)]
        s_rq = [sem(f"s_rq{i}") for i in range(2)]
        s_hot = sem("s_hot")
        s_O = sem("s_O")
        s_pick = sem("s_pick")
        s_sc = sem("s_sc")
        s_scc = sem("s_scc")
        s_b2 = sem("s_b2")
        s_top = sem("s_top")
        s_ex = sem("s_ex")
        s_hg = [sem(f"s_hg{i}") for i in range(HGR)]
        s_bcb = [sem(f"s_bcb{i}") for i in range(2)]
        s_xb = sem("s_xb")
        s_xe = sem("s_xe")
        s_eqb = sem("s_eqb")
        s_dupb = sem("s_dupb")
        s_tofb = sem("s_tofb")
        s_tob = sem("s_tob")
        s_YB = sem("s_YB")
        s_YBc = sem("s_YBc")
        s_out = sem("s_out")

        PARTS = 4
        tiles_per_part = -(-NT // PARTS)
        part_of_tile = [t // tiles_per_part for t in range(NT)]

        def part_cols(i):
            return slice(i * tiles_per_part * P, min((i + 1) * tiles_per_part * P, N))

        def ring_total(ring, slot, n):
            return 16 * len([i for i in range(n) if i % ring == slot])

        def group_arrivals(ring, g):
            return 16 * sum(len(blocks_of_group(i)) for i in range(g % ring, g + 1, ring))

        def wait_stage_n0(eng):
            for k in range(N0R):
                eng.wait_ge(s_ta[k], ring_total(N0R, k, NT))
                eng.wait_ge(s_tb[k], ring_total(N0R, k, NT))
            eng.wait_ge(s_rqd, 16)
            eng.wait_ge(s_wl, 4)

        def wait_stage_a(eng):
            for k in range(TABLES):
                eng.wait_ge(s_scA[k], ring_total(TABLES, k, NB))

        def load_tables(eng, tables, width, base):
            for t in range(NT):
                u = base + t
                if u >= TSR:
                    eng.wait_ge(s_sum2, u - TSR + 1)
                for k in range(TABLES):
                    eng.dma_start(tab[:, u % TSR, k, 0:width],
                                  tables[k][t * P:(t + 1) * P, :]).then_inc(s_tab[u % TSR], 16)

        block = ctx.enter_context(nc.Block())

        @block.sync
        def _(sp):
            sp.dma_start(W0f[:, :, :], W0.rearrange("(k p) n -> p k n", p=P)).then_inc(s_w0, 16)
            for i in range(PARTS):
                sp.dma_start(xTf[:, :, part_cols(i)],
                             xT[:, part_cols(i)].rearrange("(k p) n -> p k n", p=P)).then_inc(s_ldx[i], 16)
            sp.dma_start(b0b[:, :], b0.partition_broadcast(P)).then_inc(s_w0, 16)
            sp.dma_start(src_c[:, :], src_cols).then_inc(s_ldi, 16)
            sp.dma_start(dst_c[:, :], dst_cols).then_inc(s_ldi, 16)
            sp.dma_start(idx_rows[:, 0, :], src_row.rearrange("(p j) -> p j", p=RQ)).then_inc(s_ldi, 16)
            sp.dma_start(idx_rows[:, 1, :], dst_row.rearrange("(p j) -> p j", p=RQ)).then_inc(s_ldi, 16)
            for c in range(C1):
                sp.dma_start(W1f[0:k1(c), c, :], W1[c * K1:c * K1 + k1(c), :]).then_inc(s_ldw, 16)
            for m in range(C2):
                sp.dma_start(W2f[0:k2(m), m, :], W2[m * K2:m * K2 + k2(m), :]).then_inc(s_ldw, 16)
                sp.dma_start(b1c[0:k2(m), m:m + 1],
                             b1[m * K2:m * K2 + k2(m)].rearrange("(p a) -> p a", a=1)).then_inc(s_ldw, 16)
            sp.dma_start(W2f[k2(C2 - 1):k2(C2 - 1) + 1, C2 - 1, :],
                         b2.rearrange("(a n) -> a n", a=1)).then_inc(s_ldw, 16)
            sp.dma_start(Wgf[:, :], Wg).then_inc(s_ldw, 16)
            full = (N // P) * P
            sp.dma_start(xn[:, 0:N // P, :], x[0:full, :].rearrange("(t p) d -> p t d", p=P)).then_inc(s_xn, 16)
            sp.dma_start(xn[0:N - full, N // P, :], x[full:N, :]).then_inc(s_xn, 16)
            sp.dma_start(w_c[:, :], w_cols).then_inc(s_xn, 16)
            for t in range(NT):
                n = rows_of_tile(t)
                sp.wait_ge(s_n0a, t + 1)
                sp.dma_start(TA[t * P:t * P + n, :], stA[0:n, t % N0R, :]).then_inc(s_ta[t % N0R], 16)
                sp.wait_ge(s_n0b, t + 1)
                sp.dma_start(TB[t * P:t * P + n, :], stB[0:n, t % N0R, :]).then_inc(s_tb[t % N0R], 16)
            sp.wait_ge(s_dc, DC["rq"])
            sp.dma_start(RQD.rearrange("k (p j) -> p k j", p=RQ), rq_b[:, :, :]).then_inc(s_rqd, 16)
            sp.wait_ge(s_dc, DC["zeros"])
            for table, width in [(t, AW) for t in accA] + [(t, BW) for t in accB]:
                sp.dma_start(table.rearrange("(t p) d -> p t d", p=P),
                             zeros[:, 0:width].unsqueeze(1).to_broadcast([P, TR // P, width])).then_inc(s_zero, 16)
            wait_stage_n0(sp)
            for g in range(NG):
                n = edges_of_group(g)
                if g >= 2:
                    sp.wait_ge(s_eh, g - 1)
                    sp.wait_ge(s_el, g - 1)
                sp.dma_start(ef[:, g % 2, 0:n], eT[:, g * GE:g * GE + n]).then_inc(s_e[g % 2], 16)
                if g >= 2:
                    sp.wait_ge(s_dup, g * BLOCKS_PER_GROUP - BLOCKS_PER_GROUP)
                sp.dma_start(bcast_i[:, g % 2, 0:n],
                             src_row[g * GE:g * GE + n].partition_broadcast(P)).then_inc(s_bc[g % 2], 16)
            wait_stage_a(sp)
            sp.dma_start(Wc[:, :, 0:OUT], Wcat.rearrange("(k p) n -> p k n", p=P)).then_inc(s_ldc, 16)
            sp.dma_start(WcT[:, :, :], WcatT.rearrange("(k p) n -> p k n", p=P)).then_inc(s_ldc, 16)
            sp.wait_ge(s_dc, DC["ablk"])
            for h in range(HEADS):
                k, r = divmod(h * HD, P)
                sp.dma_start(ablk[r:r + HD, k, h:h + 1], a_src[h, :, :]).then_inc(s_ldc, 16)
                sp.dma_start(ablk[r:r + HD, k, HEADS + h:HEADS + h + 1], a_dst[h, :, :]).then_inc(s_ldc, 16)
            load_tables(sp, accA, AW, 0)
            for t in range(NT):
                n = rows_of_tile(t)
                sp.wait_ge(s_hc, t + 1)
                sp.dma_start(HT[t * P:t * P + n, :], hst[0:n, t % 4, :]).then_inc(s_ht[t % 4], 16)
            for i in range(0, -(-NG // RQG)):
                a, n = i * RQG * GE, min(RQG * GE, E - i * RQG * GE)
                if i == 0:
                    sp.wait_ge(s_rqd, 16)
                if i >= 2:
                    sp.wait_ge(s_pick, 2 * (i - 1) * RQG)
                sp.dma_start(rqb[:, i % 2, :, 0:n], RQD[:, a:a + n].partition_broadcast(P)).then_inc(s_rq[i % 2], 16)
            for g in range(NG):
                n = edges_of_group(g)
                if g >= 2:
                    sp.wait_ge(s_dupb, g * BLOCKS_PER_GROUP - BLOCKS_PER_GROUP)
                sp.dma_start(bcast_i[:, g % 2, 0:n],
                             dst_row[g * GE:g * GE + n].partition_broadcast(P)).then_inc(s_bcb[g % 2], 16)
            for k in range(TABLES):
                sp.wait_ge(s_scB[k], ring_total(TABLES, k, NB))
            load_tables(sp, accB, BW, NT)
            for t in range(NT):
                n = rows_of_tile(t)
                sp.wait_ge(s_x1, NT + t + 1)
                sp.dma_start(out[t * P:t * P + n, :], xn[0:n, t, :]).then_inc(s_out, 16)
            sp.wait_ge(s_out, 16 * NT)

        @block.gpsimd
        def _(pool):
            pool.iota(iota_i[:, :], pattern=[[1, P]], base=0, channel_multiplier=0).then_inc(s_const, 1)
            pool.iota(p_i[:, :], pattern=[[0, 1]], base=0, channel_multiplier=1).then_inc(s_const, 1)
            wait_stage_n0(pool)
            pool.wait_ge(s_zero, 16 * 2 * TABLES)

            def gather_a(b, g):
                n = rows_of_block(b)
                pool.indirect_dma_start(
                    out=GA[0:n, b % (GAR * BLOCKS_PER_GROUP), :], out_offset=None, in_=TA,
                    in_offset=bass.IndirectOffsetOnAxis(ap=src_c[0:n, b:b + 1], axis=0)).then_inc(s_ga[g % GAR], 16)

            def gather_b(b, g):
                n = rows_of_block(b)
                pool.indirect_dma_start(
                    out=GB[0:n, b % (GBR * BLOCKS_PER_GROUP), :], out_offset=None, in_=TB,
                    in_offset=bass.IndirectOffsetOnAxis(ap=dst_c[0:n, b:b + 1], axis=0)).then_inc(s_gb[g % GBR], 16)

            def scatter(b, tables, width, rows, copied, landed):
                n = rows_of_block(b)
                pool.wait_ge(copied, b + 1)
                if b >= TABLES:
                    pool.wait_ge(landed[b % TABLES], 16 * (b // TABLES))
                pool.indirect_dma_start(
                    out=tables[b % TABLES], out_offset=bass.IndirectOffsetOnAxis(ap=rows[0:n, b:b + 1], axis=0),
                    in_=ystage[0:n, b % Y_RING, 0:width], in_offset=None,
                    bounds_check=TR - 1, oob_is_err=True,
                    compute_op=ALU.add).then_inc(landed[b % TABLES], 16)

            for s in range(-3, NG + 2):
                ahead, behind = s + 3, s - 2
                for j in range(BLOCKS_PER_GROUP):
                    if 0 <= ahead < NG and j < len(blocks_of_group(ahead)):
                        if j == 0 and ahead >= GAR:
                            pool.wait_ge(s_T, C1 * (ahead - GAR + 1))
                        if j == 0 and ahead >= GBR:
                            pool.wait_ge(s_add, ahead - GBR + 1)
                        gather_a(blocks_of_group(ahead)[j], ahead)
                        gather_b(blocks_of_group(ahead)[j], ahead)
                    if 0 <= behind < NG and j < len(blocks_of_group(behind)):
                        if j == 0:
                            pool.wait_ge(s_to, behind + 1)
                        scatter(blocks_of_group(behind)[j], accA, AW, to_a, s_Yc, s_scA)

            def gather_h(g):
                if g >= HGR:
                    pool.wait_ge(s_xb, (g - HGR + 1) * BLOCKS_PER_GROUP)
                for b in blocks_of_group(g):
                    n = rows_of_block(b)
                    pool.indirect_dma_start(
                        out=Hg[0:n, b % (HGR * BLOCKS_PER_GROUP), :], out_offset=None, in_=HT,
                        in_offset=bass.IndirectOffsetOnAxis(ap=src_c[0:n, b:b + 1], axis=0)).then_inc(s_hg[g % HGR], 16)

            for k in range(4):
                pool.wait_ge(s_ht[k], ring_total(4, k, NT))
            for g in range(min(HGR, NG)):
                gather_h(g)
            pool.wait_ge(s_b2, B2["top"])
            pool.partition_all_reduce(top_all[:, :], top[:, :], P, bass.bass_isa.ReduceOp.max).then_inc(s_top, 1)
            for g in range(NG):
                for b in blocks_of_group(g):
                    if b == blocks_of_group(g)[0]:
                        pool.wait_ge(s_tob, g + 1)
                    scatter(b, accB, BW, to_b, s_YBc, s_scB)
                if g + HGR - 1 < NG and g >= 1:
                    gather_h(g + HGR - 1)

        @block.tensor
        def _(pe):
            def split_product(o, lh, ll, rh, rl, first, last):
                pe.matmul(o, lh, rh, start=first, stop=False)
                pe.matmul(o, lh, rl, start=False, stop=False)
                return pe.matmul(o, ll, rh, start=False, stop=last)

            pe.wait_ge(s_wl, 1)
            for t in range(NT):
                n = rows_of_tile(t)
                pe.wait_ge(s_xl, part_of_tile[t] + 1)
                for half in range(2):
                    u = 2 * t + half
                    if u >= 8:
                        pe.wait_ge(s_n0a if half == 0 else s_n0b, t - 3)
                    o = bank[u % 8][0:n, 0:H0]
                    for k in range(DK):
                        last = split_product(o, xTh[:, k, t * P:t * P + n], xTl[:, k, t * P:t * P + n],
                                             W0h[:, half * DK + k, :], W0l[:, half * DK + k, :],
                                             k == 0, k == DK - 1)
                    last.then_inc(s_n0, 1)

            def transpose_chunk(g, c):
                u = C1 * g + c
                if c == 0:
                    pe.wait_ge(s_add, g + 1)
                if u >= 2:
                    pe.wait_ge(s_tanh1, u - 1)
                for j, b in enumerate(blocks_of_group(g)):
                    n = rows_of_block(b)
                    last = pe.transpose(PT[u % 2][0:k1(c), j * P:j * P + n],
                                        GA[0:n, b % (GAR * BLOCKS_PER_GROUP), c * K1:c * K1 + k1(c)],
                                        ident[0:n, 0:n])
                last.then_inc(s_T, 1)

            def hidden2(g, m):
                u, n = C2 * g + m, edges_of_group(g)
                if m == 0:
                    pe.wait_ge(s_h1l, C1 * (g + 1))
                if u >= 2:
                    pe.wait_ge(s_tanh2, u - 1)
                o = PL1[u % 2][0:k2(m), 0:n]
                for c in range(C1):
                    ms = slice(m * K2, m * K2 + k2(m))
                    last = split_product(o, W1h[0:k1(c), c, ms], W1l[0:k1(c), c, ms],
                                         h1h[0:k1(c), g % 2, c, 0:n], h1l[0:k1(c), g % 2, c, 0:n],
                                         c == 0, c == C1 - 1)
                last.then_inc(s_L1, 1)

            def gate_pair(g, q):
                pe.wait_ge(s_el, g + 1)
                if q >= 1:
                    pe.wait_ge(s_gate, q)
                for i, b in enumerate(blocks_of_pair(q)):
                    n, a = rows_of_block(b), (b - g * BLOCKS_PER_GROUP) * P
                    last = split_product(PG[0:n, i * OUT:(i + 1) * OUT], eh[:, g % 2, a:a + n],
                                         el[:, g % 2, a:a + n], Wgh[:, :], Wgl[:, :], True, True)
                last.then_inc(s_G, 1)

            def output_pair(g, q):
                pe.wait_ge(s_h2l, C2 * (g + 1))
                if q >= 1:
                    pe.wait_ge(s_mul, q)
                for i, b in enumerate(blocks_of_pair(q)):
                    n, a = rows_of_block(b), (b - g * BLOCKS_PER_GROUP) * P
                    for m in range(C2):
                        k = k2(m) + (m == C2 - 1)
                        last = split_product(P2[0:n, i * OUT:(i + 1) * OUT], h2h[0:k, g % 2, m, a:a + n],
                                             h2l[0:k, g % 2, m, a:a + n], W2h[0:k, m, :], W2l[0:k, m, :],
                                             m == 0, m == C2 - 1)
                last.then_inc(s_L2, 1)

            def block_sums(b):
                n, q = rows_of_block(b), b // 2
                pe.wait_ge(s_ml, q + 1)
                pe.wait_ge(s_eq, b + 1)
                if b >= 2:
                    pe.wait_ge(s_Yc, b - 1)
                o = PY[b % 2][0:n, 0:AW]
                pe.matmul(o, eqA[0:n, b % EQR, 0:n], mh[0:n, q % 2, b % 2, :], start=True, stop=False)
                pe.matmul(o, eqA[0:n, b % EQR, 0:n], ml[0:n, q % 2, b % 2, :], start=False, stop=True)\
                    .then_inc(s_Y, 1)

            pe.wait_ge(s_n0a, NT)
            pe.wait_ge(s_n0b, NT)
            pe.wait_ge(s_wl, 4)
            pe.wait_ge(s_dc, DC["ones"])
            for s in range(-1, NG + 1):
                now, nxt, prev = 0 <= s < NG, s + 1 < NG, s >= 1
                pairs = pairs_of_group(s - 1) if prev else []
                if now:
                    hidden2(s, 0)
                for i in range(2):
                    if i < len(pairs):
                        gate_pair(s - 1, pairs[i])
                        output_pair(s - 1, pairs[i])
                    if nxt:
                        transpose_chunk(s + 1, 2 * i)
                        transpose_chunk(s + 1, 2 * i + 1)
                    if now:
                        hidden2(s, i + 1)
                    if i < len(pairs):
                        for b in blocks_of_pair(pairs[i]):
                            block_sums(b)

            pe.wait_ge(s_Yc, NB)
            pe.wait_ge(s_ldc, 16 * (2 + 2 * HEADS))
            for i in range(DK):
                for k in range(DK):
                    last = pe.matmul(bank[0][:, i * 8:i * 8 + 2 * HEADS], WcT[:, k, i * P:(i + 1) * P],
                                     ablk[:, k, :], start=k == 0, stop=k == DK - 1)
            last.then_inc(s_wa, 1)
            pe.wait_ge(s_wac, 1)
            def x1_transposes(t):
                n = rows_of_tile(t)
                pe.wait_ge(s_x1, t + 1)
                if t >= 2:
                    pe.wait_ge(s_x1c, t - 1)
                for k in range(DK):
                    last = pe.transpose(PT[t % 2][:, k * P:k * P + n], xn[0:n, t, k * P:(k + 1) * P],
                                        ident[0:n, 0:n])
                last.then_inc(s_x1t, 1)

            def node_products(t):
                n = rows_of_tile(t)
                pe.wait_ge(s_x1c, t + 1)
                if t >= 2:
                    pe.wait_ge(s_hc, t - 1)
                    pe.wait_ge(s_sl, t - 1)
                for k in range(DK):
                    last = pe.matmul(PL1[t % 2][0:n, 0:OUT + 2 * HEADS], x1T[:, t % 2, k, 0:n], Wc[:, k, :],
                                     start=k == 0, stop=k == DK - 1)
                last.then_inc(s_H, 1)

            x1_transposes(0)
            for t in range(NT):
                if t + 1 < NT:
                    x1_transposes(t + 1)
                node_products(t)

            pe.wait_ge(s_hc, NT)
            pe.wait_ge(s_sl, NT)
            def candidates(g):
                n = edges_of_group(g)
                for side in range(2):
                    u = 2 * g + side
                    pe.wait_ge(s_hot, u + 1)
                    if u >= 4:
                        pe.wait_ge(s_pick, u - 3)
                    o = bank[u % 4][0:TQ, 0:n]
                    pe.matmul(o, score_h[:, side, :, :].rearrange("p t h -> p (t h)"),
                              hot[:, g % 2, side, 0:n], start=True, stop=False)
                    pe.matmul(o, score_l[:, side, :, :].rearrange("p t h -> p (t h)"),
                              hot[:, g % 2, side, 0:n], start=False, stop=True).then_inc(s_O, 1)

            def edge_scores(g):
                pe.wait_ge(s_pick, 2 * g + 2)
                if g >= 4:
                    pe.wait_ge(s_scc, g - 3)
                for j, b in enumerate(blocks_of_group(g)):
                    n = rows_of_block(b)
                    for side in range(2):
                        last = pe.matmul(bank[4 + g % 4][0:n, j * HEADS:(j + 1) * HEADS],
                                         picked[:, g % 2, side, j * P:j * P + n],
                                         select[0:TQ, :], start=side == 0, stop=side == 1)
                last.then_inc(s_sc, 1)

            candidates(0)
            for g in range(NG):
                if g + 1 < NG:
                    candidates(g + 1)
                edge_scores(g)

            pe.wait_ge(s_scc, NG)
            for b in range(NB):
                n = rows_of_block(b)
                pe.wait_ge(s_xb, b + 1)
                pe.wait_ge(s_xe, b + 1)
                pe.wait_ge(s_eqb, b + 1)
                if b >= 4:
                    pe.wait_ge(s_YBc, b - 3)
                pe.matmul(bank[b % 4][0:n, 0:BW], eqB[0:n, b % XBR, 0:n], xb[0:n, b % XBR, :],
                          start=True, stop=True).then_inc(s_YB, 1)

        def rows_copy(act, copy, t):
            n = rows_of_tile(t)
            act.wait_ge(s_H, t + 1)
            act.wait_ge(s_sl, t + 1)
            if t >= 4:
                act.wait_ge(s_ht[t % 4], 16 * (t // 4))
            copy(hst[0:n, t % 4, :], PL1[t % 2][0:n, 0:OUT]).then_inc(s_hc, 1)

        @block.scalar
        def _(act):
            def copy(o, i):
                return act.activation(o, i, ACT.Copy)

            act.wait_ge(s_w0, 32)
            copy(W0h[:, :, :], W0f[:, :, :]).then_inc(s_wh, 1)
            for i in range(PARTS):
                act.wait_ge(s_ldx[i], 16)
                copy(xTh[:, :, part_cols(i)], xTf[:, :, part_cols(i)]).then_inc(s_xh, 1)
            act.wait_ge(s_ldw, 16 * (C1 + 2 * C2 + 2))
            for c in range(C1):
                last = copy(W1h[0:k1(c), c, :], W1f[0:k1(c), c, :])
            last.then_inc(s_wh, 1)
            for m in range(C2):
                k = k2(m) + (m == C2 - 1)
                last = copy(W2h[0:k, m, :], W2f[0:k, m, :])
            last.then_inc(s_wh, 1)
            copy(Wgh[:, :], Wgf[:, :]).then_inc(s_wh, 1)
            for t in range(NT):
                n = rows_of_tile(t)
                act.wait_ge(s_n0, 2 * t + 2)
                if t >= N0R:
                    act.wait_ge(s_tb[t % N0R], 16 * (t // N0R))
                copy(stB[0:n, t % N0R, :], bank[(2 * t + 1) % 8][0:n, 0:H0]).then_inc(s_n0b, 1)

            def tanh1(g, c):
                u, n = C1 * g + c, edges_of_group(g)
                act.wait_ge(s_T, u + 1)
                if g >= 1:
                    act.wait_ge(s_h1l, u - C1 + 1)
                act.activation(h1f[0:k1(c), c, 0:n], PT[u % 2][0:k1(c), 0:n], ACT.Tanh).then_inc(s_tanh1, 1)

            def tanh2(g, m):
                u, n = C2 * g + m, edges_of_group(g)
                act.wait_ge(s_L1, u + 1)
                if g >= 1:
                    act.wait_ge(s_h2l, u - C2 + 1)
                act.activation(h2f[0:k2(m), m, 0:n], PL1[u % 2][0:k2(m), 0:n], ACT.Tanh,
                               bias=b1c[0:k2(m), m:m + 1]).then_inc(s_tanh2, 1)

            def edge_hi(g):
                n = edges_of_group(g)
                act.wait_ge(s_e[g % 2], 16 * (g // 2 + 1))
                if g >= 2:
                    act.wait_ge(s_G, 2 * (g - 1))
                copy(eh[:, g % 2, 0:n], ef[:, g % 2, 0:n]).then_inc(s_eh, 1)

            def gate_copy(q):
                act.wait_ge(s_G, q + 1)
                if q >= 2:
                    act.wait_ge(s_mul, q - 1)
                k, n = len(blocks_of_pair(q)), rows_of_block(2 * q)
                copy(gate[0:n, q % 2, 0:k, :].rearrange("p i d -> p (i d)"), PG[0:n, 0:k * OUT]).then_inc(s_gate, 1)

            def gated_hi(q):
                act.wait_ge(s_mul, q + 1)
                if q >= 2:
                    act.wait_ge(s_Y, 2 * (q - 1))
                k, n = len(blocks_of_pair(q)), rows_of_block(2 * q)
                copy(mh[0:n, q % 2, 0:k, 0:OUT], mf[0:n, q % 2, 0:k, :]).then_inc(s_mh, 1)

            def sums_copy(b, banks, width, done, landed, copied):
                n = rows_of_block(b)
                act.wait_ge(done, b + 1)
                if b >= Y_RING:
                    act.wait_ge(landed[b % TABLES], 16 * ((b - Y_RING) // TABLES + 1))
                copy(ystage[0:n, b % Y_RING, 0:width], banks[b % len(banks)][0:n, 0:width]).then_inc(copied, 1)

            wait_stage_n0(act)
            for s in range(-1, NG + 2):
                if 0 <= s - 1 < NG:
                    tanh2(s - 1, 2)
                if 0 <= s - 2 < NG:
                    for q in list(pairs_of_group(s - 2))[1:]:
                        for b in blocks_of_pair(q):
                            sums_copy(b, PY, AW, s_Y, s_scA, s_Yc)
                if 0 <= s < NG:
                    tanh2(s, 0)
                    edge_hi(s)
                pairs = list(pairs_of_group(s - 1)) if 0 <= s - 1 < NG else []
                for i in range(2):
                    if i < len(pairs):
                        gate_copy(pairs[i])
                    if s + 1 < NG:
                        tanh1(s + 1, 2 * i)
                        tanh1(s + 1, 2 * i + 1)
                    if i < len(pairs):
                        gated_hi(pairs[i])
                    if i == 0:
                        if 0 <= s < NG:
                            tanh2(s, 1)
                        if pairs:
                            for b in blocks_of_pair(pairs[0]):
                                sums_copy(b, PY, AW, s_Y, s_scA, s_Yc)

            wait_stage_a(act)
            act.wait_ge(s_wa, 1)
            copy(Wc[:, :, OUT:OUT + 2 * HEADS],
                 bank[0][:, 0:DK * 8].rearrange("p (i c) -> p i c", c=8)).then_inc(s_wac, 1)
            act.wait_ge(s_mv, NT)
            act.wait_ge(s_dc, DC["eps"])
            act.activation(std[:, :], mv[:, :, 1], ACT.Sqrt, bias=eps[:, :]).then_inc(s_std, 1)
            for t in range(NT):
                n = rows_of_tile(t)
                act.wait_ge(s_x1t, t + 1)
                if t >= 2:
                    act.wait_ge(s_H, t - 1)
                copy(x1T[:, t % 2, :, 0:n],
                     PT[t % 2][:, 0:DK * P].rearrange("p (k r) -> p k r", r=P)[:, :, 0:n]).then_inc(s_x1c, 1)
                if t >= 1:
                    rows_copy(act, copy, t - 1)
            rows_copy(act, copy, NT - 1)

            for g in range(NG):
                act.wait_ge(s_sc, g + 1)
                for run in same_rows(blocks_of_group(g)):
                    n, j, k = rows_of_block(run[0]), run[0] - g * BLOCKS_PER_GROUP, len(run)
                    last = copy(score[0:n, run[0]:run[0] + k, :],
                                bank[4 + g % 4][0:n, j * HEADS:(j + k) * HEADS].rearrange("p (b h) -> p b h", h=HEADS))
                last.then_inc(s_scc, 1)
            act.wait_ge(s_b2, B2["neg"])
            act.activation(score2[:, :, :], score[:, :, :], ACT.Exp, bias=neg_top[:, :]).then_inc(s_ex, 1)
            act.wait_ge(s_ex, 1)
            for i in range(NB + 2):
                if i < NB:
                    n = rows_of_block(i)
                    if i >= XBR:
                        act.wait_ge(s_YB, i - XBR + 1)
                    copy(xb[0:n, i % XBR, OUT:BW], score2[0:n, i, :]).then_inc(s_xe, 1)
                if i >= 2:
                    sums_copy(i - 2, bank[0:4], BW, s_YB, s_scB, s_YBc)
            act.wait_ge(s_mv, 2 * NT)
            act.activation(std[:, :], mv[:, :, 1], ACT.Sqrt, bias=eps[:, :]).then_inc(s_std, 1)

        @block.vector
        def _(dve):
            dc = [0]

            def const(ins):
                dc[0] += 1
                ins.then_inc(s_dc, 1)
                dve.wait_ge(s_dc, dc[0])
                return dc[0]

            def lo(o, full, hi):
                return dve.tensor_tensor(o, full, hi.bitcast(f32), ALU.subtract)

            const(dve.memset(zeros[:, :], 0.0))
            assert dc[0] == DC["zeros"]
            const(dve.memset(eps[:, :], LN_EPS))
            assert dc[0] == DC["eps"]
            const(dve.memset(mv[:, :, :], 0.0))
            dve.wait_ge(s_const, 2)
            const(dve.tensor_copy(iota_row[:, :], iota_i[:, :]))
            const(dve.tensor_copy(p_f[:, :], p_i[:, :]))
            const(dve.tensor_scalar(ident[:, :], iota_row[:, :], p_f[:, :], None, ALU.is_equal))
            const(dve.tensor_scalar(lower[:, :], iota_row[:, :], p_f[:, :], None, ALU.is_lt))
            const(dve.tensor_scalar(trash[:, :], p_f[:, :], float(N), None, ALU.add))
            const(dve.tensor_single_scalar(q_i[:, :], p_i[:, :], HEADS.bit_length() - 1, ALU.logical_shift_right))
            const(dve.tensor_single_scalar(h_i[:, :], p_i[:, :], HEADS - 1, ALU.bitwise_and))
            const(dve.tensor_copy(q_of_p[:, :], q_i[:, :]))
            const(dve.tensor_copy(h_of_p[:, :], h_i[:, :]))
            const(dve.tensor_scalar(select[:, :], iota_row[:, 0:HEADS], h_of_p[:, :], None, ALU.is_equal))
            dve.wait_ge(s_wh, 1)
            lo(W0l[:, :, :], W0f[:, :, :], W0h[:, :, :]).then_inc(s_wl, 1)
            for i in range(PARTS):
                dve.wait_ge(s_xh, i + 1)
                lo(xTl[:, :, part_cols(i)], xTf[:, :, part_cols(i)], xTh[:, :, part_cols(i)]).then_inc(s_xl, 1)
            dve.wait_ge(s_ldi, 64)
            for cols, as_f, less in ((src_c, src_f, src_t), (dst_c, dst_f, dst_t)):
                const(dve.tensor_copy(as_f[:, :], cols[:, :]))
                const(dve.tensor_scalar(less[:, :], as_f[:, :], trash[:, :], None, ALU.subtract))
            const(dve.tensor_single_scalar(rq_i[:, 0:2, :], idx_rows[:, :, :], P - 1, ALU.bitwise_and))
            const(dve.tensor_single_scalar(rq_i[:, 2:4, :], idx_rows[:, :, :], P.bit_length() - 1, ALU.logical_shift_right))
            const(dve.tensor_copy(rq_b[:, :, :], rq_i[:, :, :]))
            assert dc[0] == DC["rq"], dc[0]
            for t in range(NT):
                n = rows_of_tile(t)
                dve.wait_ge(s_n0, 2 * t + 1)
                if t >= N0R:
                    dve.wait_ge(s_ta[t % N0R], 16 * (t // N0R))
                dve.tensor_tensor(stA[0:n, t % N0R, :], bank[(2 * t) % 8][0:n, 0:H0], b0b[0:n, :], ALU.add)\
                    .then_inc(s_n0a, 1)
            dve.wait_ge(s_wh, 4)
            for c in range(C1):
                last = lo(W1l[0:k1(c), c, :], W1f[0:k1(c), c, :], W1h[0:k1(c), c, :])
            last.then_inc(s_wl, 1)
            for m in range(C2):
                k = k2(m) + (m == C2 - 1)
                last = lo(W2l[0:k, m, :], W2f[0:k, m, :], W2h[0:k, m, :])
            last.then_inc(s_wl, 1)
            lo(Wgl[:, :], Wgf[:, :], Wgh[:, :]).then_inc(s_wl, 1)
            wait_stage_n0(dve)
            r = k2(C2 - 1) // 32 * 32
            const(dve.memset(h2h[r:K2, :, C2 - 1, :].bitcast(f32), 1.0))
            const(dve.memset(h2l[r:K2, :, C2 - 1, :].bitcast(f32), 0.0))
            const(dve.memset(mh[:, :, :, OUT:OUT + 1].bitcast(f32), 1.0))
            const(dve.memset(mh[:, :, :, OUT + 1:AW].bitcast(f32), 0.0))
            const(dve.memset(ml[:, :, :, OUT:AW].bitcast(f32), 0.0))
            assert dc[0] == DC["ones"], dc[0]

            def add_rows(g):
                dve.wait_ge(s_ga[g % GAR], group_arrivals(GAR, g))
                dve.wait_ge(s_gb[g % GBR], group_arrivals(GBR, g))
                for run in same_rows(blocks_of_group(g)):
                    n, k = rows_of_block(run[0]), len(run)
                    a, b = run[0] % (GAR * BLOCKS_PER_GROUP), run[0] % (GBR * BLOCKS_PER_GROUP)
                    last = dve.tensor_tensor(GA[0:n, a:a + k, :], GA[0:n, a:a + k, :], GB[0:n, b:b + k, :], ALU.add)
                last.then_inc(s_add, 1)

            def split_h1(g, c):
                u, n = C1 * g + c, edges_of_group(g)
                dve.wait_ge(s_tanh1, u + 1)
                if g >= 2:
                    dve.wait_ge(s_L1, C2 * (g - 1))
                dve.tensor_copy(h1h[0:k1(c), g % 2, c, 0:n], h1f[0:k1(c), c, 0:n]).then_inc(s_h1h, 1)
                dve.wait_ge(s_h1h, u + 1)
                lo(h1l[0:k1(c), g % 2, c, 0:n], h1f[0:k1(c), c, 0:n], h1h[0:k1(c), g % 2, c, 0:n]).then_inc(s_h1l, 1)

            def split_h2(g, m):
                u, n = C2 * g + m, edges_of_group(g)
                dve.wait_ge(s_tanh2, u + 1)
                if g >= 2:
                    dve.wait_ge(s_L2, 2 * (g - 1))
                dve.tensor_copy(h2h[0:k2(m), g % 2, m, 0:n], h2f[0:k2(m), m, 0:n]).then_inc(s_h2h, 1)
                dve.wait_ge(s_h2h, u + 1)
                lo(h2l[0:k2(m), g % 2, m, 0:n], h2f[0:k2(m), m, 0:n], h2h[0:k2(m), g % 2, m, 0:n]).then_inc(s_h2l, 1)

            def edge_lo(g):
                n = edges_of_group(g)
                dve.wait_ge(s_eh, g + 1)
                lo(el[:, g % 2, 0:n], ef[:, g % 2, 0:n], eh[:, g % 2, 0:n]).then_inc(s_el, 1)

            def multiply(q):
                k, n = len(blocks_of_pair(q)), rows_of_block(2 * q)
                dve.wait_ge(s_L2, q + 1)
                dve.wait_ge(s_gate, q + 1)
                if q >= 2:
                    dve.wait_ge(s_ml, q - 1)
                dve.tensor_tensor(mf[0:n, q % 2, 0:k, :].rearrange("p i d -> p (i d)"), P2[0:n, 0:k * OUT],
                                  gate[0:n, q % 2, 0:k, :].rearrange("p i d -> p (i d)"), ALU.mult).then_inc(s_mul, 1)

            def gated_lo(q):
                k, n = len(blocks_of_pair(q)), rows_of_block(2 * q)
                dve.wait_ge(s_mh, q + 1)
                lo(ml[0:n, q % 2, 0:k, 0:OUT], mf[0:n, q % 2, 0:k, :], mh[0:n, q % 2, 0:k, 0:OUT]).then_inc(s_ml, 1)

            def equality(g, eq, ring, used, done, loaded, as_f, less, low, dup, dup_done, to, tof_done, to_done):
                dve.wait_ge(loaded[g % 2], 16 * (g // 2 + 1))
                for j, b in enumerate(blocks_of_group(g)):
                    n = rows_of_block(b)
                    if b >= ring:
                        dve.wait_ge(used, b - ring + 1)
                    dve.tensor_scalar(eq[0:n, b % ring, 0:n], bcast_i[0:n, g % 2, j * P:j * P + n],
                                      as_f[0:n, b:b + 1], None, ALU.is_equal).then_inc(done, 1)
                    if b >= 2:
                        dve.wait_ge(dup_done, b - 1)
                    dve.scalar_tensor_tensor(low[0:n, b % 2, 0:n], bcast_i[0:n, g % 2, j * P:j * P + n],
                                             as_f[0:n, b:b + 1], lower[0:n, 0:n], ALU.is_equal, ALU.mult,
                                             accum_out=dup[0:n, b:b + 1]).then_inc(dup_done, 1)
                dve.wait_ge(dup_done, blocks_of_group(g)[-1] + 1)
                runs = same_rows(blocks_of_group(g))
                if g >= 1:
                    dve.wait_ge(to_done, g)
                for run in runs:
                    n, b, k = rows_of_block(run[0]), run[0], len(run)
                    last = dve.scalar_tensor_tensor(to_f[0:n, b % 4:b % 4 + k], dup[0:n, b:b + k], 0.0,
                                                    less[0:n, b:b + k], ALU.is_equal, ALU.mult)
                last.then_inc(tof_done, 1)
                dve.wait_ge(tof_done, g + 1)
                for run in runs:
                    n, b, k = rows_of_block(run[0]), run[0], len(run)
                    last = dve.tensor_scalar(to[0:n, b:b + k], to_f[0:n, b % 4:b % 4 + k], trash[0:n, :], None, ALU.add)
                last.then_inc(to_done, 1)

            for s in range(-2, NG + 1):
                pairs = list(pairs_of_group(s - 1)) if 0 <= s - 1 < NG else []
                if 0 <= s - 1 < NG:
                    split_h2(s - 1, 2)
                if s + 2 < NG:
                    add_rows(s + 2)
                if 0 <= s < NG:
                    split_h2(s, 0)
                for i in range(2):
                    if i < len(pairs):
                        multiply(pairs[i])
                    if 0 <= s + 1 < NG:
                        split_h1(s + 1, 2 * i)
                        split_h1(s + 1, 2 * i + 1)
                    if i < len(pairs):
                        gated_lo(pairs[i])
                    if i == 0 and 0 <= s < NG:
                        split_h2(s, 1)
                        edge_lo(s)
                        equality(s, eqA, EQR, s_Y, s_eq, s_bc, src_f, src_t, eq_low, dup, s_dup, to_a, s_tof, s_to)

            def sum_tables(t, u, width):
                dve.wait_ge(s_tab[u % TSR], 16 * TABLES * (u // TSR + 1))
                if u >= 2:
                    dve.wait_ge(s_res, u - 1)
                dve.tensor_tensor(tsum[:, u % 2, 0, 0:width], tab[:, u % TSR, 0, 0:width],
                                  tab[:, u % TSR, 1, 0:width], ALU.add).then_inc(s_sum1, 1)
                dve.wait_ge(s_sum1, u + 1)
                dve.tensor_tensor(tsum[:, u % 2, 1, 0:width], tsum[:, u % 2, 0, 0:width],
                                  tab[:, u % TSR, 2, 0:width], ALU.add).then_inc(s_sum2, 1)
                dve.wait_ge(s_sum2, u + 1)

            def moments(t, u):
                n = rows_of_tile(t)
                dve.wait_ge(s_res, u + 1)
                dve.bn_stats(stats[0:n, t, :], xn[0:n, t, :]).then_inc(s_stat, 1)
                dve.wait_ge(s_stat, u + 1)
                dve.bn_aggr(mv[0:n, t, :], stats[0:n, t, :]).then_inc(s_mv, 1)

            def normalise(base):
                dve.wait_ge(s_std, base // NT + 1)
                dve.reciprocal(rstd[:, :], std[:, :]).then_inc(s_rstd, 1)
                dve.wait_ge(s_rstd, base // NT + 1)
                for t in range(NT):
                    n = rows_of_tile(t)
                    dve.tensor_scalar(xn[0:n, t, :], xn[0:n, t, :], mv[0:n, t, 0:1], rstd[0:n, t:t + 1],
                                      ALU.subtract, ALU.mult).then_inc(s_x1, 1)
                    if base == 0 and t >= 1:
                        split_scores(t - 1)

            def split_scores(t):
                n = rows_of_tile(t)
                dve.wait_ge(s_H, t + 1)
                pc = PL1[t % 2][0:n, OUT:OUT + 2 * HEADS].rearrange("p (s h) -> p s h", h=HEADS)
                dve.tensor_copy(score_h[0:n, :, t, :], pc).then_inc(s_sh, 1)
                dve.wait_ge(s_sh, t + 1)
                lo(score_l[0:n, :, t, :], pc, score_h[0:n, :, t, :]).then_inc(s_sl, 1)

            wait_stage_a(dve)
            const(dve.memset(ablk[:, :, :], 0.0))
            assert dc[0] == DC["ablk"], dc[0]
            const(dve.memset(score_h[:, :, :, :].bitcast(f32), 0.0))
            const(dve.memset(score_l[:, :, :, :].bitcast(f32), 0.0))
            dve.wait_ge(s_xn, 48)
            for t in range(NT):
                n, u = rows_of_tile(t), t
                sum_tables(t, u, AW)
                dve.tensor_scalar(cden[0:n, t, 0:1], tsum[0:n, u % 2, 1, OUT:OUT + 1], 1.0, None, ALU.max)\
                    .then_inc(s_cden, 1)
                dve.wait_ge(s_cden, u + 1)
                dve.reciprocal(cinv[0:n, t, 0:1], cden[0:n, t, 0:1]).then_inc(s_cinv, 1)
                dve.wait_ge(s_cinv, u + 1)
                dve.scalar_tensor_tensor(xn[0:n, t, :], tsum[0:n, u % 2, 1, 0:OUT], cinv[0:n, t, 0:1],
                                         xn[0:n, t, :], ALU.mult, ALU.add).then_inc(s_res, 1)
                moments(t, u)
            normalise(0)
            split_scores(NT - 1)

            def one_hot(g):
                i, n = g // RQG, edges_of_group(g)
                if g % RQG == 0:
                    dve.wait_ge(s_rq[i % 2], 16 * (i // 2 + 1))
                a = (g % RQG) * GE
                for side in range(2):
                    if g >= 2:
                        dve.wait_ge(s_O, 2 * (g - 2) + side + 1)
                    dve.tensor_scalar(hot[:, g % 2, side, 0:n], rqb[:, i % 2, side, a:a + n], p_f[:, :], None,
                                      ALU.is_equal).then_inc(s_hot, 1)

            def pick(g):
                i, n = g // RQG, edges_of_group(g)
                a = (g % RQG) * GE
                if g >= 2:
                    dve.wait_ge(s_sc, g - 1)
                for side in range(2):
                    u = 2 * g + side
                    dve.wait_ge(s_O, u + 1)
                    dve.scalar_tensor_tensor(picked[:, g % 2, side, 0:n], rqb[0:TQ, i % 2, 2 + side, a:a + n],
                                             q_of_p[0:TQ, :], bank[u % 4][0:TQ, 0:n], ALU.is_equal, ALU.mult)\
                        .then_inc(s_pick, 1)

            one_hot(0)
            for g in range(NG):
                if g + 1 < NG:
                    one_hot(g + 1)
                pick(g)
            b2 = [0]

            def step(ins):
                b2[0] += 1
                ins.then_inc(s_b2, 1)
                dve.wait_ge(s_b2, b2[0])
                return b2[0]

            dve.wait_ge(s_scc, NG)
            runs = same_rows(range(NB))
            for run in runs:
                n, b, k = rows_of_block(run[0]), run[0], len(run)
                v = score[0:n, b:b + k, :]
                step(dve.tensor_scalar(score2[0:n, b:b + k, :], v, NEG_SLOPE, None, ALU.mult))
                step(dve.tensor_tensor(score2[0:n, b:b + k, :], score2[0:n, b:b + k, :], v, ALU.max))
            if rows_of_block(NB - 1) < P:
                step(dve.memset(score[:, NB - 1, :], LOWEST))
            for run in runs:
                n, b, k = rows_of_block(run[0]), run[0], len(run)
                step(dve.tensor_tensor(score[0:n, b:b + k, :], score2[0:n, b:b + k, :],
                                       w_c[0:n, b:b + k].unsqueeze(2).to_broadcast([n, k, HEADS]), ALU.mult))
            top_at = step(dve.tensor_reduce(top[:, :], score[:, :, :].rearrange("p b h -> p (b h)"), AX.X, ALU.max))
            assert top_at == B2["top"], top_at
            dve.wait_ge(s_top, 1)
            neg_at = step(dve.tensor_scalar(neg_top[:, :], top_all[:, :], -1.0, None, ALU.mult))
            assert neg_at == B2["neg"]

            dve.wait_ge(s_ex, 1)
            for g in range(NG):
                equality(g, eqB, XBR, s_YB, s_eqb, s_bcb, dst_f, dst_t, eq_lowb, dup, s_dupb, to_b, s_tofb, s_tob)
                dve.wait_ge(s_hg[g % HGR], group_arrivals(HGR, g))
                for b in blocks_of_group(g):
                    n = rows_of_block(b)
                    if b >= XBR:
                        dve.wait_ge(s_YB, b - XBR + 1)
                    dve.tensor_tensor(xb[0:n, b % XBR, 0:OUT].rearrange("p (h d) -> p h d", d=HD),
                                      Hg[0:n, b % (HGR * BLOCKS_PER_GROUP), :].rearrange("p (h d) -> p h d", d=HD),
                                      score2[0:n, b, :].unsqueeze(2).to_broadcast([n, HEADS, HD]), ALU.mult)\
                        .then_inc(s_xb, 1)

            for t in range(NT):
                n, u = rows_of_tile(t), NT + t
                sum_tables(t, u, BW)
                dve.tensor_scalar(cden[0:n, t, :], tsum[0:n, u % 2, 1, OUT:BW], DENOM_EPS, None, ALU.add)\
                    .then_inc(s_cden, 1)
                dve.wait_ge(s_cden, u + 1)
                dve.reciprocal(cinv[0:n, t, :], cden[0:n, t, :]).then_inc(s_cinv, 1)
                dve.wait_ge(s_cinv, u + 1)
                dve.tensor_tensor(att[0:n, t % 2, :].rearrange("p (h d) -> p h d", d=HD),
                                  tsum[0:n, u % 2, 1, 0:OUT].rearrange("p (h d) -> p h d", d=HD),
                                  cinv[0:n, t, :].unsqueeze(2).to_broadcast([n, HEADS, HD]), ALU.mult)\
                    .then_inc(s_att, 1)
                dve.wait_ge(s_att, t + 1)
                dve.tensor_tensor(xn[0:n, t, :], xn[0:n, t, :], att[0:n, t % 2, :], ALU.add).then_inc(s_res, 1)
                moments(t, u)
            normalise(NT)


DC = {"zeros": 1, "eps": 2, "rq": 20, "ones": 25, "ablk": 26}
B2 = {"top": 8, "neg": 9}


_INS = ["xT", "x", "src_cols", "dst_cols", "src_row", "dst_row", "eT", "w_cols", "W0", "b0", "W1", "b1",
        "W2", "b2", "Wg", "Wcat", "WcatT", "a_src", "a_dst"]


def kernel(x, src, dst, edge_attr_128, edge_weight, L0_gnn_W0, L0_gnn_b0, L0_gnn_W1, L0_gnn_b1, L0_gnn_W2,
           L0_gnn_b2, L0_gnn_Wg, L1_gnn_W, L1_gnn_a_src, L1_gnn_a_dst):
    import concourse.bacc as bacc
    from concourse.bass_utils import run_bass_kernel_spmd

    def columns(v):
        v = np.asarray(v)
        full = np.zeros(-(-v.shape[0] // P) * P, v.dtype)
        full[:v.shape[0]] = v
        return full.reshape(-1, P).T

    W = np.asarray(L1_gnn_W)
    Wcat = W.transpose(1, 0, 2).reshape(W.shape[1], -1)
    laid = dict(
        xT=np.asarray(x).T, x=x, src_cols=columns(src), dst_cols=columns(dst), src_row=src, dst_row=dst,
        eT=np.asarray(edge_attr_128).T, w_cols=columns(edge_weight), W0=L0_gnn_W0, b0=L0_gnn_b0,
        W1=L0_gnn_W1, b1=L0_gnn_b1, W2=L0_gnn_W2, b2=L0_gnn_b2, Wg=L0_gnn_Wg, Wcat=Wcat, WcatT=Wcat.T,
        a_src=L1_gnn_a_src, a_dst=L1_gnn_a_dst)
    nc = bacc.Bacc("TRN2", target_bir_lowering=False, num_devices=1)
    arrays, args = {}, []
    for name in _INS:
        a = np.ascontiguousarray(laid[name])
        arrays[f"in_{name}"] = a
        args.append(nc.dram_tensor(f"in_{name}", a.shape, mybir.dt.from_np(a.dtype), kind="ExternalInput").ap())
    args.append(nc.dram_tensor("out_0", np.asarray(x).shape, mybir.dt.float32, kind="ExternalOutput").ap())
    build_program(nc, *args)
    r = run_bass_kernel_spmd(nc, [arrays], core_ids=[0])
    return r.results[0]["out_0"]
```

```python
import numpy as np
import concourse.bass as bass
from concourse import mybir
from concourse.alu_op_type import AluOpType as ALU
from contextlib import ExitStack


P = 128
BLOCKS_PER_GROUP = 4
TABLES = 2
Y_RING = 8
SUM_LAG = 3
NEG_SLOPE = 0.2
LN_EPS = 1e-5
DENOM_EPS = 1e-10
LOWEST = -3.0e38


def build_program(nc, xT, x, src_cols, dst_cols, src_row, dst_row, eT, w_cols,
                  W0, b0, W1, b1, W2, b2, Wg, Wcat, WcatT, a_src, a_dst, out):
    f32, f32r, bf16, i32 = mybir.dt.float32, mybir.dt.float32r, mybir.dt.bfloat16, mybir.dt.int32
    ACT, AX = mybir.ActivationFunctionType, mybir.AxisListType

    D, N = xT.shape
    E = src_row.shape[0]
    H0, H1, OUT = W0.shape[1], W1.shape[1], W2.shape[1]
    HEADS, HD = a_src.shape[0], a_src.shape[1]
    DK = D // P
    NT = -(-N // P)
    NB = -(-E // P)
    NG = -(-NB // BLOCKS_PER_GROUP)
    GE = BLOCKS_PER_GROUP * P
    NPAIR = -(-NB // 2)
    F1 = H0 // P
    R1 = H0 - F1 * P
    S1 = (0, 32, 64)
    KS = S1[2] + R1
    C1 = F1 + 1
    C2 = -(-H1 // P)
    K2 = -(-H1 // C2)
    AW = OUT + 2
    BW = OUT + HEADS
    TR = (NT + 1) * P
    TC = 5
    NC = -(-NT // TC)
    TQ = NT * HEADS
    RQ = 125
    QC = E // RQ
    WB = P
    assert D % P == 0 and N + P <= TR and E % RQ == 0 and TQ <= P and HEADS == 4
    assert 0 < R1 <= 32 and NG <= P and Y_RING % TABLES == 0

    def rows_of_tile(t):
        return min(P, N - t * P)

    def rows_of_block(b):
        return min(P, E - b * P)

    def blocks_of_group(g):
        return range(g * BLOCKS_PER_GROUP, min((g + 1) * BLOCKS_PER_GROUP, NB))

    def blocks_of_pair(q):
        return range(2 * q, min(2 * q + 2, NB))

    def pairs_of_group(g):
        return range(2 * g, min(2 * g + 2, NPAIR))

    def pairs(g):
        return list(pairs_of_group(g)) if 0 <= g < NG else []

    def edges_of_group(g):
        return min(GE, E - g * GE)

    def k1(c):
        return P if c < F1 else R1

    def k2(m):
        return min(K2, H1 - m * K2)

    def same_rows(blocks):
        full = [b for b in blocks if rows_of_block(b) == P]
        return [r for r in (full, [b for b in blocks if rows_of_block(b) < P]) if r]

    ctx = ExitStack()
    with ctx:
        def sb(name, shape, dt=f32, scope=ctx):
            return scope.enter_context(nc.sbuf_tensor(name, shape, dt))

        def sem(name):
            return ctx.enter_context(nc.semaphore(name))

        TA = nc.dram_tensor("TA", [N, H0], f32).ap()
        TB = nc.dram_tensor("TB", [N, H0], f32).ap()
        HT = nc.dram_tensor("HT", [N, OUT], f32).ap()
        RD = nc.dram_tensor("RD", [2, E], bf16).ap()
        accA = [nc.dram_tensor(f"accA{k}", [TR, AW], f32).ap() for k in range(TABLES)]
        accB = nc.dram_tensor("accB", [TR, BW], f32).ap()

        ident = sb("ident", [P, P])
        lower = sb("lower", [P, P])
        iota_row = sb("iota_row", [P, P])
        p_i = sb("p_i", [P, 1], i32)
        p_f = sb("p_f", [P, 1])
        trash = sb("trash", [P, 1])
        src_c = sb("src_c", [P, NB], i32)
        dst_c = sb("dst_c", [P, NB], i32)
        src_f = sb("src_f", [P, NB])
        dst_f = sb("dst_f", [P, NB])
        tile_c = sb("tile_c", [P, NB, 2], bf16)
        tile_row = sb("tile_row", [P, NT], bf16)
        src_t = sb("src_t", [P, NB])
        dst_rel = sb("dst_rel", [P, NB])
        dst_g = sb("dst_g", [NG, GE], i32)
        low_g = sb("low_g", [NG, 2])
        low_all = sb("low_all", [P, NG])
        dup = sb("dup", [P, NB])
        to_a = sb("to_a", [P, NB], i32)
        to_b = sb("to_b", [P, NG], i32)
        to_f = sb("to_f", [P, BLOCKS_PER_GROUP])
        w_c = sb("w_c", [P, NB])
        xn = sb("xn", [P, NT, D])
        mv = sb("mv", [P, NT, 2])
        std = sb("std", [P, NT])
        rstd = sb("rstd", [P, NT])
        eps = sb("eps", [P, 1])
        zeros = sb("zeros", [P, BW])
        ystage = sb("ystage", [P, Y_RING, BW])
        bcast_i = sb("bcast_i", [P, 2, GE], i32)

        sa = ExitStack()
        W1h = sb("W1h", [P, F1, H1], f32r, sa)
        W1l = sb("W1l", [P, F1, H1], f32r, sa)
        W1s = sb("W1s", [KS, H1], f32r, sa)
        W2h = sb("W2h", [K2, C2, OUT], f32r, sa)
        W2l = sb("W2l", [K2, C2, OUT], f32r, sa)
        Wgh = sb("Wgh", [P, OUT], f32r, sa)
        Wgl = sb("Wgl", [P, OUT], f32r, sa)
        b1c = sb("b1c", [K2, C2], f32, sa)
        GAR, GBR = 3, 2
        sn = ExitStack()
        xTf = sb("xTf", [P, DK, N], f32, sn)
        xTh = sb("xTh", [P, DK, N], f32r, sn)
        xTl = sb("xTl", [P, DK, N], f32r, sn)
        W0f = sb("W0f", [P, 2 * DK, H0], f32, sn)
        W0h = sb("W0h", [P, 2 * DK, H0], f32r, sn)
        W0l = sb("W0l", [P, 2 * DK, H0], f32r, sn)
        b0b = sb("b0b", [P, H0], f32, sn)
        N0R = 4
        stA = sb("stA", [P, N0R, H0], f32, sn)
        stB = sb("stB", [P, N0R, H0], f32, sn)
        idx_rows = sb("idx_rows", [RQ, 2, QC], i32, sn)
        rem_i = sb("rem_i", [RQ, 2, QC], i32, sn)
        tile_i = sb("tile_i", [P, NB, 2], i32, sn)
        iota_i = sb("iota_i", [P, P], i32, sn)
        rem_b = sb("rem_b", [RQ, 2, QC], bf16, sn)
        W1f = sb("W1f", [P, C1, H1], f32, sn)
        W2f = sb("W2f", [K2, C2, OUT], f32, sn)
        Wgf = sb("Wgf", [P, OUT], f32, sn)
        sn.close()
        GA = sb("GA", [P, GAR * BLOCKS_PER_GROUP, H0], f32, sa)
        GB = sb("GB", [P, GBR * BLOCKS_PER_GROUP, H0], f32, sa)
        h1f = sb("h1f", [P, C1, GE], f32, sa)
        h1h = sb("h1h", [P, 2, F1, GE], f32r, sa)
        h1l = sb("h1l", [P, 2, F1, GE], f32r, sa)
        h1s = sb("h1s", [KS, 2, GE], f32r, sa)
        h2f = sb("h2f", [K2, C2, GE], f32, sa)
        h2h = sb("h2h", [K2, 2, C2, GE], f32r, sa)
        h2l = sb("h2l", [K2, 2, C2, GE], f32r, sa)
        ef = sb("ef", [P, 2, GE], f32, sa)
        eh = sb("eh", [P, 2, GE], f32r, sa)
        el = sb("el", [P, 2, GE], f32r, sa)
        gate = sb("gate", [P, 2, 2, OUT], f32, sa)
        mf = sb("mf", [P, 2, 2, OUT], f32, sa)
        mh = sb("mh", [P, 2, 2, AW], f32r, sa)
        ml = sb("ml", [P, 2, 2, AW], f32r, sa)
        EQR = 3 * BLOCKS_PER_GROUP
        eqA = sb("eqA", [P, EQR, P], f32r, sa)
        eq_low = sb("eq_low", [P, 2, P], bf16, sa)
        sa.close()

        sc, s1, s2, s3 = ExitStack(), ExitStack(), ExitStack(), ExitStack()
        cinv = sb("cinv", [P, NT, HEADS], f32, sc)
        cden = sb("cden", [P, NT, HEADS], f32, sc)
        stats = sb("stats", [P, NT, 6], f32, sc)
        node = sb("node", [P, 2, TQ], f32, sc)
        node_rest = sb("node_rest", [P, 2, TQ], f32, sc)
        node_p = sb("node_p", [P, 3, 2, TQ], bf16, sc)
        score = sb("score", [P, NB, HEADS], f32, sc)
        score2 = sb("score2", [P, NB, HEADS], f32, sc)
        top = sb("top", [P, 2], f32, sc)
        top_all = sb("top_all", [P, 2], f32, sc)
        neg_top = sb("neg_top", [P, 1], f32, sc)
        low_row = sb("low_row", [NG, P], f32, sc)
        outside = sb("outside", [1, 1], i32, sc)
        TSR = 2
        tab = sb("tab", [P, TSR, TABLES, TC, BW], f32, s1)
        XTR = 4
        x1T = sb("x1T", [P, XTR, DK, P], f32, s1)
        Wc = sb("Wc", [P, DK, OUT + 2 * HEADS], f32, s1)
        WcT = sb("WcT", [P, DK, OUT], f32, s1)
        ablk = sb("ablk", [P, DK, 2 * HEADS], f32, s1)
        hst = sb("hst", [P, 4, OUT], f32, s1)
        s1.close()
        HGR = 27
        Hg = sb("Hg", [P, HGR * BLOCKS_PER_GROUP, OUT], f32, sc)
        REMG = 2
        rem = sb("rem", [P, 2, 2, REMG * GE], bf16, s2)
        HOTR = 4
        hot = sb("hot", [P, HOTR, 2, GE], bf16, s2)
        own = sb("own", [P, 2, BLOCKS_PER_GROUP * 2, NT], bf16, s2)
        picked = sb("picked", [P, 2, BLOCKS_PER_GROUP, 2 * TQ], f32, s2)
        s2.close()
        XBR = 3
        xb = sb("xb", [P, XBR, BLOCKS_PER_GROUP, BW], f32, s3)
        in_window = sb("in_window", [P, XBR, BLOCKS_PER_GROUP, P], f32, s3)
        eq_lowb = sb("eq_lowb", [P, P], f32, s3)
        to_u = sb("to_u", [P, 1], i32, s3)
        s3.close()
        sc.close()

        bank = [ctx.enter_context(nc.psum_tensor(f"bank{i}", [P, 512], f32)) for i in range(8)]
        PT, PL1, PG, P2, PY = bank[0:2], bank[2:4], bank[4], bank[5], bank[6:8]

        s_const = sem("s_const")
        s_dc = sem("s_dc")
        s_ldw = sem("s_ldw")
        s_ldx = [sem(f"s_ldx{i}") for i in range(4)]
        s_ldi = sem("s_ldi")
        s_rd = sem("s_rd")
        s_zero = sem("s_zero")
        s_w0 = sem("s_w0")
        s_xh = sem("s_xh")
        s_xl = sem("s_xl")
        s_wh = sem("s_wh")
        s_wl = sem("s_wl")
        s_n0 = sem("s_n0")
        s_n0a = sem("s_n0a")
        s_n0b = sem("s_n0b")
        s_ta = [sem(f"s_ta{i}") for i in range(N0R)]
        s_tb = [sem(f"s_tb{i}") for i in range(N0R)]
        s_ga = [sem(f"s_ga{i}") for i in range(GAR)]
        s_gb = [sem(f"s_gb{i}") for i in range(GBR)]
        s_e = [sem(f"s_e{i}") for i in range(2)]
        s_bc = [sem(f"s_bc{i}") for i in range(2)]
        s_add = sem("s_add")
        s_T = sem("s_T")
        s_tanh1 = sem("s_tanh1")
        s_h1h = sem("s_h1h")
        s_h1l = sem("s_h1l")
        s_L1 = sem("s_L1")
        s_tanh2 = sem("s_tanh2")
        s_h2h = sem("s_h2h")
        s_h2l = sem("s_h2l")
        s_eh = sem("s_eh")
        s_el = sem("s_el")
        s_G = sem("s_G")
        s_gate = sem("s_gate")
        s_L2 = sem("s_L2")
        s_mul = sem("s_mul")
        s_mh = sem("s_mh")
        s_ml = sem("s_ml")
        s_eq = sem("s_eq")
        s_dup = sem("s_dup")
        s_tof = sem("s_tof")
        s_to = sem("s_to")
        s_Y = sem("s_Y")
        s_Yc = sem("s_Yc")
        s_scA = [sem(f"s_scA{i}") for i in range(TABLES)]
        s_scB = sem("s_scB")
        s_xn = sem("s_xn")
        s_ldc = sem("s_ldc")
        s_tab = [sem(f"s_tab{i}") for i in range(TSR)]
        s_sum = sem("s_sum")
        s_low = sem("s_low")
        s_lowp = sem("s_lowp")
        s_lows = sem("s_lows")
        s_cden = sem("s_cden")
        s_cinv = sem("s_cinv")
        s_att = sem("s_att")
        s_res = sem("s_res")
        s_stat = sem("s_stat")
        s_mv = sem("s_mv")
        s_std = sem("s_std")
        s_rstd = sem("s_rstd")
        s_x1 = sem("s_x1")
        s_wa = sem("s_wa")
        s_wac = sem("s_wac")
        s_x1t = sem("s_x1t")
        s_x1c = sem("s_x1c")
        s_H = sem("s_H")
        s_hc = sem("s_hc")
        s_sl = sem("s_sl")
        s_ht = [sem(f"s_ht{i}") for i in range(4)]
        s_rem = [sem(f"s_rem{i}") for i in range(2)]
        s_hot = sem("s_hot")
        s_O = sem("s_O")
        s_pick = sem("s_pick")
        s_own = sem("s_own")
        s_sc = sem("s_sc")
        s_b2 = sem("s_b2")
        s_top = sem("s_top")
        s_ex = sem("s_ex")
        s_hg = [sem(f"s_hg{i}") for i in range(HGR)]
        s_xb = sem("s_xb")
        s_xe = sem("s_xe")
        s_win = sem("s_win")
        s_YB = sem("s_YB")
        s_YBc = sem("s_YBc")
        s_ukeep = sem("s_ukeep")
        s_ubc = sem("s_ubc")
        s_ug = sem("s_ug")
        s_ueq = sem("s_ueq")
        s_udup = sem("s_udup")
        s_utof = sem("s_utof")
        s_uto = sem("s_uto")
        s_ux = sem("s_ux")
        s_up = sem("s_up")
        s_uy = sem("s_uy")
        s_us = sem("s_us")
        s_out = sem("s_out")

        PARTS = 4
        tiles_per_part = -(-NT // PARTS)
        part_of_tile = [t // tiles_per_part for t in range(NT)]

        def part_cols(i):
            return slice(i * tiles_per_part * P, min((i + 1) * tiles_per_part * P, N))

        def ring_total(ring, slot, n):
            return 16 * len([i for i in range(n) if i % ring == slot])

        def group_arrivals(ring, g):
            return 16 * sum(len(blocks_of_group(i)) for i in range(g % ring, g + 1, ring))

        def wait_stage_n0(eng):
            for k in range(N0R):
                eng.wait_ge(s_ta[k], ring_total(N0R, k, NT))
                eng.wait_ge(s_tb[k], ring_total(N0R, k, NT))
            eng.wait_ge(s_rd, 16)
            eng.wait_ge(s_wl, 4)

        def wait_stage_a(eng):
            for k in range(TABLES):
                eng.wait_ge(s_scA[k], ring_total(TABLES, k, NB))

        def tiles_of_chunk(c):
            return range(c * TC, min((c + 1) * TC, NT))

        def load_tables(eng, tables, width, base):
            for c in range(NC):
                u, tiles = base + c, tiles_of_chunk(c)
                if u >= TSR:
                    eng.wait_ge(s_res, NT * ((u - TSR) // NC) + tiles_of_chunk((u - TSR) % NC)[-1] + 1)
                for k, table in enumerate(tables):
                    eng.dma_start(tab[:, u % TSR, k, 0:len(tiles), 0:width],
                                  table[tiles[0] * P:(tiles[-1] + 1) * P, :].rearrange("(t p) d -> p t d", p=P))\
                       .then_inc(s_tab[u % TSR], 16)

        def chunk_arrivals(u):
            return 16 * sum(TABLES if v < NC else 1 for v in range(u % TSR, u + 1, TSR))

        def if_outside(eng):
            eng.wait_ge(s_b2, B2["outside"])
            return eng.If(eng.value_load(outside[0:1, 0:1], min_val=0, max_val=1))

        block = ctx.enter_context(nc.Block())

        DC, B2 = {}, {}

        @block.vector
        def _(dve):
            dc = [0]

            def const(ins, name=None):
                dc[0] += 1
                ins.then_inc(s_dc, 1)
                dve.wait_ge(s_dc, dc[0])
                DC[name] = dc[0]

            def lo(o, full, hi):
                return dve.tensor_tensor(o, full, hi.bitcast(f32), ALU.subtract)

            const(dve.memset(zeros[:, :], 0.0), "zeros")
            const(dve.memset(eps[:, :], LN_EPS), "eps")
            const(dve.memset(mv[:, :, :], 0.0))
            dve.wait_ge(s_const, 2)
            const(dve.tensor_copy(iota_row[:, :], iota_i[:, :]))
            const(dve.tensor_copy(p_f[:, :], p_i[:, :]))
            const(dve.tensor_scalar(ident[:, :], iota_row[:, :], p_f[:, :], None, ALU.is_equal))
            const(dve.tensor_scalar(lower[:, :], iota_row[:, :], p_f[:, :], None, ALU.is_lt))
            const(dve.tensor_scalar(trash[:, :], p_f[:, :], float(N), None, ALU.add))
            const(dve.tensor_copy(tile_row[:, :], iota_row[:, 0:NT]))
            const(dve.memset(W1s[:, :].bitcast(f32), 0.0), "stack")
            dve.wait_ge(s_wh, 1)
            lo(W0l[:, :, :], W0f[:, :, :], W0h[:, :, :]).then_inc(s_wl, 1)
            for i in range(PARTS):
                dve.wait_ge(s_xh, i + 1)
                lo(xTl[:, :, part_cols(i)], xTf[:, :, part_cols(i)], xTh[:, :, part_cols(i)]).then_inc(s_xl, 1)
            dve.wait_ge(s_ldi, 16 * (5 + (E % GE > 0)))
            const(dve.tensor_copy(src_f[:, :], src_c[:, :]))
            const(dve.tensor_copy(dst_f[:, :], dst_c[:, :]))
            const(dve.tensor_scalar(src_t[:, :], src_f[:, :], trash[:, :], None, ALU.subtract))
            for side, ends in enumerate((src_c, dst_c)):
                const(dve.tensor_single_scalar(tile_i[:, :, side], ends[:, :], P.bit_length() - 1,
                                               ALU.logical_shift_right))
            const(dve.tensor_copy(tile_c[:, :, :], tile_i[:, :, :]))
            const(dve.tensor_single_scalar(rem_i[:, :, :], idx_rows[:, :, :], P - 1, ALU.bitwise_and))
            const(dve.tensor_copy(rem_b[:, :, :], rem_i[:, :, :]), "rem")
            for t in range(NT):
                n = rows_of_tile(t)
                dve.wait_ge(s_n0, 2 * t + 1)
                if t >= N0R:
                    dve.wait_ge(s_ta[t % N0R], 16 * (t // N0R))
                dve.tensor_tensor(stA[0:n, t % N0R, :], bank[(2 * t) % 8][0:n, 0:H0], b0b[0:n, :], ALU.add)\
                    .then_inc(s_n0a, 1)
            dve.wait_ge(s_wh, 4)
            lo(W1l[:, :, :], W1f[:, 0:F1, :], W1h[:, :, :])
            lo(W1s[S1[2]:KS, :], W1f[0:R1, F1, :], W1s[0:R1, :]).then_inc(s_wl, 1)
            for m in range(C2):
                k = k2(m) + (m == C2 - 1)
                last = lo(W2l[0:k, m, :], W2f[0:k, m, :], W2h[0:k, m, :])
            last.then_inc(s_wl, 1)
            lo(Wgl[:, :], Wgf[:, :], Wgh[:, :]).then_inc(s_wl, 1)
            wait_stage_n0(dve)
            r = k2(C2 - 1) // 32 * 32
            const(dve.memset(h2h[r:K2, :, C2 - 1, :].bitcast(f32), 1.0))
            const(dve.memset(h2l[r:K2, :, C2 - 1, :].bitcast(f32), 0.0))
            const(dve.memset(mh[:, :, :, OUT:OUT + 1].bitcast(f32), 1.0))
            const(dve.memset(mh[:, :, :, OUT + 1:AW].bitcast(f32), 0.0))
            const(dve.memset(h1s[:, :, :].bitcast(f32), 0.0))
            const(dve.memset(ml[:, :, :, OUT:AW].bitcast(f32), 0.0), "ones")

            def add_rows(g):
                dve.wait_ge(s_ga[g % GAR], group_arrivals(GAR, g))
                dve.wait_ge(s_gb[g % GBR], group_arrivals(GBR, g))
                for run in same_rows(blocks_of_group(g)):
                    n, k = rows_of_block(run[0]), len(run)
                    a, b = run[0] % (GAR * BLOCKS_PER_GROUP), run[0] % (GBR * BLOCKS_PER_GROUP)
                    last = dve.tensor_tensor(GA[0:n, a:a + k, :], GA[0:n, a:a + k, :], GB[0:n, b:b + k, :], ALU.add)
                last.then_inc(s_add, 1)

            def h1_lo(g, c):
                u, n = C1 * g + c, edges_of_group(g)
                dve.wait_ge(s_h1h, u + 1)
                if c < F1:
                    last = lo(h1l[:, g % 2, c, 0:n], h1f[:, c, 0:n], h1h[:, g % 2, c, 0:n])
                else:
                    last = lo(h1s[S1[1]:S1[1] + R1, g % 2, 0:n], h1f[0:R1, c, 0:n], h1s[0:R1, g % 2, 0:n])
                last.then_inc(s_h1l, 1)

            def h2_lo(g, m):
                u, n = C2 * g + m, edges_of_group(g)
                dve.wait_ge(s_h2h, u + 1)
                lo(h2l[0:k2(m), g % 2, m, 0:n], h2f[0:k2(m), m, 0:n], h2h[0:k2(m), g % 2, m, 0:n]).then_inc(s_h2l, 1)

            def edge_lo(g):
                n = edges_of_group(g)
                dve.wait_ge(s_eh, g + 1)
                lo(el[:, g % 2, 0:n], ef[:, g % 2, 0:n], eh[:, g % 2, 0:n]).then_inc(s_el, 1)

            def multiply(q):
                k, n = len(blocks_of_pair(q)), rows_of_block(2 * q)
                dve.wait_ge(s_L2, q + 1)
                dve.wait_ge(s_gate, q + 1)
                if q >= 2:
                    dve.wait_ge(s_ml, q - 1)
                dve.tensor_tensor(mf[0:n, q % 2, 0:k, :].rearrange("p i d -> p (i d)"), P2[0:n, 0:k * OUT],
                                  gate[0:n, q % 2, 0:k, :].rearrange("p i d -> p (i d)"), ALU.mult).then_inc(s_mul, 1)

            def gated_lo(q):
                k, n = len(blocks_of_pair(q)), rows_of_block(2 * q)
                dve.wait_ge(s_mh, q + 1)
                lo(ml[0:n, q % 2, 0:k, 0:OUT], mf[0:n, q % 2, 0:k, :], mh[0:n, q % 2, 0:k, 0:OUT]).then_inc(s_ml, 1)

            def equality(g, i):
                dve.wait_ge(s_bc[g % 2], 16 * (g // 2 + 1))
                for b in blocks_of_group(g)[2 * i:2 * i + 2]:
                    n, j = rows_of_block(b), b % BLOCKS_PER_GROUP
                    same = bcast_i[0:n, g % 2, j * P:j * P + n]
                    if b >= EQR:
                        dve.wait_ge(s_Y, b - EQR + 1)
                    dve.tensor_scalar(eqA[0:n, b % EQR, 0:n], same, src_f[0:n, b:b + 1], None, ALU.is_equal)\
                        .then_inc(s_eq, 1)
                    if b >= 2:
                        dve.wait_ge(s_dup, b - 1)
                    dve.scalar_tensor_tensor(eq_low[0:n, b % 2, 0:n], same, src_f[0:n, b:b + 1], lower[0:n, 0:n],
                                             ALU.is_equal, ALU.mult, accum_out=dup[0:n, b:b + 1]).then_inc(s_dup, 1)

            def table_rows(g):
                dve.wait_ge(s_dup, blocks_of_group(g)[-1] + 1)
                runs = same_rows(blocks_of_group(g))
                if g >= 1:
                    dve.wait_ge(s_to, g)
                for run in runs:
                    n, b, k = rows_of_block(run[0]), run[0], len(run)
                    j = b % BLOCKS_PER_GROUP
                    last = dve.scalar_tensor_tensor(to_f[0:n, j:j + k], dup[0:n, b:b + k], 0.0,
                                                    src_t[0:n, b:b + k], ALU.is_equal, ALU.mult)
                last.then_inc(s_tof, 1)
                dve.wait_ge(s_tof, g + 1)
                for run in runs:
                    n, b, k = rows_of_block(run[0]), run[0], len(run)
                    j = b % BLOCKS_PER_GROUP
                    last = dve.tensor_scalar(to_a[0:n, b:b + k], to_f[0:n, j:j + k], trash[0:n, :], None, ALU.add)
                last.then_inc(s_to, 1)

            for s in range(-2, NG + 1):
                if 0 <= s - 1 < NG:
                    h2_lo(s - 1, 2)
                if s + 2 < NG:
                    add_rows(s + 2)
                if 0 <= s < NG:
                    h2_lo(s, 0)
                    edge_lo(s)
                for q in pairs(s - 1)[0:1]:
                    multiply(q)
                if 0 <= s < NG:
                    equality(s, 0)
                for q in pairs(s - 1)[0:1]:
                    gated_lo(q)
                if 0 <= s + 1 < NG:
                    h1_lo(s + 1, 0)
                    h1_lo(s + 1, 1)
                if 0 <= s < NG:
                    h2_lo(s, 1)
                for q in pairs(s - 1)[1:2]:
                    multiply(q)
                if 0 <= s < NG:
                    equality(s, 1)
                    table_rows(s)
                for q in pairs(s - 1)[1:2]:
                    gated_lo(q)
                if 0 <= s + 1 < NG:
                    h1_lo(s + 1, 2)
                    h1_lo(s + 1, 3)

            def residual(c, u, width, divide):
                tiles = tiles_of_chunk(c)
                k = len(tiles)
                dve.wait_ge(s_tab[u % TSR], chunk_arrivals(u))
                divide(tab[:, u % TSR, :, 0:k, 0:width], tiles, k, u)
                for t in tiles:
                    n = rows_of_tile(t)
                    dve.wait_ge(s_res, NT * (u // NC) + t + 1)
                    dve.bn_stats(stats[0:n, t, :], xn[0:n, t, :]).then_inc(s_stat, 1)
                for t in tiles:
                    n = rows_of_tile(t)
                    dve.wait_ge(s_stat, NT * (u // NC) + t + 1)
                    dve.bn_aggr(mv[0:n, t, :], stats[0:n, t, :]).then_inc(s_mv, 1)

            def mean(rows, tiles, k, u):
                t0 = tiles[0]
                dve.tensor_tensor(rows[:, 0], rows[:, 0], rows[:, 1], ALU.add).then_inc(s_sum, 1)
                dve.wait_ge(s_sum, u + 1)
                dve.tensor_scalar(cden[:, t0:t0 + k, 0:1], rows[:, 0, :, OUT:OUT + 1], 1.0, None, ALU.max)\
                    .then_inc(s_cden, 1)
                dve.wait_ge(s_cden, u + 1)
                dve.reciprocal(cinv[:, t0:t0 + k, 0:1], cden[:, t0:t0 + k, 0:1]).then_inc(s_cinv, 1)
                dve.wait_ge(s_cinv, u + 1)
                for j, t in enumerate(tiles):
                    n = rows_of_tile(t)
                    dve.scalar_tensor_tensor(xn[0:n, t, :], rows[0:n, 0, j, 0:OUT], cinv[0:n, t, 0:1],
                                             xn[0:n, t, :], ALU.mult, ALU.add).then_inc(s_res, 1)

            def attention(rows, tiles, k, u):
                t0 = tiles[0]
                dve.tensor_scalar(cden[:, t0:t0 + k, :], rows[:, 0, :, OUT:BW], DENOM_EPS, None, ALU.add)\
                    .then_inc(s_cden, 1)
                dve.wait_ge(s_cden, u + 1)
                dve.reciprocal(cinv[:, t0:t0 + k, :], cden[:, t0:t0 + k, :]).then_inc(s_cinv, 1)
                dve.wait_ge(s_cinv, u + 1)
                heads = rows[:, 0, :, 0:OUT].rearrange("p t (h d) -> p t h d", d=HD)
                dve.tensor_tensor(heads, heads, cinv[:, t0:t0 + k, :].unsqueeze(3).to_broadcast([P, k, HEADS, HD]),
                                  ALU.mult).then_inc(s_att, 1)
                dve.wait_ge(s_att, u - NC + 1)
                for j, t in enumerate(tiles):
                    n = rows_of_tile(t)
                    dve.tensor_tensor(xn[0:n, t, :], xn[0:n, t, :], rows[0:n, 0, j, 0:OUT], ALU.add).then_inc(s_res, 1)

            def normalise(base):
                dve.wait_ge(s_std, base // NT + 1)
                dve.reciprocal(rstd[:, :], std[:, :]).then_inc(s_rstd, 1)
                dve.wait_ge(s_rstd, base // NT + 1)
                for t in range(NT):
                    n = rows_of_tile(t)
                    dve.tensor_scalar(xn[0:n, t, :], xn[0:n, t, :], mv[0:n, t, 0:1], rstd[0:n, t:t + 1],
                                      ALU.subtract, ALU.mult).then_inc(s_x1, 1)

            def node_scores(t):
                n = rows_of_tile(t)
                dve.wait_ge(s_H, t + 1)
                dve.tensor_copy(node[0:n, :, t * HEADS:(t + 1) * HEADS],
                                bank[t % 4][0:n, OUT:OUT + 2 * HEADS].rearrange("p (s h) -> p s h", h=HEADS))\
                    .then_inc(s_sl, 1)

            whole, rest = E // GE, E % GE
            if rest:
                const(dve.tensor_reduce(low_g[0:NG, 0:1], dst_g[0:NG, 0:rest], AX.X, ALU.min))
                const(dve.tensor_reduce(low_g[0:whole, 1:2], dst_g[0:whole, rest:GE], AX.X, ALU.min))
                const(dve.tensor_tensor(low_g[0:whole, 0:1], low_g[0:whole, 0:1], low_g[0:whole, 1:2], ALU.min))
            else:
                const(dve.tensor_reduce(low_g[:, 0:1], dst_g[:, :], AX.X, ALU.min))
            wait_stage_a(dve)
            dve.tensor_scalar(low_row[:, :], iota_row[0:NG, :], 0.0, low_g[:, 0:1], ALU.mult, ALU.add).then_inc(s_low, 1)
            const(dve.memset(ablk[:, :, :], 0.0), "ablk")
            const(dve.memset(node[:, :, :], 0.0))
            dve.wait_ge(s_xn, 48)
            for c in range(NC):
                residual(c, c, AW, mean)
            dve.wait_ge(s_lowp, 1)
            dve.tensor_copy(low_all[:, :], bank[1][:, 0:NG]).then_inc(s_lows, 1)
            dve.wait_ge(s_lows, 1)
            dve.tensor_scalar(to_b[:, :], low_all[:, :], p_f[:, :], None, ALU.add).then_inc(s_lows, 1)
            for g0, g1 in ((0, NB // BLOCKS_PER_GROUP), (NB // BLOCKS_PER_GROUP, NG)):
                b0_, k = g0 * BLOCKS_PER_GROUP, min(BLOCKS_PER_GROUP, NB - g0 * BLOCKS_PER_GROUP)
                if g1 > g0:
                    v = slice(b0_, b0_ + (g1 - g0) * k)
                    const(dve.tensor_tensor(dst_rel[:, v].rearrange("p (g k) -> p g k", k=k),
                                            dst_f[:, v].rearrange("p (g k) -> p g k", k=k),
                                            low_all[:, g0:g1].unsqueeze(2).to_broadcast([P, g1 - g0, k]),
                                            ALU.subtract))
            normalise(0)
            for t in range(NT):
                node_scores(t)
            dve.wait_ge(s_sl, NT)
            const(dve.tensor_copy(node_p[:, 0], node[:, :, :]))
            const(dve.tensor_tensor(node_rest[:, :, :], node[:, :, :], node_p[:, 0], ALU.subtract))
            const(dve.tensor_copy(node_p[:, 1], node_rest[:, :, :]))
            const(dve.tensor_tensor(node_p[:, 2], node_rest[:, :, :], node_p[:, 1], ALU.subtract), "node")

            def one_hot(g):
                i, n = g // REMG, edges_of_group(g)
                if g % REMG == 0:
                    dve.wait_ge(s_rem[i % 2], 16 * (i // 2 + 1))
                if g >= HOTR:
                    dve.wait_ge(s_O, g - HOTR + 1)
                a = (g % REMG) * GE
                for side in range(2):
                    dve.tensor_scalar(hot[:, g % HOTR, side, 0:n], rem[:, i % 2, side, a:a + n], p_f[:, :], None,
                                      ALU.is_equal).then_inc(s_hot, 1)

            def own_tile(g):
                if g >= 2:
                    dve.wait_ge(s_pick, 2 * (g - 1))
                for run in same_rows(blocks_of_group(g)):
                    n, b, k = rows_of_block(run[0]), run[0], len(run)
                    j = b % BLOCKS_PER_GROUP
                    last = dve.tensor_tensor(
                        own[0:n, g % 2, 2 * j:2 * (j + k), :], tile_row[0:n, :].unsqueeze(1).to_broadcast([n, 2 * k, NT]),
                        tile_c[0:n, b:b + k, :].rearrange("p b s -> p (b s)").unsqueeze(2).to_broadcast([n, 2 * k, NT]),
                        ALU.is_equal)
                last.then_inc(s_own, 1)

            def pick(g):
                dve.wait_ge(s_O, g + 1)
                dve.wait_ge(s_own, g + 1)
                if g >= 2:
                    dve.wait_ge(s_sc, g - 1)
                for half in range(2):
                    for run in same_rows(blocks_of_group(g)[2 * half:2 * half + 2]):
                        n, j, k = rows_of_block(run[0]), run[0] % BLOCKS_PER_GROUP, len(run)
                        a = (j - 2 * half) * 2 * TQ
                        last = dve.tensor_tensor(
                            picked[0:n, g % 2, j:j + k, :].rearrange("p b (s t h) -> p (b s) t h", s=2, h=HEADS),
                            bank[(2 * g + half) % 8][0:n, a:a + k * 2 * TQ].rearrange("p (s t h) -> p s t h", t=NT, h=HEADS),
                            own[0:n, g % 2, 2 * j:2 * (j + k), :].unsqueeze(3).to_broadcast([n, 2 * k, NT, HEADS]),
                            ALU.mult)
                    last.then_inc(s_pick, 1)

            def edge_scores(g):
                dve.wait_ge(s_pick, 2 * g + 2)
                for run in same_rows(blocks_of_group(g)):
                    n, b, k = rows_of_block(run[0]), run[0], len(run)
                    j = b % BLOCKS_PER_GROUP
                    last = dve.tensor_reduce(score[0:n, b:b + k, :],
                                             picked[0:n, g % 2, j:j + k, :].rearrange("p b (u h) -> p b h u", h=HEADS),
                                             AX.X, ALU.add)
                last.then_inc(s_sc, 1)

            for g in range(-2, NG + 1):
                if g + 2 < NG:
                    one_hot(g + 2)
                if 0 <= g < NG:
                    own_tile(g)
                    pick(g)
                if g >= 1:
                    edge_scores(g - 1)
            b2 = [0]

            def step(ins, name=None):
                b2[0] += 1
                ins.then_inc(s_b2, 1)
                dve.wait_ge(s_b2, b2[0])
                B2[name] = b2[0]

            dve.wait_ge(s_sc, NG)
            runs = same_rows(range(NB))
            for run in runs:
                n, b, k = rows_of_block(run[0]), run[0], len(run)
                v = score[0:n, b:b + k, :]
                step(dve.tensor_scalar(score2[0:n, b:b + k, :], v, NEG_SLOPE, None, ALU.mult))
                step(dve.tensor_tensor(score2[0:n, b:b + k, :], score2[0:n, b:b + k, :], v, ALU.max))
            if rows_of_block(NB - 1) < P:
                step(dve.memset(score[:, NB - 1, :], LOWEST))
            for run in runs:
                n, b, k = rows_of_block(run[0]), run[0], len(run)
                step(dve.tensor_tensor(score[0:n, b:b + k, :], score2[0:n, b:b + k, :],
                                       w_c[0:n, b:b + k].unsqueeze(2).to_broadcast([n, k, HEADS]), ALU.mult))
            step(dve.tensor_reduce(top[:, 1:2], dst_rel[:, :], AX.X, ALU.max))
            step(dve.tensor_reduce(top[:, 0:1], score[:, :, :].rearrange("p b h -> p (b h)"), AX.X, ALU.max), "top")
            dve.wait_ge(s_top, 1)
            step(dve.tensor_scalar(neg_top[:, :], top_all[:, 0:1], -1.0, None, ALU.mult), "neg")
            step(dve.tensor_scalar(outside[:, :], top_all[0:1, 1:2], float(WB), None, ALU.is_ge), "outside")

            def weigh(o, rows, weights, n, k):
                return dve.tensor_tensor(o.rearrange("p k (h d) -> p k h d", d=HD),
                                         rows.rearrange("p k (h d) -> p k h d", d=HD),
                                         weights.unsqueeze(3).to_broadcast([n, k, HEADS, HD]), ALU.mult)

            dve.wait_ge(s_ex, 1)
            for g in range(NG):
                if g >= XBR:
                    dve.wait_ge(s_YB, g - XBR + 1)
                runs = same_rows(blocks_of_group(g))
                for run in runs:
                    n, b, k = rows_of_block(run[0]), run[0], len(run)
                    j = b % BLOCKS_PER_GROUP
                    last = dve.tensor_tensor(in_window[0:n, g % XBR, j:j + k, :],
                                             iota_row[0:n, :].unsqueeze(1).to_broadcast([n, k, WB]),
                                             dst_rel[0:n, b:b + k].unsqueeze(2).to_broadcast([n, k, WB]), ALU.is_equal)
                last.then_inc(s_win, 1)
                dve.wait_ge(s_hg[g % HGR], group_arrivals(HGR, g))
                for run in runs:
                    n, b, k = rows_of_block(run[0]), run[0], len(run)
                    j, r = b % BLOCKS_PER_GROUP, b % (HGR * BLOCKS_PER_GROUP)
                    last = weigh(xb[0:n, g % XBR, j:j + k, 0:OUT], Hg[0:n, r:r + k, :], score2[0:n, b:b + k, :], n, k)
                last.then_inc(s_xb, 1)
            with if_outside(dve):
                dve.wait_ge(s_YB, NG)
                for run in same_rows(range(NB)):
                    n, b, k = rows_of_block(run[0]), run[0], len(run)
                    last = dve.scalar_tensor_tensor(
                        score[0:n, b:b + k, :], dst_rel[0:n, b:b + k].unsqueeze(2).to_broadcast([n, k, HEADS]),
                        float(WB), score2[0:n, b:b + k, :], ALU.is_ge, ALU.mult)
                last.then_inc(s_ukeep, 1)
                dve.wait_ge(s_ukeep, 1)
                dve.wait_ge(s_dup, NB)
                for b in range(NB):
                    n = rows_of_block(b)
                    dve.wait_ge(s_ubc, 16 * (b + 1))
                    if b >= 1:
                        dve.wait_ge(s_up, b)
                        dve.wait_ge(s_us, 16 * b)
                    same = bcast_i[0:n, 0, 0:n]
                    dve.tensor_scalar(in_window[0:n, 0, 0, 0:n], same, dst_f[0:n, b:b + 1], None, ALU.is_equal)\
                        .then_inc(s_ueq, 1)
                    dve.scalar_tensor_tensor(eq_lowb[0:n, 0:n], same, dst_f[0:n, b:b + 1], lower[0:n, 0:n],
                                             ALU.is_equal, ALU.mult, accum_out=dup[0:n, b:b + 1]).then_inc(s_udup, 1)
                    dve.wait_ge(s_udup, b + 1)
                    dve.tensor_scalar(to_f[0:n, 0:1], dst_f[0:n, b:b + 1], trash[0:n, :], None, ALU.subtract)\
                        .then_inc(s_utof, 1)
                    dve.wait_ge(s_utof, 2 * b + 1)
                    dve.scalar_tensor_tensor(to_f[0:n, 1:2], dup[0:n, b:b + 1], 0.0, to_f[0:n, 0:1],
                                             ALU.is_equal, ALU.mult).then_inc(s_utof, 1)
                    dve.wait_ge(s_utof, 2 * b + 2)
                    dve.tensor_scalar(to_u[0:n, :], to_f[0:n, 1:2], trash[0:n, :], None, ALU.add).then_inc(s_uto, 1)
                    dve.wait_ge(s_uto, b + 1)
                    dve.wait_ge(s_ug, 16 * (b + 1))
                    dve.tensor_copy(xb[0:n, 0, 0, OUT:BW], score[0:n, b, :])
                    weigh(xb[0:n, 0, 0:1, 0:OUT], Hg[0:n, 0:1, :], score[0:n, b:b + 1, :], n, 1).then_inc(s_ux, 1)

            for c in range(NC):
                residual(c, NC + c, BW, attention)
            normalise(NT)

        @block.sync
        def _(sp):
            sp.dma_start(W0f[:, :, :], W0.rearrange("(k p) n -> p k n", p=P)).then_inc(s_w0, 16)
            for i in range(PARTS):
                sp.dma_start(xTf[:, :, part_cols(i)],
                             xT[:, part_cols(i)].rearrange("(k p) n -> p k n", p=P)).then_inc(s_ldx[i], 16)
            sp.dma_start(b0b[:, :], b0.partition_broadcast(P)).then_inc(s_w0, 16)
            sp.dma_start(src_c[:, :], src_cols).then_inc(s_ldi, 16)
            sp.dma_start(dst_c[:, :], dst_cols).then_inc(s_ldi, 16)
            full = (E // GE) * GE
            sp.dma_start(dst_g[0:E // GE, :], dst_row[0:full].rearrange("(g e) -> g e", e=GE)).then_inc(s_ldi, 16)
            if full < E:
                sp.dma_start(dst_g[E // GE:NG, 0:E - full], dst_row[full:E].rearrange("(g e) -> g e", g=1))\
                  .then_inc(s_ldi, 16)
            sp.dma_start(idx_rows[:, 0, :], src_row.rearrange("(p j) -> p j", p=RQ)).then_inc(s_ldi, 16)
            sp.dma_start(idx_rows[:, 1, :], dst_row.rearrange("(p j) -> p j", p=RQ)).then_inc(s_ldi, 16)
            for c in range(C1):
                sp.dma_start(W1f[0:k1(c), c, :], W1[c * P:c * P + k1(c), :]).then_inc(s_ldw, 16)
            for m in range(C2):
                sp.dma_start(W2f[0:k2(m), m, :], W2[m * K2:m * K2 + k2(m), :]).then_inc(s_ldw, 16)
                sp.dma_start(b1c[0:k2(m), m:m + 1],
                             b1[m * K2:m * K2 + k2(m)].rearrange("(p a) -> p a", a=1)).then_inc(s_ldw, 16)
            sp.dma_start(W2f[k2(C2 - 1):k2(C2 - 1) + 1, C2 - 1, :],
                         b2.rearrange("(a n) -> a n", a=1)).then_inc(s_ldw, 16)
            sp.dma_start(Wgf[:, :], Wg).then_inc(s_ldw, 16)
            full = (N // P) * P
            sp.dma_start(xn[:, 0:N // P, :], x[0:full, :].rearrange("(t p) d -> p t d", p=P)).then_inc(s_xn, 16)
            sp.dma_start(xn[0:N - full, N // P, :], x[full:N, :]).then_inc(s_xn, 16)
            sp.dma_start(w_c[:, :], w_cols).then_inc(s_xn, 16)
            for t in range(NT):
                n = rows_of_tile(t)
                sp.wait_ge(s_n0a, t + 1)
                sp.dma_start(TA[t * P:t * P + n, :], stA[0:n, t % N0R, :]).then_inc(s_ta[t % N0R], 16)
                sp.wait_ge(s_n0b, t + 1)
                sp.dma_start(TB[t * P:t * P + n, :], stB[0:n, t % N0R, :]).then_inc(s_tb[t % N0R], 16)
            sp.wait_ge(s_dc, DC["rem"])
            sp.dma_start(RD.rearrange("k (p j) -> p k j", p=RQ), rem_b[:, :, :]).then_inc(s_rd, 16)
            wait_stage_n0(sp)
            for g in range(NG):
                n = edges_of_group(g)
                if g >= 2:
                    sp.wait_ge(s_eh, g - 1)
                    sp.wait_ge(s_el, g - 1)
                sp.dma_start(ef[:, g % 2, 0:n], eT[:, g * GE:g * GE + n]).then_inc(s_e[g % 2], 16)
                if g >= 2:
                    sp.wait_ge(s_dup, g * BLOCKS_PER_GROUP - BLOCKS_PER_GROUP)
                sp.dma_start(bcast_i[:, g % 2, 0:n],
                             src_row[g * GE:g * GE + n].partition_broadcast(P)).then_inc(s_bc[g % 2], 16)
                for table, width in {0: [(accA[0], AW)], 1: [(accA[1], AW)], 8: [(accB, BW)]}.get(g, []):
                    sp.dma_start(table.rearrange("(t p) d -> p t d", p=P),
                                 zeros[:, 0:width].unsqueeze(1).to_broadcast([P, TR // P, width])).then_inc(s_zero, 16)
            wait_stage_a(sp)
            sp.dma_start(Wc[:, :, 0:OUT], Wcat.rearrange("(k p) n -> p k n", p=P)).then_inc(s_ldc, 16)
            sp.dma_start(WcT[:, :, :], WcatT.rearrange("(k p) n -> p k n", p=P)).then_inc(s_ldc, 16)
            sp.wait_ge(s_dc, DC["ablk"])
            for h in range(HEADS):
                k, r = divmod(h * HD, P)
                sp.dma_start(ablk[r:r + HD, k, h:h + 1], a_src[h, :, :]).then_inc(s_ldc, 16)
                sp.dma_start(ablk[r:r + HD, k, HEADS + h:HEADS + h + 1], a_dst[h, :, :]).then_inc(s_ldc, 16)
            load_tables(sp, accA, AW, 0)
            for t in range(NT):
                n = rows_of_tile(t)
                sp.wait_ge(s_hc, t + 1)
                sp.dma_start(HT[t * P:t * P + n, :], hst[0:n, t % 4, :]).then_inc(s_ht[t % 4], 16)
            for i in range(0, -(-NG // REMG)):
                a, n = i * REMG * GE, min(REMG * GE, E - i * REMG * GE)
                if i == 0:
                    sp.wait_ge(s_rd, 16)
                if i >= 2:
                    sp.wait_ge(s_hot, 2 * (i - 1) * REMG)
                sp.dma_start(rem[:, i % 2, :, 0:n], RD[:, a:a + n].partition_broadcast(P)).then_inc(s_rem[i % 2], 16)
            with if_outside(sp):
                for b in range(NB):
                    n = rows_of_block(b)
                    if b >= 1:
                        sp.wait_ge(s_udup, b)
                    sp.dma_start(bcast_i[:, 0, 0:n], dst_row[b * P:b * P + n].partition_broadcast(P)).then_inc(s_ubc, 16)
                sp.wait_ge(s_us, 16 * NB)
            sp.wait_ge(s_scB, 16 * NG)
            load_tables(sp, [accB], BW, NC)
            for t in range(NT):
                n = rows_of_tile(t)
                sp.wait_ge(s_x1, NT + t + 1)
                sp.dma_start(out[t * P:t * P + n, :], xn[0:n, t, :]).then_inc(s_out, 16)
            sp.wait_ge(s_out, 16 * NT)

        @block.gpsimd
        def _(pool):
            pool.iota(iota_i[:, :], pattern=[[1, P]], base=0, channel_multiplier=0).then_inc(s_const, 1)
            pool.iota(p_i[:, :], pattern=[[0, 1]], base=0, channel_multiplier=1).then_inc(s_const, 1)
            wait_stage_n0(pool)

            def add_to_table(table, rows, sums):
                return pool.indirect_dma_start(
                    out=table, out_offset=bass.IndirectOffsetOnAxis(ap=rows, axis=0), in_=sums, in_offset=None,
                    bounds_check=TR - 1, oob_is_err=True, compute_op=ALU.add)

            def gather_a(b, g):
                n = rows_of_block(b)
                pool.indirect_dma_start(
                    out=GA[0:n, b % (GAR * BLOCKS_PER_GROUP), :], out_offset=None, in_=TA,
                    in_offset=bass.IndirectOffsetOnAxis(ap=src_c[0:n, b:b + 1], axis=0)).then_inc(s_ga[g % GAR], 16)

            def gather_b(b, g):
                n = rows_of_block(b)
                pool.indirect_dma_start(
                    out=GB[0:n, b % (GBR * BLOCKS_PER_GROUP), :], out_offset=None, in_=TB,
                    in_offset=bass.IndirectOffsetOnAxis(ap=dst_c[0:n, b:b + 1], axis=0)).then_inc(s_gb[g % GBR], 16)

            def scatter_a(b):
                n = rows_of_block(b)
                pool.wait_ge(s_Yc, b + 1)
                if b >= TABLES:
                    pool.wait_ge(s_scA[b % TABLES], 16 * (b // TABLES))
                add_to_table(accA[b % TABLES], to_a[0:n, b:b + 1], ystage[0:n, b % Y_RING, 0:AW])\
                    .then_inc(s_scA[b % TABLES], 16)

            for s in range(-3, NG + SUM_LAG):
                ahead, behind = s + 3, s - SUM_LAG
                if behind == 0:
                    pool.wait_ge(s_zero, 16 * TABLES)
                for j in range(BLOCKS_PER_GROUP):
                    if 0 <= ahead < NG and j < len(blocks_of_group(ahead)):
                        if j == 0 and ahead >= GAR:
                            pool.wait_ge(s_T, C1 * (ahead - GAR + 1))
                        if j == 0 and ahead >= GBR:
                            pool.wait_ge(s_add, ahead - GBR + 1)
                        gather_a(blocks_of_group(ahead)[j], ahead)
                        gather_b(blocks_of_group(ahead)[j], ahead)
                    if 0 <= behind < NG and j < len(blocks_of_group(behind)):
                        if j == 0:
                            pool.wait_ge(s_to, behind + 1)
                        scatter_a(blocks_of_group(behind)[j])

            def gather_h_rows(b, slot, landed):
                n = rows_of_block(b)
                pool.indirect_dma_start(
                    out=Hg[0:n, slot, :], out_offset=None, in_=HT,
                    in_offset=bass.IndirectOffsetOnAxis(ap=src_c[0:n, b:b + 1], axis=0)).then_inc(landed, 16)

            def gather_h(g):
                if g >= HGR:
                    pool.wait_ge(s_xb, g - HGR + 1)
                for b in blocks_of_group(g):
                    gather_h_rows(b, b % (HGR * BLOCKS_PER_GROUP), s_hg[g % HGR])

            def scatter_b(g):
                pool.wait_ge(s_YBc, g + 1)
                if g >= 1:
                    pool.wait_ge(s_scB, 16 * g)
                add_to_table(accB, to_b[:, g:g + 1], ystage[:, g % Y_RING, :]).then_inc(s_scB, 16)

            for k in range(4):
                pool.wait_ge(s_ht[k], ring_total(4, k, NT))
            for g in range(min(HGR, NG)):
                gather_h(g)
            pool.wait_ge(s_b2, B2["top"])
            pool.partition_all_reduce(top_all[:, :], top[:, :], P, bass.bass_isa.ReduceOp.max).then_inc(s_top, 1)
            pool.wait_ge(s_lows, 2)
            pool.wait_ge(s_zero, 16 * (TABLES + 1))
            for g in range(NG + 2):
                if HGR <= g + HGR - 2 < NG:
                    gather_h(g + HGR - 2)
                if g >= 2:
                    scatter_b(g - 2)
            with if_outside(pool):
                pool.wait_ge(s_scB, 16 * NG)
                for b in range(NB):
                    n = rows_of_block(b)
                    if b >= 1:
                        pool.wait_ge(s_ux, b)
                    else:
                        pool.wait_ge(s_xb, NG)
                    gather_h_rows(b, 0, s_ug)
                    pool.wait_ge(s_uto, b + 1)
                    pool.wait_ge(s_uy, b + 1)
                    if b >= 1:
                        pool.wait_ge(s_us, 16 * b)
                    add_to_table(accB, to_u[0:n, :], ystage[0:n, 0, :]).then_inc(s_us, 16)

        @block.tensor
        def _(pe):
            def split_product(o, lh, ll, rh, rl, first, last):
                pe.matmul(o, lh, rh, start=first, stop=False)
                pe.matmul(o, lh, rl, start=False, stop=False)
                return pe.matmul(o, ll, rh, start=False, stop=last)

            pe.wait_ge(s_wl, 1)
            for t in range(NT):
                n = rows_of_tile(t)
                pe.wait_ge(s_xl, part_of_tile[t] + 1)
                for half in range(2):
                    u = 2 * t + half
                    if u >= 8:
                        pe.wait_ge(s_n0a if half == 0 else s_n0b, t - 3)
                    o = bank[u % 8][0:n, 0:H0]
                    for k in range(DK):
                        last = split_product(o, xTh[:, k, t * P:t * P + n], xTl[:, k, t * P:t * P + n],
                                             W0h[:, half * DK + k, :], W0l[:, half * DK + k, :],
                                             k == 0, k == DK - 1)
                    last.then_inc(s_n0, 1)

            def transpose_chunk(g, c):
                u = C1 * g + c
                if c == 0:
                    pe.wait_ge(s_add, g + 1)
                if u >= 2:
                    pe.wait_ge(s_tanh1, u - 1)
                for j, b in enumerate(blocks_of_group(g)):
                    n = rows_of_block(b)
                    last = pe.transpose(PT[u % 2][0:k1(c), j * P:j * P + n],
                                        GA[0:n, b % (GAR * BLOCKS_PER_GROUP), c * P:c * P + k1(c)],
                                        ident[0:n, 0:n])
                last.then_inc(s_T, 1)

            def hidden2(g, m):
                u, n = C2 * g + m, edges_of_group(g)
                if u >= 2:
                    pe.wait_ge(s_tanh2, u - 1)
                o = PL1[u % 2][0:k2(m), 0:n]
                ms = slice(m * K2, m * K2 + k2(m))
                for c in range(F1):
                    if m == 0:
                        pe.wait_ge(s_h1l, C1 * g + c + 1)
                    split_product(o, W1h[:, c, ms], W1l[:, c, ms],
                                  h1h[:, g % 2, c, 0:n], h1l[:, g % 2, c, 0:n], c == 0, False)
                if m == 0:
                    pe.wait_ge(s_h1l, C1 * (g + 1))
                pe.matmul(o, W1s[:, ms], h1s[:, g % 2, 0:n], start=False, stop=True).then_inc(s_L1, 1)

            def gate_pair(g, q):
                pe.wait_ge(s_el, g + 1)
                if q >= 1:
                    pe.wait_ge(s_gate, q)
                for i, b in enumerate(blocks_of_pair(q)):
                    n, a = rows_of_block(b), (b - g * BLOCKS_PER_GROUP) * P
                    last = split_product(PG[0:n, i * OUT:(i + 1) * OUT], eh[:, g % 2, a:a + n],
                                         el[:, g % 2, a:a + n], Wgh[:, :], Wgl[:, :], True, True)
                last.then_inc(s_G, 1)

            def output_pair(g, q):
                if q >= 1:
                    pe.wait_ge(s_mul, q)
                for i, b in enumerate(blocks_of_pair(q)):
                    n, a = rows_of_block(b), (b - g * BLOCKS_PER_GROUP) * P
                    for m in range(C2):
                        if q % 2 == 0 and i == 0:
                            pe.wait_ge(s_h2l, C2 * g + m + 1)
                        k = k2(m) + (m == C2 - 1)
                        last = split_product(P2[0:n, i * OUT:(i + 1) * OUT], h2h[0:k, g % 2, m, a:a + n],
                                             h2l[0:k, g % 2, m, a:a + n], W2h[0:k, m, :], W2l[0:k, m, :],
                                             m == 0, m == C2 - 1)
                last.then_inc(s_L2, 1)

            def block_sums(b):
                n, q = rows_of_block(b), b // 2
                pe.wait_ge(s_ml, q + 1)
                pe.wait_ge(s_eq, b + 1)
                if b >= 2:
                    pe.wait_ge(s_Yc, b - 1)
                o = PY[b % 2][0:n, 0:AW]
                pe.matmul(o, eqA[0:n, b % EQR, 0:n], mh[0:n, q % 2, b % 2, :], start=True, stop=False)
                pe.matmul(o, eqA[0:n, b % EQR, 0:n], ml[0:n, q % 2, b % 2, :], start=False, stop=True)\
                    .then_inc(s_Y, 1)

            pe.wait_ge(s_n0a, NT)
            pe.wait_ge(s_n0b, NT)
            pe.wait_ge(s_wl, 4)
            pe.wait_ge(s_dc, DC["ones"])
            def pair_sums(g, i):
                for q in pairs(g)[i:i + 1]:
                    for b in blocks_of_pair(q):
                        block_sums(b)

            for s in range(-1, NG + 2):
                if 0 <= s < NG:
                    hidden2(s, 0)
                pair_sums(s - 2, 1)
                for q in pairs(s - 1)[0:1]:
                    gate_pair(s - 1, q)
                    output_pair(s - 1, q)
                if s + 1 < NG:
                    transpose_chunk(s + 1, 0)
                    transpose_chunk(s + 1, 1)
                if 0 <= s < NG:
                    hidden2(s, 1)
                for q in pairs(s - 1)[1:2]:
                    gate_pair(s - 1, q)
                    output_pair(s - 1, q)
                pair_sums(s - 1, 0)
                if s + 1 < NG:
                    transpose_chunk(s + 1, 2)
                    transpose_chunk(s + 1, 3)
                if 0 <= s < NG:
                    hidden2(s, 2)

            pe.wait_ge(s_Yc, NB)
            pe.wait_ge(s_ldc, 16 * (2 + 2 * HEADS))
            for i in range(DK):
                for k in range(DK):
                    last = pe.matmul(bank[0][:, i * 8:i * 8 + 2 * HEADS], WcT[:, k, i * P:(i + 1) * P],
                                     ablk[:, k, :], start=k == 0, stop=k == DK - 1)
            last.then_inc(s_wa, 1)
            pe.wait_ge(s_low, 1)
            pe.matmul(bank[1][:, 0:NG], low_row[:, :], ident[0:NG, 0:NG], start=True, stop=True).then_inc(s_lowp, 1)
            pe.wait_ge(s_wac, 1)
            pe.wait_ge(s_lows, 1)

            def x1_transposes(t):
                n = rows_of_tile(t)
                pe.wait_ge(s_x1, t + 1)
                if t >= 4:
                    pe.wait_ge(s_x1c, t - 3)
                for k in range(DK):
                    last = pe.transpose(bank[4 + t % 4][:, k * P:k * P + n], xn[0:n, t, k * P:(k + 1) * P],
                                        ident[0:n, 0:n])
                last.then_inc(s_x1t, 1)

            def node_products(t):
                n = rows_of_tile(t)
                pe.wait_ge(s_x1c, t + 1)
                if t >= 4:
                    pe.wait_ge(s_hc, t - 3)
                for k in range(DK):
                    last = pe.matmul(bank[t % 4][0:n, 0:OUT + 2 * HEADS], x1T[:, t % XTR, k, 0:n], Wc[:, k, :],
                                     start=k == 0, stop=k == DK - 1)
                last.then_inc(s_H, 1)

            for t in range(NT + 2):
                if t < NT:
                    x1_transposes(t)
                if t >= 2:
                    node_products(t - 2)

            pe.wait_ge(s_hc, NT)
            pe.wait_ge(s_dc, DC["node"])
            for g in range(NG):
                pe.wait_ge(s_hot, 2 * g + 2)
                if g >= 4:
                    pe.wait_ge(s_pick, 2 * (g - 3))
                for j, b in enumerate(blocks_of_group(g)):
                    n = rows_of_block(b)
                    for side in range(2):
                        a = (j % 2 * 2 + side) * TQ
                        for part in range(3):
                            last = pe.matmul(bank[(2 * g + j // 2) % 8][0:n, a:a + TQ],
                                             hot[:, g % HOTR, side, j * P:j * P + n], node_p[:, part, side, :],
                                             start=part == 0, stop=part == 2)
                last.then_inc(s_O, 1)

            pe.wait_ge(s_pick, 2 * NG)
            for g in range(NG):
                pe.wait_ge(s_win, g + 1)
                pe.wait_ge(s_xb, g + 1)
                pe.wait_ge(s_xe, g + 1)
                if g >= 8:
                    pe.wait_ge(s_YBc, g - 7)
                for j, b in enumerate(blocks_of_group(g)):
                    n = rows_of_block(b)
                    last = pe.matmul(bank[g % 8][0:WB, 0:BW], in_window[0:n, g % XBR, j, :],
                                     xb[0:n, g % XBR, j, :], start=j == 0, stop=b == blocks_of_group(g)[-1])
                last.then_inc(s_YB, 1)
            with if_outside(pe):
                pe.wait_ge(s_YBc, NG)
                for b in range(NB):
                    n = rows_of_block(b)
                    pe.wait_ge(s_ueq, b + 1)
                    pe.wait_ge(s_ux, b + 1)
                    if b >= 1:
                        pe.wait_ge(s_uy, b)
                    pe.matmul(bank[0][0:n, 0:BW], in_window[0:n, 0, 0, 0:n], xb[0:n, 0, 0, :],
                              start=True, stop=True).then_inc(s_up, 1)

        def rows_copy(act, copy, t):
            n = rows_of_tile(t)
            act.wait_ge(s_H, t + 1)
            act.wait_ge(s_sl, t + 1)
            if t >= 4:
                act.wait_ge(s_ht[t % 4], 16 * (t // 4))
            copy(hst[0:n, t % 4, :], bank[t % 4][0:n, 0:OUT]).then_inc(s_hc, 1)

        @block.scalar
        def _(act):
            def copy(o, i):
                return act.activation(o, i, ACT.Copy)

            act.wait_ge(s_w0, 32)
            copy(W0h[:, :, :], W0f[:, :, :]).then_inc(s_wh, 1)
            for i in range(PARTS):
                act.wait_ge(s_ldx[i], 16)
                copy(xTh[:, :, part_cols(i)], xTf[:, :, part_cols(i)]).then_inc(s_xh, 1)
            act.wait_ge(s_ldw, 16 * (C1 + 2 * C2 + 2))
            copy(W1h[:, :, :], W1f[:, 0:F1, :])
            act.wait_ge(s_dc, DC["stack"])
            for r in S1[0:2]:
                last = copy(W1s[r:r + R1, :], W1f[0:R1, F1, :])
            last.then_inc(s_wh, 1)
            for m in range(C2):
                k = k2(m) + (m == C2 - 1)
                last = copy(W2h[0:k, m, :], W2f[0:k, m, :])
            last.then_inc(s_wh, 1)
            copy(Wgh[:, :], Wgf[:, :]).then_inc(s_wh, 1)
            for t in range(NT):
                n = rows_of_tile(t)
                act.wait_ge(s_n0, 2 * t + 2)
                if t >= N0R:
                    act.wait_ge(s_tb[t % N0R], 16 * (t // N0R))
                copy(stB[0:n, t % N0R, :], bank[(2 * t + 1) % 8][0:n, 0:H0]).then_inc(s_n0b, 1)

            def tanh1(g, c):
                u, n = C1 * g + c, edges_of_group(g)
                act.wait_ge(s_T, u + 1)
                if g >= 1:
                    act.wait_ge(s_h1l, u - C1 + 1)
                act.activation(h1f[0:k1(c), c, 0:n], PT[u % 2][0:k1(c), 0:n], ACT.Tanh).then_inc(s_tanh1, 1)

            def h1_hi(g, c):
                u, n = C1 * g + c, edges_of_group(g)
                act.wait_ge(s_tanh1, u + 1)
                if g >= 2:
                    act.wait_ge(s_L1, C2 * (g - 1))
                if c < F1:
                    last = copy(h1h[:, g % 2, c, 0:n], h1f[:, c, 0:n])
                else:
                    for r in (S1[0], S1[2]):
                        last = copy(h1s[r:r + R1, g % 2, 0:n], h1f[0:R1, c, 0:n])
                last.then_inc(s_h1h, 1)

            def h1_chunks(g, chunks):
                for c in chunks:
                    tanh1(g, c)
                for c in chunks:
                    h1_hi(g, c)

            def tanh2(g, m):
                u, n = C2 * g + m, edges_of_group(g)
                act.wait_ge(s_L1, u + 1)
                if g >= 1:
                    act.wait_ge(s_h2l, u - C2 + 1)
                act.activation(h2f[0:k2(m), m, 0:n], PL1[u % 2][0:k2(m), 0:n], ACT.Tanh,
                               bias=b1c[0:k2(m), m:m + 1]).then_inc(s_tanh2, 1)
                act.wait_ge(s_tanh2, u + 1)
                if g >= 2:
                    act.wait_ge(s_L2, 2 * (g - 1))
                copy(h2h[0:k2(m), g % 2, m, 0:n], h2f[0:k2(m), m, 0:n]).then_inc(s_h2h, 1)

            def edge_hi(g):
                n = edges_of_group(g)
                act.wait_ge(s_e[g % 2], 16 * (g // 2 + 1))
                if g >= 2:
                    act.wait_ge(s_G, 2 * (g - 1))
                copy(eh[:, g % 2, 0:n], ef[:, g % 2, 0:n]).then_inc(s_eh, 1)

            def gate_copy(q):
                act.wait_ge(s_G, q + 1)
                if q >= 2:
                    act.wait_ge(s_mul, q - 1)
                k, n = len(blocks_of_pair(q)), rows_of_block(2 * q)
                copy(gate[0:n, q % 2, 0:k, :].rearrange("p i d -> p (i d)"), PG[0:n, 0:k * OUT]).then_inc(s_gate, 1)

            def gated_hi(q):
                act.wait_ge(s_mul, q + 1)
                if q >= 2:
                    act.wait_ge(s_Y, 2 * (q - 1))
                k, n = len(blocks_of_pair(q)), rows_of_block(2 * q)
                copy(mh[0:n, q % 2, 0:k, 0:OUT], mf[0:n, q % 2, 0:k, :]).then_inc(s_mh, 1)

            def sums_copy(b, banks, width, done, landed, tables, copied):
                n = rows_of_block(b)
                act.wait_ge(done, b + 1)
                if b >= Y_RING:
                    act.wait_ge(landed[b % tables], 16 * ((b - Y_RING) // tables + 1))
                copy(ystage[0:n, b % Y_RING, 0:width], banks[b % len(banks)][0:n, 0:width]).then_inc(copied, 1)

            wait_stage_n0(act)
            act.wait_ge(s_dc, DC["ones"])
            def pair_copies(g, i):
                for q in pairs(g)[i:i + 1]:
                    for b in blocks_of_pair(q):
                        sums_copy(b, PY, AW, s_Y, s_scA, TABLES, s_Yc)

            for s in range(-1, NG + 2):
                if 0 <= s - 1 < NG:
                    tanh2(s - 1, 2)
                if 0 <= s < NG:
                    tanh2(s, 0)
                    edge_hi(s)
                pair_copies(s - 2, 1)
                for q in pairs(s - 1)[0:1]:
                    gate_copy(q)
                    gated_hi(q)
                if s + 1 < NG:
                    h1_chunks(s + 1, (0, 1))
                if 0 <= s < NG:
                    tanh2(s, 1)
                for q in pairs(s - 1)[1:2]:
                    gate_copy(q)
                    gated_hi(q)
                pair_copies(s - 1, 0)
                if s + 1 < NG:
                    h1_chunks(s + 1, (2, 3))

            wait_stage_a(act)
            act.wait_ge(s_wa, 1)
            copy(Wc[:, :, OUT:OUT + 2 * HEADS],
                 bank[0][:, 0:DK * 8].rearrange("p (i c) -> p i c", c=8)).then_inc(s_wac, 1)
            act.wait_ge(s_mv, NT)
            act.wait_ge(s_dc, DC["eps"])
            act.activation(std[:, :], mv[:, :, 1], ACT.Sqrt, bias=eps[:, :]).then_inc(s_std, 1)
            for t in range(NT):
                n = rows_of_tile(t)
                act.wait_ge(s_x1t, t + 1)
                if t >= XTR:
                    act.wait_ge(s_H, t - XTR + 1)
                copy(x1T[:, t % XTR, :, 0:n],
                     bank[4 + t % 4][:, 0:DK * P].rearrange("p (k r) -> p k r", r=P)[:, :, 0:n]).then_inc(s_x1c, 1)
                if t >= 2:
                    rows_copy(act, copy, t - 2)
            rows_copy(act, copy, NT - 2)
            rows_copy(act, copy, NT - 1)

            act.wait_ge(s_b2, B2["neg"])
            act.activation(score2[:, :, :], score[:, :, :], ACT.Exp, bias=neg_top[:, :]).then_inc(s_ex, 1)
            act.wait_ge(s_ex, 1)
            for g in range(NG + 2):
                if g < NG:
                    if g >= XBR:
                        act.wait_ge(s_YB, g - XBR + 1)
                    for run in same_rows(blocks_of_group(g)):
                        n, j, k = rows_of_block(run[0]), run[0] - g * BLOCKS_PER_GROUP, len(run)
                        last = copy(xb[0:n, g % XBR, j:j + k, OUT:BW], score2[0:n, run[0]:run[0] + k, :])
                    last.then_inc(s_xe, 1)
                if g >= 2:
                    w = g - 2
                    act.wait_ge(s_YB, w + 1)
                    if w == 0:
                        for k in range(TABLES):
                            act.wait_ge(s_scA[k], ring_total(TABLES, k, NB))
                    if w >= Y_RING:
                        act.wait_ge(s_scB, 16 * (w - Y_RING + 1))
                    copy(ystage[:, w % Y_RING, :], bank[w % 8][:, 0:BW]).then_inc(s_YBc, 1)
            with if_outside(act):
                act.wait_ge(s_scB, 16 * NG)
                for b in range(NB):
                    n = rows_of_block(b)
                    act.wait_ge(s_up, b + 1)
                    if b >= 1:
                        act.wait_ge(s_us, 16 * b)
                    copy(ystage[0:n, 0, :], bank[0][0:n, 0:BW]).then_inc(s_uy, 1)
            act.wait_ge(s_mv, 2 * NT)
            act.activation(std[:, :], mv[:, :, 1], ACT.Sqrt, bias=eps[:, :]).then_inc(s_std, 1)


_INS = ["xT", "x", "src_cols", "dst_cols", "src_row", "dst_row", "eT", "w_cols", "W0", "b0", "W1", "b1",
        "W2", "b2", "Wg", "Wcat", "WcatT", "a_src", "a_dst"]


def kernel(x, src, dst, edge_attr_128, edge_weight, L0_gnn_W0, L0_gnn_b0, L0_gnn_W1, L0_gnn_b1, L0_gnn_W2,
           L0_gnn_b2, L0_gnn_Wg, L1_gnn_W, L1_gnn_a_src, L1_gnn_a_dst):
    import concourse.bacc as bacc
    from concourse.bass_utils import run_bass_kernel_spmd

    def columns(v):
        v = np.asarray(v)
        full = np.zeros(-(-v.shape[0] // P) * P, v.dtype)
        full[:v.shape[0]] = v
        return full.reshape(-1, P).T

    W = np.asarray(L1_gnn_W)
    Wcat = W.transpose(1, 0, 2).reshape(W.shape[1], -1)
    laid = dict(
        xT=np.asarray(x).T, x=x, src_cols=columns(src), dst_cols=columns(dst), src_row=src, dst_row=dst,
        eT=np.asarray(edge_attr_128).T, w_cols=columns(edge_weight), W0=L0_gnn_W0, b0=L0_gnn_b0,
        W1=L0_gnn_W1, b1=L0_gnn_b1, W2=L0_gnn_W2, b2=L0_gnn_b2, Wg=L0_gnn_Wg, Wcat=Wcat, WcatT=Wcat.T,
        a_src=L1_gnn_a_src, a_dst=L1_gnn_a_dst)
    nc = bacc.Bacc("TRN2", target_bir_lowering=False, num_devices=1)
    arrays, args = {}, []
    for name in _INS:
        a = np.ascontiguousarray(laid[name])
        arrays[f"in_{name}"] = a
        args.append(nc.dram_tensor(f"in_{name}", a.shape, mybir.dt.from_np(a.dtype), kind="ExternalInput").ap())
    args.append(nc.dram_tensor("out_0", np.asarray(x).shape, mybir.dt.float32, kind="ExternalOutput").ap())
    build_program(nc, *args)
    r = run_bass_kernel_spmd(nc, [arrays], core_ids=[0])
    return r.results[0]["out_0"]
```

```python
import numpy as np
import concourse.bass as bass
from concourse import mybir
from concourse.alu_op_type import AluOpType as ALU
from contextlib import ExitStack


P = 128
BLOCKS_PER_GROUP = 4
TABLES = 2
Y_RING = 8
SUM_LAG = 3
NEG_SLOPE = 0.2
LN_EPS = 1e-5
DENOM_EPS = 1e-10
LOWEST = -3.0e38


def build_program(nc, xT, x, src_cols, dst_cols, src_row, dst_row, eT, w_cols,
                  W0, b0, W1, b1, W2, b2, Wg, Wcat, WcatT, a_src, a_dst, out):
    f32, f32r, bf16, i32 = mybir.dt.float32, mybir.dt.float32r, mybir.dt.bfloat16, mybir.dt.int32
    ACT, AX = mybir.ActivationFunctionType, mybir.AxisListType

    D, N = xT.shape
    E = src_row.shape[0]
    H0, H1, OUT = W0.shape[1], W1.shape[1], W2.shape[1]
    HEADS, HD = a_src.shape[0], a_src.shape[1]
    DK = D // P
    NT = -(-N // P)
    NB = -(-E // P)
    NG = -(-NB // BLOCKS_PER_GROUP)
    GE = BLOCKS_PER_GROUP * P
    NPAIR = -(-NB // 2)
    F1 = H0 // P
    R1 = H0 - F1 * P
    S1 = (0, 32, 64)
    KS = S1[2] + R1
    C1 = F1 + 1
    C2 = -(-H1 // P)
    K2 = -(-H1 // C2)
    AW = OUT + 2
    BW = OUT + HEADS
    TR = (NT + 1) * P
    TC = 5
    NC = -(-NT // TC)
    TQ = NT * HEADS
    RQ = 125
    QC = E // RQ
    WB = P
    assert D % P == 0 and N + P <= TR and E % RQ == 0 and TQ <= P and HEADS == 4
    assert 0 < R1 <= 32 and NG <= P and Y_RING % TABLES == 0

    def rows_of_tile(t):
        return min(P, N - t * P)

    def rows_of_block(b):
        return min(P, E - b * P)

    def blocks_of_group(g):
        return range(g * BLOCKS_PER_GROUP, min((g + 1) * BLOCKS_PER_GROUP, NB))

    def blocks_of_pair(q):
        return range(2 * q, min(2 * q + 2, NB))

    def pairs_of_group(g):
        return range(2 * g, min(2 * g + 2, NPAIR))

    def pairs(g):
        return list(pairs_of_group(g)) if 0 <= g < NG else []

    def edges_of_group(g):
        return min(GE, E - g * GE)

    def k1(c):
        return P if c < F1 else R1

    def k2(m):
        return min(K2, H1 - m * K2)

    def same_rows(blocks):
        full = [b for b in blocks if rows_of_block(b) == P]
        return [r for r in (full, [b for b in blocks if rows_of_block(b) < P]) if r]

    ctx = ExitStack()
    with ctx:
        def sb(name, shape, dt=f32, scope=ctx):
            return scope.enter_context(nc.sbuf_tensor(name, shape, dt))

        def sem(name):
            return ctx.enter_context(nc.semaphore(name))

        TA = nc.dram_tensor("TA", [N, H0], f32).ap()
        TB = nc.dram_tensor("TB", [N, H0], f32).ap()
        HT = nc.dram_tensor("HT", [N, BW], f32).ap()
        ST = nc.dram_tensor("ST", [N, HEADS], f32).ap()
        RD = nc.dram_tensor("RD", [2, E], bf16).ap()
        accA = [nc.dram_tensor(f"accA{k}", [TR, AW], f32).ap() for k in range(TABLES)]
        accB = nc.dram_tensor("accB", [TR, BW], f32).ap()

        ident = sb("ident", [P, P])
        lower = sb("lower", [P, P])
        iota_row = sb("iota_row", [P, P])
        p_i = sb("p_i", [P, 1], i32)
        p_f = sb("p_f", [P, 1])
        trash = sb("trash", [P, 1])
        src_c = sb("src_c", [P, NB], i32)
        dst_c = sb("dst_c", [P, NB], i32)
        dst_f = sb("dst_f", [P, NB])
        tile_c = sb("tile_c", [P, NB, 2], bf16)
        tile_row = sb("tile_row", [P, NT], bf16)
        dst_rel = sb("dst_rel", [P, NB])
        dst_g = sb("dst_g", [NG, GE], i32)
        low_g = sb("low_g", [NG, 2])
        low_all = sb("low_all", [P, NG])
        to_b = sb("to_b", [P, NG], i32)
        to_f = sb("to_f", [P, BLOCKS_PER_GROUP])
        w_c = sb("w_c", [P, NB])
        xn = sb("xn", [P, NT, D])
        mv = sb("mv", [P, NT, 2])
        std = sb("std", [P, NT])
        rstd = sb("rstd", [P, NT])
        shift = sb("shift", [P, NT])
        eps = sb("eps", [P, 1])
        zeros = sb("zeros", [P, BW])
        ystage = sb("ystage", [P, Y_RING, BW])

        sa = ExitStack()
        src_f = sb("src_f", [P, NB], f32, sa)
        src_t = sb("src_t", [P, NB], f32, sa)
        dup = sb("dup", [P, NB], f32, sa)
        to_a = sb("to_a", [P, NB], i32, sa)
        bcast_i = sb("bcast_i", [P, 2, GE], i32, sa)
        W1h = sb("W1h", [P, F1, H1], f32r, sa)
        W1l = sb("W1l", [P, F1, H1], f32r, sa)
        W1s = sb("W1s", [KS, H1], f32r, sa)
        W2h = sb("W2h", [K2, C2, OUT], f32r, sa)
        W2l = sb("W2l", [K2, C2, OUT], f32r, sa)
        Wgh = sb("Wgh", [P, OUT], f32r, sa)
        Wgl = sb("Wgl", [P, OUT], f32r, sa)
        b1c = sb("b1c", [K2, C2], f32, sa)
        GAR, GBR = 3, 2
        sn = ExitStack()
        xTf = sb("xTf", [P, DK, N], f32, sn)
        xTh = sb("xTh", [P, DK, N], f32r, sn)
        xTl = sb("xTl", [P, DK, N], f32r, sn)
        W0f = sb("W0f", [P, 2 * DK, H0], f32, sn)
        W0h = sb("W0h", [P, 2 * DK, H0], f32r, sn)
        W0l = sb("W0l", [P, 2 * DK, H0], f32r, sn)
        b0b = sb("b0b", [P, H0], f32, sn)
        N0R = 4
        stA = sb("stA", [P, N0R, H0], f32, sn)
        stB = sb("stB", [P, N0R, H0], f32, sn)
        idx_rows = sb("idx_rows", [RQ, 2, QC], i32, sn)
        rem_i = sb("rem_i", [RQ, 2, QC], i32, sn)
        tile_i = sb("tile_i", [P, NB, 2], i32, sn)
        iota_i = sb("iota_i", [P, P], i32, sn)
        rem_b = sb("rem_b", [RQ, 2, QC], bf16, sn)
        W1f = sb("W1f", [P, C1, H1], f32, sn)
        W2f = sb("W2f", [K2, C2, OUT], f32, sn)
        Wgf = sb("Wgf", [P, OUT], f32, sn)
        sn.close()
        GA = sb("GA", [P, GAR * BLOCKS_PER_GROUP, H0], f32, sa)
        GB = sb("GB", [P, GBR * BLOCKS_PER_GROUP, H0], f32, sa)
        h1f = sb("h1f", [P, C1, GE], f32, sa)
        h1h = sb("h1h", [P, 2, F1, GE], f32r, sa)
        h1l = sb("h1l", [P, 2, F1, GE], f32r, sa)
        h1s = sb("h1s", [KS, 2, GE], f32r, sa)
        h2f = sb("h2f", [K2, C2, GE], f32, sa)
        h2h = sb("h2h", [K2, 2, C2, GE], f32r, sa)
        h2l = sb("h2l", [K2, 2, C2, GE], f32r, sa)
        ef = sb("ef", [P, 2, GE], f32, sa)
        eh = sb("eh", [P, 2, GE], f32r, sa)
        el = sb("el", [P, 2, GE], f32r, sa)
        gate = sb("gate", [P, 2, 2, OUT], f32, sa)
        mf = sb("mf", [P, 2, 2, OUT], f32, sa)
        mh = sb("mh", [P, 2, 2, AW], f32r, sa)
        ml = sb("ml", [P, 2, 2, AW], f32r, sa)
        EQR = 3 * BLOCKS_PER_GROUP
        eqA = sb("eqA", [P, EQR, P], f32r, sa)
        eq_low = sb("eq_low", [P, 2, P], bf16, sa)
        sa.close()

        sc, s1, s2, s3 = ExitStack(), ExitStack(), ExitStack(), ExitStack()
        cinv = sb("cinv", [P, NT, HEADS], f32, sc)
        cden = sb("cden", [P, NT, HEADS], f32, sc)
        stats = sb("stats", [P, NT, 6], f32, sc)
        node = sb("node", [P, 2, TQ], f32, sc)
        node_rest = sb("node_rest", [P, 2, TQ], f32, sc)
        node_p = sb("node_p", [P, 3, 2, TQ], bf16, sc)
        score = sb("score", [P, NB, HEADS], f32, sc)
        top = sb("top", [P, 2], f32, sc)
        top_all = sb("top_all", [P, 2], f32, sc)
        neg_top = sb("neg_top", [P, 1], f32, sc)
        low_row = sb("low_row", [NG, P], f32, sc)
        outside = sb("outside", [1, 1], i32, sc)
        TSR = 2
        tab = sb("tab", [P, TSR, TABLES, TC, BW], f32, s1)
        XTR = 4
        x1T = sb("x1T", [P, XTR, DK, P], f32, s1)
        Wc = sb("Wc", [P, DK, OUT + 2 * HEADS], f32, s1)
        WcT = sb("WcT", [P, DK, OUT], f32, s1)
        ablk = sb("ablk", [P, DK, 2 * HEADS], f32, s1)
        hst = sb("hst", [P, 4, BW], f32, s1)
        s1.close()
        HGR = 30
        Hg = sb("Hg", [P, HGR * BLOCKS_PER_GROUP, BW], f32, sc)
        SCORED = 18
        scored = sb("scored", [P, SCORED * BLOCKS_PER_GROUP, HEADS], f32, sc)
        LEAD = 2
        REMG = 2
        rem = sb("rem", [P, 2, 2, REMG * GE], bf16, s2)
        HOTR = 4
        hot = sb("hot", [P, HOTR, 2, GE], bf16, s2)
        own = sb("own", [P, 2, BLOCKS_PER_GROUP * 2 * NT], bf16, s2)
        picked = sb("picked", [P, 2, BLOCKS_PER_GROUP * 2 * TQ], f32, s2)
        s2.close()
        XBR = 3
        xb = sb("xb", [P, XBR, BLOCKS_PER_GROUP, BW], f32, s3)
        in_window = sb("in_window", [P, XBR, BLOCKS_PER_GROUP, P], f32, s3)
        eq_lowb = sb("eq_lowb", [P, P], f32, s3)
        dup_u = sb("dup_u", [P, 1], f32, s3)
        dst_u = sb("dst_u", [P, P], i32, s3)
        to_u = sb("to_u", [P, 1], i32, s3)
        s3.close()
        sc.close()

        bank = [ctx.enter_context(nc.psum_tensor(f"bank{i}", [P, 512], f32)) for i in range(8)]
        PT, PL1, PG, P2, PY = bank[0:2], bank[2:4], bank[4], bank[5], bank[6:8]

        s_const = sem("s_const")
        s_dc = sem("s_dc")
        s_ldw = sem("s_ldw")
        s_ldx = [sem(f"s_ldx{i}") for i in range(4)]
        s_ldi = sem("s_ldi")
        s_rd = sem("s_rd")
        s_zero = sem("s_zero")
        s_w0 = sem("s_w0")
        s_b0 = sem("s_b0")
        s_xh = sem("s_xh")
        s_xl = sem("s_xl")
        s_wh = sem("s_wh")
        s_wl = sem("s_wl")
        s_n0 = sem("s_n0")
        s_n0a = sem("s_n0a")
        s_n0b = sem("s_n0b")
        s_ta = [sem(f"s_ta{i}") for i in range(N0R)]
        s_tb = [sem(f"s_tb{i}") for i in range(N0R)]
        s_ga = [sem(f"s_ga{i}") for i in range(GAR)]
        s_gb = [sem(f"s_gb{i}") for i in range(GBR)]
        s_e = [sem(f"s_e{i}") for i in range(2)]
        s_bc = [sem(f"s_bc{i}") for i in range(2)]
        s_add = sem("s_add")
        s_T = sem("s_T")
        s_tanh1 = sem("s_tanh1")
        s_h1h = sem("s_h1h")
        s_h1l = sem("s_h1l")
        s_L1 = sem("s_L1")
        s_tanh2 = sem("s_tanh2")
        s_h2h = sem("s_h2h")
        s_h2l = sem("s_h2l")
        s_eh = sem("s_eh")
        s_el = sem("s_el")
        s_G = sem("s_G")
        s_gate = sem("s_gate")
        s_L2 = sem("s_L2")
        s_mul = sem("s_mul")
        s_mh = sem("s_mh")
        s_ml = sem("s_ml")
        s_eq = sem("s_eq")
        s_dup = sem("s_dup")
        s_tof = sem("s_tof")
        s_to = sem("s_to")
        s_Y = sem("s_Y")
        s_Yc = sem("s_Yc")
        s_scA = [sem(f"s_scA{i}") for i in range(TABLES)]
        s_scB = sem("s_scB")
        s_xn = sem("s_xn")
        s_ldc = sem("s_ldc")
        s_tab = [sem(f"s_tab{i}") for i in range(TSR)]
        s_sum = sem("s_sum")
        s_low = sem("s_low")
        s_lowp = sem("s_lowp")
        s_lows = sem("s_lows")
        s_cden = sem("s_cden")
        s_cinv = sem("s_cinv")
        s_att = sem("s_att")
        s_res = sem("s_res")
        s_stat = sem("s_stat")
        s_mv = sem("s_mv")
        s_std = sem("s_std")
        s_rstd = sem("s_rstd")
        s_shift = sem("s_shift")
        s_x1 = sem("s_x1")
        s_wa = sem("s_wa")
        s_wac = sem("s_wac")
        s_x1t = sem("s_x1t")
        s_x1c = sem("s_x1c")
        s_H = sem("s_H")
        s_hc = sem("s_hc")
        s_ht = [sem(f"s_ht{i}") for i in range(4)]
        s_rem = [sem(f"s_rem{i}") for i in range(2)]
        s_hot = sem("s_hot")
        s_O = sem("s_O")
        s_pick = sem("s_pick")
        s_own = sem("s_own")
        s_st = sem("s_st")
        s_sg = sem("s_sg")
        s_sc = sem("s_sc")
        s_b2 = sem("s_b2")
        s_top = sem("s_top")
        s_ex = sem("s_ex")
        s_hg = [sem(f"s_hg{i}") for i in range(HGR)]
        s_xb = sem("s_xb")
        s_xe = sem("s_xe")
        s_win = sem("s_win")
        s_YB = sem("s_YB")
        s_YBc = sem("s_YBc")
        s_ukeep = sem("s_ukeep")
        s_ubc = sem("s_ubc")
        s_ug = sem("s_ug")
        s_ueq = sem("s_ueq")
        s_udup = sem("s_udup")
        s_utof = sem("s_utof")
        s_uto = sem("s_uto")
        s_ux = sem("s_ux")
        s_up = sem("s_up")
        s_uy = sem("s_uy")
        s_us = sem("s_us")
        s_out = sem("s_out")

        PARTS = 4
        tiles_per_part = -(-NT // PARTS)
        part_of_tile = [t // tiles_per_part for t in range(NT)]

        def part_cols(i):
            return slice(i * tiles_per_part * P, min((i + 1) * tiles_per_part * P, N))

        assert HGR % REMG == 0 and SCORED % REMG == 0 and NG % REMG == 0 and HGR + SCORED < NG

        def b1_group(i):
            return (i + HGR + SCORED) % NG

        def b1_sides(i):
            return (1,) if b1_group(i) < HGR + SCORED else (0, 1)

        def b1_banks(i):
            blocks = blocks_of_group(b1_group(i))
            k = BLOCKS_PER_GROUP // len(b1_sides(i))
            return [((2 * i + a // k) % 8, blocks[a:a + k]) for a in range(0, len(blocks), k)]

        def ring_total(ring, slot, n):
            return 16 * len([i for i in range(n) if i % ring == slot])

        def group_arrivals(ring, g):
            return 16 * sum(len(blocks_of_group(i)) for i in range(g % ring, g + 1, ring))

        def wait_stage_n0(eng):
            for k in range(N0R):
                eng.wait_ge(s_ta[k], ring_total(N0R, k, NT))
                eng.wait_ge(s_tb[k], ring_total(N0R, k, NT))
            eng.wait_ge(s_rd, 16)
            eng.wait_ge(s_wl, 4)

        def wait_stage_a(eng):
            for k in range(TABLES):
                eng.wait_ge(s_scA[k], ring_total(TABLES, k, NB))

        def tiles_of_chunk(c):
            return range(c * TC, min((c + 1) * TC, NT))

        def load_tables(eng, tables, width, base, chunks):
            for c in chunks:
                u, tiles = base + c, tiles_of_chunk(c)
                if u >= TSR:
                    eng.wait_ge(s_res, NT * ((u - TSR) // NC) + tiles_of_chunk((u - TSR) % NC)[-1] + 1)
                for k, table in enumerate(tables):
                    eng.dma_start(tab[:, u % TSR, k, 0:len(tiles), 0:width],
                                  table[tiles[0] * P:(tiles[-1] + 1) * P, :].rearrange("(t p) d -> p t d", p=P))\
                       .then_inc(s_tab[u % TSR], 16)

        def chunk_arrivals(u):
            return 16 * sum(TABLES if v < NC else 1 for v in range(u % TSR, u + 1, TSR))

        def if_outside(eng):
            eng.wait_ge(s_b2, B2["outside"])
            return eng.If(eng.value_load(outside[0:1, 0:1], min_val=0, max_val=1))

        block = ctx.enter_context(nc.Block())

        DC, B2 = {}, {}

        @block.vector
        def _(dve):
            dc = [0]

            def const(ins, name=None):
                dc[0] += 1
                ins.then_inc(s_dc, 1)
                dve.wait_ge(s_dc, dc[0])
                DC[name] = dc[0]

            def lo(o, full, hi):
                return dve.tensor_tensor(o, full, hi.bitcast(f32), ALU.subtract)

            const(dve.memset(zeros[:, :], 0.0), "zeros")
            const(dve.memset(eps[:, :], LN_EPS), "eps")
            const(dve.memset(mv[:, :, :], 0.0))
            dve.wait_ge(s_const, 2)
            const(dve.tensor_copy(iota_row[:, :], iota_i[:, :]))
            const(dve.tensor_copy(p_f[:, :], p_i[:, :]))
            const(dve.tensor_scalar(ident[:, :], iota_row[:, :], p_f[:, :], None, ALU.is_equal))
            const(dve.tensor_scalar(lower[:, :], iota_row[:, :], p_f[:, :], None, ALU.is_lt))
            const(dve.tensor_scalar(trash[:, :], p_f[:, :], float(N), None, ALU.add))
            const(dve.tensor_copy(tile_row[:, :], iota_row[:, 0:NT]))
            const(dve.memset(W1s[:, :].bitcast(f32), 0.0), "stack")
            dve.wait_ge(s_wh, 1)
            lo(W0l[:, :, :], W0f[:, :, :], W0h[:, :, :]).then_inc(s_wl, 1)
            for i in range(PARTS):
                dve.wait_ge(s_xh, i + 1)
                lo(xTl[:, :, part_cols(i)], xTf[:, :, part_cols(i)], xTh[:, :, part_cols(i)]).then_inc(s_xl, 1)
            dve.wait_ge(s_ldi, 16 * (5 + (E % GE > 0)))
            const(dve.tensor_copy(src_f[:, :], src_c[:, :]))
            const(dve.tensor_copy(dst_f[:, :], dst_c[:, :]))
            const(dve.tensor_scalar(src_t[:, :], src_f[:, :], trash[:, :], None, ALU.subtract))
            for side, ends in enumerate((src_c, dst_c)):
                const(dve.tensor_single_scalar(tile_i[:, :, side], ends[:, :], P.bit_length() - 1,
                                               ALU.logical_shift_right))
            const(dve.tensor_copy(tile_c[:, :, :], tile_i[:, :, :]))
            const(dve.tensor_single_scalar(rem_i[:, :, :], idx_rows[:, :, :], P - 1, ALU.bitwise_and))
            const(dve.tensor_copy(rem_b[:, :, :], rem_i[:, :, :]), "rem")
            dve.wait_ge(s_b0, 16)
            for t in range(NT):
                n = rows_of_tile(t)
                dve.wait_ge(s_n0, 2 * t + 1)
                if t >= N0R:
                    dve.wait_ge(s_ta[t % N0R], 16 * (t // N0R))
                dve.tensor_tensor(stA[0:n, t % N0R, :], bank[(2 * t) % 8][0:n, 0:H0], b0b[0:n, :], ALU.add)\
                    .then_inc(s_n0a, 1)
            dve.wait_ge(s_wh, 4)
            lo(W1l[:, :, :], W1f[:, 0:F1, :], W1h[:, :, :])
            lo(W1s[S1[2]:KS, :], W1f[0:R1, F1, :], W1s[0:R1, :]).then_inc(s_wl, 1)
            for m in range(C2):
                k = k2(m) + (m == C2 - 1)
                last = lo(W2l[0:k, m, :], W2f[0:k, m, :], W2h[0:k, m, :])
            last.then_inc(s_wl, 1)
            lo(Wgl[:, :], Wgf[:, :], Wgh[:, :]).then_inc(s_wl, 1)
            wait_stage_n0(dve)
            r = k2(C2 - 1) // 32 * 32
            const(dve.memset(h2h[r:K2, :, C2 - 1, :].bitcast(f32), 1.0))
            const(dve.memset(h2l[r:K2, :, C2 - 1, :].bitcast(f32), 0.0))
            const(dve.memset(mh[:, :, :, OUT:OUT + 1].bitcast(f32), 1.0))
            const(dve.memset(mh[:, :, :, OUT + 1:AW].bitcast(f32), 0.0))
            const(dve.memset(h1s[:, :, :].bitcast(f32), 0.0))
            const(dve.memset(ml[:, :, :, OUT:AW].bitcast(f32), 0.0), "ones")

            def add_rows(g):
                dve.wait_ge(s_ga[g % GAR], group_arrivals(GAR, g))
                dve.wait_ge(s_gb[g % GBR], group_arrivals(GBR, g))
                for run in same_rows(blocks_of_group(g)):
                    n, k = rows_of_block(run[0]), len(run)
                    a, b = run[0] % (GAR * BLOCKS_PER_GROUP), run[0] % (GBR * BLOCKS_PER_GROUP)
                    last = dve.tensor_tensor(GA[0:n, a:a + k, :], GA[0:n, a:a + k, :], GB[0:n, b:b + k, :], ALU.add)
                last.then_inc(s_add, 1)

            def h1_lo(g, c):
                u, n = C1 * g + c, edges_of_group(g)
                dve.wait_ge(s_h1h, u + 1)
                if c < F1:
                    last = lo(h1l[:, g % 2, c, 0:n], h1f[:, c, 0:n], h1h[:, g % 2, c, 0:n])
                else:
                    last = lo(h1s[S1[1]:S1[1] + R1, g % 2, 0:n], h1f[0:R1, c, 0:n], h1s[0:R1, g % 2, 0:n])
                last.then_inc(s_h1l, 1)

            def h2_lo(g, m):
                u, n = C2 * g + m, edges_of_group(g)
                dve.wait_ge(s_h2h, u + 1)
                lo(h2l[0:k2(m), g % 2, m, 0:n], h2f[0:k2(m), m, 0:n], h2h[0:k2(m), g % 2, m, 0:n]).then_inc(s_h2l, 1)

            def edge_lo(g):
                n = edges_of_group(g)
                dve.wait_ge(s_eh, g + 1)
                lo(el[:, g % 2, 0:n], ef[:, g % 2, 0:n], eh[:, g % 2, 0:n]).then_inc(s_el, 1)

            def multiply(q):
                k, n = len(blocks_of_pair(q)), rows_of_block(2 * q)
                dve.wait_ge(s_L2, q + 1)
                dve.wait_ge(s_gate, q + 1)
                if q >= 2:
                    dve.wait_ge(s_ml, q - 1)
                dve.tensor_tensor(mf[0:n, q % 2, 0:k, :].rearrange("p i d -> p (i d)"), P2[0:n, 0:k * OUT],
                                  gate[0:n, q % 2, 0:k, :].rearrange("p i d -> p (i d)"), ALU.mult).then_inc(s_mul, 1)

            def gated_lo(q):
                k, n = len(blocks_of_pair(q)), rows_of_block(2 * q)
                dve.wait_ge(s_mh, q + 1)
                lo(ml[0:n, q % 2, 0:k, 0:OUT], mf[0:n, q % 2, 0:k, :], mh[0:n, q % 2, 0:k, 0:OUT]).then_inc(s_ml, 1)

            def equality(g, i):
                dve.wait_ge(s_bc[g % 2], 16 * (g // 2 + 1))
                for b in blocks_of_group(g)[2 * i:2 * i + 2]:
                    n, j = rows_of_block(b), b % BLOCKS_PER_GROUP
                    same = bcast_i[0:n, g % 2, j * P:j * P + n]
                    if b >= EQR:
                        dve.wait_ge(s_Y, b - EQR + 1)
                    dve.tensor_scalar(eqA[0:n, b % EQR, 0:n], same, src_f[0:n, b:b + 1], None, ALU.is_equal)\
                        .then_inc(s_eq, 1)
                    if b >= 2:
                        dve.wait_ge(s_dup, b - 1)
                    dve.scalar_tensor_tensor(eq_low[0:n, b % 2, 0:n], same, src_f[0:n, b:b + 1], lower[0:n, 0:n],
                                             ALU.is_equal, ALU.mult, accum_out=dup[0:n, b:b + 1]).then_inc(s_dup, 1)

            def table_rows(g):
                dve.wait_ge(s_dup, blocks_of_group(g)[-1] + 1)
                runs = same_rows(blocks_of_group(g))
                if g >= 1:
                    dve.wait_ge(s_to, g)
                for run in runs:
                    n, b, k = rows_of_block(run[0]), run[0], len(run)
                    j = b % BLOCKS_PER_GROUP
                    last = dve.scalar_tensor_tensor(to_f[0:n, j:j + k], dup[0:n, b:b + k], 0.0,
                                                    src_t[0:n, b:b + k], ALU.is_equal, ALU.mult)
                last.then_inc(s_tof, 1)
                dve.wait_ge(s_tof, g + 1)
                for run in runs:
                    n, b, k = rows_of_block(run[0]), run[0], len(run)
                    j = b % BLOCKS_PER_GROUP
                    last = dve.tensor_scalar(to_a[0:n, b:b + k], to_f[0:n, j:j + k], trash[0:n, :], None, ALU.add)
                last.then_inc(s_to, 1)

            for s in range(-2, NG + 1):
                if 0 <= s - 1 < NG:
                    h2_lo(s - 1, 2)
                if s + 2 < NG and s != -1:
                    add_rows(s + 2)
                if 0 <= s < NG:
                    h2_lo(s, 0)
                    edge_lo(s)
                for q in pairs(s - 1)[0:1]:
                    multiply(q)
                if 0 <= s < NG:
                    equality(s, 0)
                for q in pairs(s - 1)[0:1]:
                    gated_lo(q)
                if 0 <= s + 1 < NG:
                    h1_lo(s + 1, 0)
                    h1_lo(s + 1, 1)
                if 0 <= s < NG:
                    h2_lo(s, 1)
                for q in pairs(s - 1)[1:2]:
                    multiply(q)
                if 0 <= s < NG:
                    equality(s, 1)
                    table_rows(s)
                for q in pairs(s - 1)[1:2]:
                    gated_lo(q)
                if 0 <= s + 1 < NG:
                    h1_lo(s + 1, 2)
                    h1_lo(s + 1, 3)
                if s == -1:
                    add_rows(1)

            def residual(c, u, width, divide):
                tiles = tiles_of_chunk(c)
                k = len(tiles)
                dve.wait_ge(s_tab[u % TSR], chunk_arrivals(u))
                divide(tab[:, u % TSR, :, 0:k, 0:width], tiles, k, u)
                for t in tiles:
                    n = rows_of_tile(t)
                    dve.wait_ge(s_res, NT * (u // NC) + t + 1)
                    dve.bn_stats(stats[0:n, t, :], xn[0:n, t, :]).then_inc(s_stat, 1)
                for t in tiles:
                    n = rows_of_tile(t)
                    dve.wait_ge(s_stat, NT * (u // NC) + t + 1)
                    dve.bn_aggr(mv[0:n, t, :], stats[0:n, t, :]).then_inc(s_mv, 1)

            def mean(rows, tiles, k, u):
                t0 = tiles[0]
                dve.tensor_tensor(rows[:, 0], rows[:, 0], rows[:, 1], ALU.add).then_inc(s_sum, 1)
                dve.wait_ge(s_sum, u + 1)
                dve.tensor_scalar(cden[:, t0:t0 + k, 0:1], rows[:, 0, :, OUT:OUT + 1], 1.0, None, ALU.max)\
                    .then_inc(s_cden, 1)
                dve.wait_ge(s_cden, u + 1)
                dve.reciprocal(cinv[:, t0:t0 + k, 0:1], cden[:, t0:t0 + k, 0:1]).then_inc(s_cinv, 1)
                dve.wait_ge(s_cinv, u + 1)
                for j, t in enumerate(tiles):
                    n = rows_of_tile(t)
                    dve.scalar_tensor_tensor(xn[0:n, t, :], rows[0:n, 0, j, 0:OUT], cinv[0:n, t, 0:1],
                                             xn[0:n, t, :], ALU.mult, ALU.add).then_inc(s_res, 1)

            def attention(rows, tiles, k, u):
                t0 = tiles[0]
                dve.tensor_scalar(cden[:, t0:t0 + k, :], rows[:, 0, :, OUT:BW], DENOM_EPS, None, ALU.add)\
                    .then_inc(s_cden, 1)
                dve.wait_ge(s_cden, u + 1)
                dve.reciprocal(cinv[:, t0:t0 + k, :], cden[:, t0:t0 + k, :]).then_inc(s_cinv, 1)
                dve.wait_ge(s_cinv, u + 1)
                heads = rows[:, 0, :, 0:OUT].rearrange("p t (h d) -> p t h d", d=HD)
                dve.tensor_tensor(heads, heads, cinv[:, t0:t0 + k, :].unsqueeze(3).to_broadcast([P, k, HEADS, HD]),
                                  ALU.mult).then_inc(s_att, 1)
                dve.wait_ge(s_att, u - NC + 1)
                for j, t in enumerate(tiles):
                    n = rows_of_tile(t)
                    dve.tensor_tensor(xn[0:n, t, :], xn[0:n, t, :], rows[0:n, 0, j, 0:OUT], ALU.add).then_inc(s_res, 1)

            def norm_factors(c, u):
                tiles = tiles_of_chunk(c)
                v = slice(tiles[0], tiles[-1] + 1)
                dve.wait_ge(s_std, u + 1)
                dve.reciprocal(rstd[:, v], std[:, v]).then_inc(s_rstd, 1)
                dve.wait_ge(s_rstd, u + 1)
                dve.scalar_tensor_tensor(shift[:, v], mv[:, v, 0], -1.0, rstd[:, v], ALU.mult, ALU.mult)\
                    .then_inc(s_shift, 1)

            whole, rest = E // GE, E % GE
            if rest:
                const(dve.tensor_reduce(low_g[0:NG, 0:1], dst_g[0:NG, 0:rest], AX.X, ALU.min))
                const(dve.tensor_reduce(low_g[0:whole, 1:2], dst_g[0:whole, rest:GE], AX.X, ALU.min))
                const(dve.tensor_tensor(low_g[0:whole, 0:1], low_g[0:whole, 0:1], low_g[0:whole, 1:2], ALU.min))
            else:
                const(dve.tensor_reduce(low_g[:, 0:1], dst_g[:, :], AX.X, ALU.min))
            wait_stage_a(dve)
            dve.tensor_scalar(low_row[:, :], iota_row[0:NG, :], 0.0, low_g[:, 0:1], ALU.mult, ALU.add).then_inc(s_low, 1)
            const(dve.memset(ablk[:, :, :], 0.0), "ablk")
            const(dve.memset(node[:, :, :], 0.0), "node clear")
            dve.wait_ge(s_xn, 48)
            for c in range(NC):
                residual(c, c, AW, mean)
                if c == 0:
                    dve.wait_ge(s_lowp, 1)
                    dve.tensor_copy(low_all[:, :], bank[1][:, 0:NG]).then_inc(s_lows, 1)
                    dve.wait_ge(s_lows, 1)
                    dve.tensor_scalar(to_b[:, :], low_all[:, :], p_f[:, :], None, ALU.add).then_inc(s_lows, 1)
                if c >= 1:
                    norm_factors(c - 1, c - 1)
            norm_factors(NC - 1, NC - 1)
            for g0, g1 in ((0, NB // BLOCKS_PER_GROUP), (NB // BLOCKS_PER_GROUP, NG)):
                b0_, k = g0 * BLOCKS_PER_GROUP, min(BLOCKS_PER_GROUP, NB - g0 * BLOCKS_PER_GROUP)
                if g1 > g0:
                    v = slice(b0_, b0_ + (g1 - g0) * k)
                    const(dve.tensor_tensor(dst_rel[:, v].rearrange("p (g k) -> p g k", k=k),
                                            dst_f[:, v].rearrange("p (g k) -> p g k", k=k),
                                            low_all[:, g0:g1].unsqueeze(2).to_broadcast([P, g1 - g0, k]),
                                            ALU.subtract))
            dve.wait_ge(s_hc, NT)
            const(dve.tensor_copy(node_p[:, 0], node[:, :, :]))
            const(dve.tensor_tensor(node_rest[:, :, :], node[:, :, :], node_p[:, 0], ALU.subtract))
            const(dve.tensor_copy(node_p[:, 1], node_rest[:, :, :]))
            const(dve.tensor_tensor(node_p[:, 2], node_rest[:, :, :], node_p[:, 1], ALU.subtract), "node")

            const(dve.tensor_reduce(top[:, 1:2], dst_rel[:, :], AX.X, ALU.max))

            if rows_of_block(NB - 1) < P:
                const(dve.memset(score[:, NB - 1, :], LOWEST))

            def one_hot(i):
                g, sides = b1_group(i), b1_sides(i)
                n, load = edges_of_group(g), i // REMG
                if i % REMG == 0:
                    dve.wait_ge(s_rem[load % 2], 16 * (load // 2 + 1))
                if i >= HOTR:
                    dve.wait_ge(s_O, i - HOTR + 1)
                a, v = (g % REMG) * GE, slice(sides[0], 2)
                dve.tensor_scalar(hot[:, i % HOTR, v, 0:n], rem[:, load % 2, v, a:a + n], p_f[:, :], None,
                                  ALU.is_equal).then_inc(s_hot, 1)

            def own_tile(i):
                m = len(b1_sides(i))
                if i >= 2:
                    dve.wait_ge(s_pick, i - 1)
                for run in same_rows(blocks_of_group(b1_group(i))):
                    n, b, k = rows_of_block(run[0]), run[0], len(run)
                    j = b % BLOCKS_PER_GROUP
                    last = dve.tensor_tensor(
                        own[0:n, i % 2, m * NT * j:m * NT * (j + k)].rearrange("p (b s t) -> p b s t", s=m, t=NT),
                        tile_row[0:n, :].unsqueeze(1).unsqueeze(1).to_broadcast([n, k, m, NT]),
                        tile_c[0:n, b:b + k, 2 - m:2].unsqueeze(3).to_broadcast([n, k, m, NT]), ALU.is_equal)
                last.then_inc(s_own, 1)

            def pick(i):
                m = len(b1_sides(i))
                dve.wait_ge(s_O, i + 1)
                dve.wait_ge(s_own, i + 1)
                if i >= 2:
                    dve.wait_ge(s_sc, i - 1)
                for k_bank, blocks in b1_banks(i):
                    for run in same_rows(blocks):
                        n, j, k = rows_of_block(run[0]), run[0] % BLOCKS_PER_GROUP, len(run)
                        a, u = (run[0] - blocks[0]) * m * TQ, k * m
                        last = dve.tensor_tensor(
                            picked[0:n, i % 2, m * TQ * j:m * TQ * (j + k)].rearrange("p (u t h) -> p u t h", t=NT, h=HEADS),
                            bank[k_bank][0:n, a:a + u * TQ].rearrange("p (u t h) -> p u t h", t=NT, h=HEADS),
                            own[0:n, i % 2, m * NT * j:m * NT * (j + k)].rearrange("p (u t) -> p u t", t=NT)
                            .unsqueeze(3).to_broadcast([n, u, NT, HEADS]), ALU.mult)
                last.then_inc(s_pick, 1)

            def edge_scores(i):
                m = len(b1_sides(i))
                dve.wait_ge(s_pick, i + 1)
                for run in same_rows(blocks_of_group(b1_group(i))):
                    n, b, k = rows_of_block(run[0]), run[0], len(run)
                    j = b % BLOCKS_PER_GROUP
                    last = dve.tensor_reduce(
                        score[0:n, b:b + k, :],
                        picked[0:n, i % 2, m * TQ * j:m * TQ * (j + k)].rearrange("p (b u h) -> p b h u", b=k, h=HEADS),
                        AX.X, ALU.add)
                last.then_inc(s_sc, 1)

            for i in range(-2, NG + 1):
                if i + 2 < NG:
                    one_hot(i + 2)
                if 0 <= i + 1 < NG:
                    own_tile(i + 1)
                if 0 <= i < NG:
                    pick(i)
                if i >= 1:
                    edge_scores(i - 1)
            dve.wait_ge(s_sc, NG)
            for g in range(HGR):
                dve.wait_ge(s_hg[g], group_arrivals(HGR, g))
            ring_blocks, behind = HGR * BLOCKS_PER_GROUP, (HGR + SCORED) * BLOCKS_PER_GROUP
            dve.tensor_tensor(score[:, 0:ring_blocks, :], score[:, 0:ring_blocks, :], Hg[:, :, OUT:BW],
                              ALU.add).then_inc(s_sc, 1)
            dve.wait_ge(s_sg, 16 * (behind - ring_blocks))
            dve.tensor_tensor(score[:, ring_blocks:behind, :], score[:, ring_blocks:behind, :], scored[:, :, :],
                              ALU.add).then_inc(s_sc, 1)
            b2 = [0]

            def step(ins, name=None):
                b2[0] += 1
                ins.then_inc(s_b2, 1)
                dve.wait_ge(s_b2, b2[0])
                B2[name] = b2[0]

            dve.wait_ge(s_sc, NG + 2)
            runs = same_rows(range(NB))
            for run in runs:
                n, b, k = rows_of_block(run[0]), run[0], len(run)
                v = score[0:n, b:b + k, :]
                step(dve.scalar_tensor_tensor(score[0:n, b:b + k, :], v, NEG_SLOPE, v, ALU.mult, ALU.max))
            for run in runs:
                n, b, k = rows_of_block(run[0]), run[0], len(run)
                step(dve.tensor_tensor(score[0:n, b:b + k, :], score[0:n, b:b + k, :],
                                       w_c[0:n, b:b + k].unsqueeze(2).to_broadcast([n, k, HEADS]), ALU.mult))
            step(dve.tensor_reduce(top[:, 0:1], score[:, :, :].rearrange("p b h -> p (b h)"), AX.X, ALU.max), "top")
            dve.wait_ge(s_top, 1)
            step(dve.tensor_scalar(neg_top[:, :], top_all[:, 0:1], -1.0, None, ALU.mult), "neg")
            step(dve.tensor_scalar(outside[:, :], top_all[0:1, 1:2], float(WB), None, ALU.is_ge), "outside")

            def weigh(o, rows, weights, n, k):
                return dve.tensor_tensor(o.rearrange("p k (h d) -> p k h d", d=HD),
                                         rows.rearrange("p k (h d) -> p k h d", d=HD),
                                         weights.unsqueeze(3).to_broadcast([n, k, HEADS, HD]), ALU.mult)

            dve.wait_ge(s_ex, 1)
            for g in range(NG):
                if g >= XBR:
                    dve.wait_ge(s_YB, g - XBR + 1)
                runs = same_rows(blocks_of_group(g))
                for run in runs:
                    n, b, k = rows_of_block(run[0]), run[0], len(run)
                    j = b % BLOCKS_PER_GROUP
                    last = dve.tensor_tensor(in_window[0:n, g % XBR, j:j + k, :],
                                             iota_row[0:n, :].unsqueeze(1).to_broadcast([n, k, WB]),
                                             dst_rel[0:n, b:b + k].unsqueeze(2).to_broadcast([n, k, WB]), ALU.is_equal)
                last.then_inc(s_win, 1)
                dve.wait_ge(s_hg[g % HGR], group_arrivals(HGR, g))
                for run in runs:
                    n, b, k = rows_of_block(run[0]), run[0], len(run)
                    j, r = b % BLOCKS_PER_GROUP, b % (HGR * BLOCKS_PER_GROUP)
                    last = weigh(xb[0:n, g % XBR, j:j + k, 0:OUT], Hg[0:n, r:r + k, 0:OUT], score[0:n, b:b + k, :], n, k)
                last.then_inc(s_xb, 1)
            with if_outside(dve):
                dve.wait_ge(s_YB, NG)
                for run in same_rows(range(NB)):
                    n, b, k = rows_of_block(run[0]), run[0], len(run)
                    last = dve.scalar_tensor_tensor(
                        score[0:n, b:b + k, :], dst_rel[0:n, b:b + k].unsqueeze(2).to_broadcast([n, k, HEADS]),
                        float(WB), score[0:n, b:b + k, :], ALU.is_ge, ALU.mult)
                last.then_inc(s_ukeep, 1)
                dve.wait_ge(s_ukeep, 1)
                for b in range(NB):
                    n = rows_of_block(b)
                    dve.wait_ge(s_ubc, 16 * (b + 1))
                    if b >= 1:
                        dve.wait_ge(s_up, b)
                        dve.wait_ge(s_us, 16 * b)
                    same = dst_u[0:n, 0:n]
                    dve.tensor_scalar(in_window[0:n, 0, 0, 0:n], same, dst_f[0:n, b:b + 1], None, ALU.is_equal)\
                        .then_inc(s_ueq, 1)
                    dve.scalar_tensor_tensor(eq_lowb[0:n, 0:n], same, dst_f[0:n, b:b + 1], lower[0:n, 0:n],
                                             ALU.is_equal, ALU.mult, accum_out=dup_u[0:n, :]).then_inc(s_udup, 1)
                    dve.wait_ge(s_udup, b + 1)
                    dve.tensor_scalar(to_f[0:n, 0:1], dst_f[0:n, b:b + 1], trash[0:n, :], None, ALU.subtract)\
                        .then_inc(s_utof, 1)
                    dve.wait_ge(s_utof, 2 * b + 1)
                    dve.scalar_tensor_tensor(to_f[0:n, 1:2], dup_u[0:n, :], 0.0, to_f[0:n, 0:1],
                                             ALU.is_equal, ALU.mult).then_inc(s_utof, 1)
                    dve.wait_ge(s_utof, 2 * b + 2)
                    dve.tensor_scalar(to_u[0:n, :], to_f[0:n, 1:2], trash[0:n, :], None, ALU.add).then_inc(s_uto, 1)
                    dve.wait_ge(s_uto, b + 1)
                    dve.wait_ge(s_ug, 16 * (b + 1))
                    dve.tensor_copy(xb[0:n, 0, 0, OUT:BW], score[0:n, b, :])
                    weigh(xb[0:n, 0, 0:1, 0:OUT], Hg[0:n, 0:1, 0:OUT], score[0:n, b:b + 1, :], n, 1).then_inc(s_ux, 1)

            for c in range(NC):
                residual(c, NC + c, BW, attention)
                if c >= 1:
                    norm_factors(c - 1, NC + c - 1)
            norm_factors(NC - 1, 2 * NC - 1)

        @block.sync
        def _(sp):
            sp.dma_start(W0f[:, :, :], W0.rearrange("(k p) n -> p k n", p=P)).then_inc(s_w0, 16)
            for i in range(PARTS):
                sp.dma_start(xTf[:, :, part_cols(i)],
                             xT[:, part_cols(i)].rearrange("(k p) n -> p k n", p=P)).then_inc(s_ldx[i], 16)
            sp.dma_start(b0b[:, :], b0.partition_broadcast(P)).then_inc(s_b0, 16)
            sp.dma_start(src_c[:, :], src_cols).then_inc(s_ldi, 16)
            sp.dma_start(dst_c[:, :], dst_cols).then_inc(s_ldi, 16)
            full = (E // GE) * GE
            sp.dma_start(dst_g[0:E // GE, :], dst_row[0:full].rearrange("(g e) -> g e", e=GE)).then_inc(s_ldi, 16)
            if full < E:
                sp.dma_start(dst_g[E // GE:NG, 0:E - full], dst_row[full:E].rearrange("(g e) -> g e", g=1))\
                  .then_inc(s_ldi, 16)
            sp.dma_start(idx_rows[:, 0, :], src_row.rearrange("(p j) -> p j", p=RQ)).then_inc(s_ldi, 16)
            sp.dma_start(idx_rows[:, 1, :], dst_row.rearrange("(p j) -> p j", p=RQ)).then_inc(s_ldi, 16)
            for c in range(C1):
                sp.dma_start(W1f[0:k1(c), c, :], W1[c * P:c * P + k1(c), :]).then_inc(s_ldw, 16)
            for m in range(C2):
                sp.dma_start(W2f[0:k2(m), m, :], W2[m * K2:m * K2 + k2(m), :]).then_inc(s_ldw, 16)
                sp.dma_start(b1c[0:k2(m), m:m + 1],
                             b1[m * K2:m * K2 + k2(m)].rearrange("(p a) -> p a", a=1)).then_inc(s_ldw, 16)
            sp.dma_start(W2f[k2(C2 - 1):k2(C2 - 1) + 1, C2 - 1, :],
                         b2.rearrange("(a n) -> a n", a=1)).then_inc(s_ldw, 16)
            sp.dma_start(Wgf[:, :], Wg).then_inc(s_ldw, 16)
            for t in range(NT):
                n = rows_of_tile(t)
                sp.wait_ge(s_n0a, t + 1)
                sp.dma_start(TA[t * P:t * P + n, :], stA[0:n, t % N0R, :]).then_inc(s_ta[t % N0R], 16)
                sp.wait_ge(s_n0b, t + 1)
                sp.dma_start(TB[t * P:t * P + n, :], stB[0:n, t % N0R, :]).then_inc(s_tb[t % N0R], 16)
            sp.wait_ge(s_dc, DC["rem"])
            sp.dma_start(RD.rearrange("k (p j) -> p k j", p=RQ), rem_b[:, :, :]).then_inc(s_rd, 16)
            wait_stage_n0(sp)

            def clear(table, width, half):
                rows = TR // P // 2
                tiles = slice(0, rows) if half == 0 else slice(rows, TR // P)
                k = tiles.stop - tiles.start
                sp.dma_start(table[tiles.start * P:tiles.stop * P, :].rearrange("(t p) d -> p t d", p=P),
                             zeros[:, 0:width].unsqueeze(1).to_broadcast([P, k, width])).then_inc(s_zero, 16)

            for g in range(NG):
                n = edges_of_group(g)
                if g >= 2:
                    sp.wait_ge(s_eh, g - 1)
                    sp.wait_ge(s_el, g - 1)
                sp.dma_start(ef[:, g % 2, 0:n], eT[:, g * GE:g * GE + n]).then_inc(s_e[g % 2], 16)
                if g >= 2:
                    sp.wait_ge(s_dup, g * BLOCKS_PER_GROUP - BLOCKS_PER_GROUP)
                sp.dma_start(bcast_i[:, g % 2, 0:n],
                             src_row[g * GE:g * GE + n].partition_broadcast(P)).then_inc(s_bc[g % 2], 16)
                for table, width in {2: [(t, AW) for t in accA], 8: [(accB, BW)]}.get(g, []):
                    clear(table, width, 0)
                for table, width in {3: [(t, AW) for t in accA], 9: [(accB, BW)]}.get(g, []):
                    clear(table, width, 1)
                if g == 6:
                    full = (N // P) * P
                    sp.dma_start(xn[:, 0:N // P, :], x[0:full, :].rearrange("(t p) d -> p t d", p=P)).then_inc(s_xn, 16)
                    sp.dma_start(xn[0:N - full, N // P, :], x[full:N, :]).then_inc(s_xn, 16)
                    sp.dma_start(w_c[:, :], w_cols).then_inc(s_xn, 16)
            wait_stage_a(sp)
            load_tables(sp, accA, AW, 0, range(TSR))
            sp.dma_start(Wc[:, :, 0:OUT], Wcat.rearrange("(k p) n -> p k n", p=P)).then_inc(s_ldc, 16)
            sp.dma_start(WcT[:, :, :], WcatT.rearrange("(k p) n -> p k n", p=P)).then_inc(s_ldc, 16)
            sp.wait_ge(s_dc, DC["ablk"])
            for h in range(HEADS):
                k, r = divmod(h * HD, P)
                sp.dma_start(ablk[r:r + HD, k, h:h + 1], a_src[h, :, :]).then_inc(s_ldc, 16)
                sp.dma_start(ablk[r:r + HD, k, HEADS + h:HEADS + h + 1], a_dst[h, :, :]).then_inc(s_ldc, 16)
            load_tables(sp, accA, AW, 0, range(TSR, NC))
            for t in range(NT):
                n = rows_of_tile(t)
                sp.wait_ge(s_hc, t + 1)
                sp.dma_start(HT[t * P:t * P + n, :], hst[0:n, t % 4, :]).then_inc(s_ht[t % 4], 16)
            sp.wait_ge(s_hc, NT)
            full = N // P
            sp.dma_start(ST[0:full * P, :].rearrange("(t p) h -> p t h", p=P),
                         node[:, 0, 0:full * HEADS].rearrange("p (t h) -> p t h", h=HEADS)).then_inc(s_st, 16)
            sp.dma_start(ST[full * P:N, :], node[0:N - full * P, 0, full * HEADS:TQ]).then_inc(s_st, 16)
            for i in range(NG // REMG):
                g = b1_group(i * REMG)
                a, n = g * GE, min(REMG * GE, E - g * GE)
                if i == 0:
                    sp.wait_ge(s_rd, 16)
                if i >= 2:
                    sp.wait_ge(s_hot, (i - 1) * REMG)
                sp.dma_start(rem[:, i % 2, :, 0:n], RD[:, a:a + n].partition_broadcast(P)).then_inc(s_rem[i % 2], 16)
            with if_outside(sp):
                for b in range(NB):
                    n = rows_of_block(b)
                    if b >= 1:
                        sp.wait_ge(s_udup, b)
                    sp.dma_start(dst_u[:, 0:n], dst_row[b * P:b * P + n].partition_broadcast(P)).then_inc(s_ubc, 16)
                sp.wait_ge(s_us, 16 * NB)
            sp.wait_ge(s_scB, 16 * NG)
            load_tables(sp, [accB], BW, NC, range(NC))
            for t in range(NT):
                n = rows_of_tile(t)
                sp.wait_ge(s_x1, NT + t + 1)
                sp.dma_start(out[t * P:t * P + n, :], xn[0:n, t, :]).then_inc(s_out, 16)
            sp.wait_ge(s_out, 16 * NT)

        @block.gpsimd
        def _(pool):
            pool.iota(iota_i[:, :], pattern=[[1, P]], base=0, channel_multiplier=0).then_inc(s_const, 1)
            pool.iota(p_i[:, :], pattern=[[0, 1]], base=0, channel_multiplier=1).then_inc(s_const, 1)
            wait_stage_n0(pool)

            def add_to_table(table, rows, sums):
                return pool.indirect_dma_start(
                    out=table, out_offset=bass.IndirectOffsetOnAxis(ap=rows, axis=0), in_=sums, in_offset=None,
                    bounds_check=TR - 1, oob_is_err=True, compute_op=ALU.add)

            def gather_a(b, g):
                n = rows_of_block(b)
                pool.indirect_dma_start(
                    out=GA[0:n, b % (GAR * BLOCKS_PER_GROUP), :], out_offset=None, in_=TA,
                    in_offset=bass.IndirectOffsetOnAxis(ap=src_c[0:n, b:b + 1], axis=0)).then_inc(s_ga[g % GAR], 16)

            def gather_b(b, g):
                n = rows_of_block(b)
                pool.indirect_dma_start(
                    out=GB[0:n, b % (GBR * BLOCKS_PER_GROUP), :], out_offset=None, in_=TB,
                    in_offset=bass.IndirectOffsetOnAxis(ap=dst_c[0:n, b:b + 1], axis=0)).then_inc(s_gb[g % GBR], 16)

            def scatter_a(b):
                n = rows_of_block(b)
                pool.wait_ge(s_Yc, b + 1)
                if b >= TABLES:
                    pool.wait_ge(s_scA[b % TABLES], 16 * (b // TABLES))
                add_to_table(accA[b % TABLES], to_a[0:n, b:b + 1], ystage[0:n, b % Y_RING, 0:AW])\
                    .then_inc(s_scA[b % TABLES], 16)

            for s in range(-3, NG + SUM_LAG):
                ahead, behind = s + 3, s - SUM_LAG
                if behind == 0:
                    pool.wait_ge(s_zero, 32 * TABLES)
                for j in range(BLOCKS_PER_GROUP):
                    if 0 <= ahead < NG and j < len(blocks_of_group(ahead)):
                        if j == 0 and ahead >= GAR:
                            pool.wait_ge(s_T, C1 * (ahead - GAR + 1))
                        if j == 0 and ahead >= GBR:
                            pool.wait_ge(s_add, ahead - GBR + 1)
                        gather_a(blocks_of_group(ahead)[j], ahead)
                        gather_b(blocks_of_group(ahead)[j], ahead)
                    if 0 <= behind < NG and j < len(blocks_of_group(behind)):
                        if j == 0:
                            pool.wait_ge(s_to, behind + 1)
                        scatter_a(blocks_of_group(behind)[j])

            def gather_h_rows(b, slot, landed):
                n = rows_of_block(b)
                pool.indirect_dma_start(
                    out=Hg[0:n, slot, :], out_offset=None, in_=HT,
                    in_offset=bass.IndirectOffsetOnAxis(ap=src_c[0:n, b:b + 1], axis=0)).then_inc(landed, 16)

            def gather_h(g):
                for b in blocks_of_group(g):
                    gather_h_rows(b, b % (HGR * BLOCKS_PER_GROUP), s_hg[g % HGR])

            def scatter_b(g):
                pool.wait_ge(s_YBc, g + 1)
                if g >= 1:
                    pool.wait_ge(s_scB, 16 * g)
                add_to_table(accB, to_b[:, g:g + 1], ystage[:, g % Y_RING, :]).then_inc(s_scB, 16)

            for k in range(4):
                pool.wait_ge(s_ht[k], ring_total(4, k, NT))
            for g in range(min(HGR, NG)):
                gather_h(g)
            pool.wait_ge(s_st, 32)
            for j in range(SCORED * BLOCKS_PER_GROUP):
                b = HGR * BLOCKS_PER_GROUP + j
                pool.indirect_dma_start(
                    out=scored[:, j, :], out_offset=None, in_=ST,
                    in_offset=bass.IndirectOffsetOnAxis(ap=src_c[:, b:b + 1], axis=0)).then_inc(s_sg, 16)
            pool.wait_ge(s_b2, B2["top"])
            pool.partition_all_reduce(top_all[:, :], top[:, :], P, bass.bass_isa.ReduceOp.max).then_inc(s_top, 1)
            pool.wait_ge(s_lows, 2)
            pool.wait_ge(s_zero, 32 * (TABLES + 1))
            scattered = 0
            for g in range(min(HGR, NG), NG):
                pool.wait_ge(s_xb, g - HGR + 1)
                for j, b in enumerate(blocks_of_group(g)):
                    gather_h_rows(b, b % (HGR * BLOCKS_PER_GROUP), s_hg[g % HGR])
                    if g > HGR and (j == 1 and g - scattered > LEAD or j == 3):
                        scatter_b(scattered)
                        scattered += 1
            for g in range(scattered, NG):
                scatter_b(g)
            with if_outside(pool):
                pool.wait_ge(s_scB, 16 * NG)
                for b in range(NB):
                    n = rows_of_block(b)
                    if b >= 1:
                        pool.wait_ge(s_ux, b)
                    else:
                        pool.wait_ge(s_xb, NG)
                    gather_h_rows(b, 0, s_ug)
                    pool.wait_ge(s_uto, b + 1)
                    pool.wait_ge(s_uy, b + 1)
                    if b >= 1:
                        pool.wait_ge(s_us, 16 * b)
                    add_to_table(accB, to_u[0:n, :], ystage[0:n, 0, :]).then_inc(s_us, 16)

        @block.tensor
        def _(pe):
            def split_product(o, lh, ll, rh, rl, first, last):
                pe.matmul(o, lh, rh, start=first, stop=False)
                pe.matmul(o, lh, rl, start=False, stop=False)
                return pe.matmul(o, ll, rh, start=False, stop=last)

            pe.wait_ge(s_wl, 1)
            for t in range(NT):
                n = rows_of_tile(t)
                pe.wait_ge(s_xl, part_of_tile[t] + 1)
                for half in range(2):
                    u = 2 * t + half
                    if u >= 8:
                        pe.wait_ge(s_n0a if half == 0 else s_n0b, t - 3)
                    o = bank[u % 8][0:n, 0:H0]
                    for k in range(DK):
                        last = split_product(o, xTh[:, k, t * P:t * P + n], xTl[:, k, t * P:t * P + n],
                                             W0h[:, half * DK + k, :], W0l[:, half * DK + k, :],
                                             k == 0, k == DK - 1)
                    last.then_inc(s_n0, 1)

            def transpose_chunk(g, c):
                u = C1 * g + c
                if c == 0:
                    pe.wait_ge(s_add, g + 1)
                if u >= 2:
                    pe.wait_ge(s_tanh1, u - 1)
                for j, b in enumerate(blocks_of_group(g)):
                    n = rows_of_block(b)
                    last = pe.transpose(PT[u % 2][0:k1(c), j * P:j * P + n],
                                        GA[0:n, b % (GAR * BLOCKS_PER_GROUP), c * P:c * P + k1(c)],
                                        ident[0:n, 0:n])
                last.then_inc(s_T, 1)

            def hidden2(g, m):
                u, n = C2 * g + m, edges_of_group(g)
                if u >= 2:
                    pe.wait_ge(s_tanh2, u - 1)
                o = PL1[u % 2][0:k2(m), 0:n]
                ms = slice(m * K2, m * K2 + k2(m))
                for c in range(F1):
                    if m == 0:
                        pe.wait_ge(s_h1l, C1 * g + c + 1)
                    split_product(o, W1h[:, c, ms], W1l[:, c, ms],
                                  h1h[:, g % 2, c, 0:n], h1l[:, g % 2, c, 0:n], c == 0, False)
                if m == 0:
                    pe.wait_ge(s_h1l, C1 * (g + 1))
                pe.matmul(o, W1s[:, ms], h1s[:, g % 2, 0:n], start=False, stop=True).then_inc(s_L1, 1)

            def gate_pair(g, q):
                pe.wait_ge(s_el, g + 1)
                if q >= 1:
                    pe.wait_ge(s_gate, q)
                for i, b in enumerate(blocks_of_pair(q)):
                    n, a = rows_of_block(b), (b - g * BLOCKS_PER_GROUP) * P
                    last = split_product(PG[0:n, i * OUT:(i + 1) * OUT], eh[:, g % 2, a:a + n],
                                         el[:, g % 2, a:a + n], Wgh[:, :], Wgl[:, :], True, True)
                last.then_inc(s_G, 1)

            def output_pair(g, q):
                if q >= 1:
                    pe.wait_ge(s_mul, q)
                for i, b in enumerate(blocks_of_pair(q)):
                    n, a = rows_of_block(b), (b - g * BLOCKS_PER_GROUP) * P
                    for m in range(C2):
                        if q % 2 == 0 and i == 0:
                            pe.wait_ge(s_h2l, C2 * g + m + 1)
                        k = k2(m) + (m == C2 - 1)
                        last = split_product(P2[0:n, i * OUT:(i + 1) * OUT], h2h[0:k, g % 2, m, a:a + n],
                                             h2l[0:k, g % 2, m, a:a + n], W2h[0:k, m, :], W2l[0:k, m, :],
                                             m == 0, m == C2 - 1)
                last.then_inc(s_L2, 1)

            def block_sums(b):
                n, q = rows_of_block(b), b // 2
                pe.wait_ge(s_ml, q + 1)
                pe.wait_ge(s_eq, b + 1)
                if b >= 2:
                    pe.wait_ge(s_Yc, b - 1)
                o = PY[b % 2][0:n, 0:AW]
                pe.matmul(o, eqA[0:n, b % EQR, 0:n], mh[0:n, q % 2, b % 2, :], start=True, stop=False)
                pe.matmul(o, eqA[0:n, b % EQR, 0:n], ml[0:n, q % 2, b % 2, :], start=False, stop=True)\
                    .then_inc(s_Y, 1)

            pe.wait_ge(s_n0a, NT)
            pe.wait_ge(s_n0b, NT)
            pe.wait_ge(s_wl, 4)
            pe.wait_ge(s_dc, DC["ones"])
            def pair_sums(g, i):
                for q in pairs(g)[i:i + 1]:
                    for b in blocks_of_pair(q):
                        block_sums(b)

            for s in range(-1, NG + 2):
                if 0 <= s < NG:
                    hidden2(s, 0)
                pair_sums(s - 2, 1)
                for q in pairs(s - 1)[0:1]:
                    gate_pair(s - 1, q)
                    output_pair(s - 1, q)
                if s + 1 < NG:
                    transpose_chunk(s + 1, 0)
                    transpose_chunk(s + 1, 1)
                if 0 <= s < NG:
                    hidden2(s, 1)
                for q in pairs(s - 1)[1:2]:
                    gate_pair(s - 1, q)
                    output_pair(s - 1, q)
                pair_sums(s - 1, 0)
                if s + 1 < NG:
                    transpose_chunk(s + 1, 2)
                    transpose_chunk(s + 1, 3)
                if 0 <= s < NG:
                    hidden2(s, 2)

            pe.wait_ge(s_Yc, NB)
            pe.wait_ge(s_ldc, 16 * (2 + 2 * HEADS))
            for i in range(DK):
                for k in range(DK):
                    last = pe.matmul(bank[0][:, i * 8:i * 8 + 2 * HEADS], WcT[:, k, i * P:(i + 1) * P],
                                     ablk[:, k, :], start=k == 0, stop=k == DK - 1)
            last.then_inc(s_wa, 1)
            pe.wait_ge(s_low, 1)
            pe.matmul(bank[1][:, 0:NG], low_row[:, :], ident[0:NG, 0:NG], start=True, stop=True).then_inc(s_lowp, 1)
            pe.wait_ge(s_wac, 1)
            pe.wait_ge(s_lows, 1)

            def x1_transposes(t):
                n = rows_of_tile(t)
                pe.wait_ge(s_x1, t + 1)
                if t >= 4:
                    pe.wait_ge(s_x1c, t - 3)
                for k in range(DK):
                    last = pe.transpose(bank[4 + t % 4][:, k * P:k * P + n], xn[0:n, t, k * P:(k + 1) * P],
                                        ident[0:n, 0:n])
                last.then_inc(s_x1t, 1)

            def node_products(t):
                n = rows_of_tile(t)
                pe.wait_ge(s_x1c, t + 1)
                if t >= 4:
                    pe.wait_ge(s_hc, t - 3)
                for k in range(DK):
                    last = pe.matmul(bank[t % 4][0:n, 0:OUT + 2 * HEADS], x1T[:, t % XTR, k, 0:n], Wc[:, k, :],
                                     start=k == 0, stop=k == DK - 1)
                last.then_inc(s_H, 1)

            for t in range(NT + 2):
                if t < NT:
                    x1_transposes(t)
                if t >= 2:
                    node_products(t - 2)

            pe.wait_ge(s_hc, NT)
            pe.wait_ge(s_dc, DC["node"])
            for i in range(NG):
                m = len(b1_sides(i))
                pe.wait_ge(s_hot, i + 1)
                if i >= 4:
                    pe.wait_ge(s_pick, i - 3)
                for k_bank, blocks in b1_banks(i):
                    for b in blocks:
                        n, j = rows_of_block(b), b % BLOCKS_PER_GROUP
                        for side in b1_sides(i):
                            a = ((b - blocks[0]) * m + side - (2 - m)) * TQ
                            for part in range(3):
                                last = pe.matmul(bank[k_bank][0:n, a:a + TQ],
                                                 hot[:, i % HOTR, side, j * P:j * P + n], node_p[:, part, side, :],
                                                 start=part == 0, stop=part == 2)
                last.then_inc(s_O, 1)

            pe.wait_ge(s_pick, NG)
            for g in range(NG):
                pe.wait_ge(s_win, g + 1)
                pe.wait_ge(s_xb, g + 1)
                pe.wait_ge(s_xe, g + 1)
                if g >= 8:
                    pe.wait_ge(s_YBc, g - 7)
                for j, b in enumerate(blocks_of_group(g)):
                    n = rows_of_block(b)
                    last = pe.matmul(bank[g % 8][0:WB, 0:BW], in_window[0:n, g % XBR, j, :],
                                     xb[0:n, g % XBR, j, :], start=j == 0, stop=b == blocks_of_group(g)[-1])
                last.then_inc(s_YB, 1)
            with if_outside(pe):
                pe.wait_ge(s_YBc, NG)
                for b in range(NB):
                    n = rows_of_block(b)
                    pe.wait_ge(s_ueq, b + 1)
                    pe.wait_ge(s_ux, b + 1)
                    if b >= 1:
                        pe.wait_ge(s_uy, b)
                    pe.matmul(bank[0][0:n, 0:BW], in_window[0:n, 0, 0, 0:n], xb[0:n, 0, 0, :],
                              start=True, stop=True).then_inc(s_up, 1)

        def rows_copy(act, copy, t):
            n = rows_of_tile(t)
            act.wait_ge(s_H, t + 1)
            if t >= 4:
                act.wait_ge(s_ht[t % 4], 16 * (t // 4))
            copy(node[0:n, :, t * HEADS:(t + 1) * HEADS],
                 bank[t % 4][0:n, OUT:OUT + 2 * HEADS].rearrange("p (s h) -> p s h", h=HEADS))
            copy(hst[0:n, t % 4, :], bank[t % 4][0:n, 0:BW]).then_inc(s_hc, 1)

        @block.scalar
        def _(act):
            def copy(o, i):
                return act.activation(o, i, ACT.Copy)

            act.wait_ge(s_w0, 16)
            copy(W0h[:, :, :], W0f[:, :, :]).then_inc(s_wh, 1)
            for i in range(PARTS):
                act.wait_ge(s_ldx[i], 16)
                copy(xTh[:, :, part_cols(i)], xTf[:, :, part_cols(i)]).then_inc(s_xh, 1)
            act.wait_ge(s_ldw, 16 * (C1 + 2 * C2 + 2))
            copy(W1h[:, :, :], W1f[:, 0:F1, :])
            act.wait_ge(s_dc, DC["stack"])
            for r in S1[0:2]:
                last = copy(W1s[r:r + R1, :], W1f[0:R1, F1, :])
            last.then_inc(s_wh, 1)
            for m in range(C2):
                k = k2(m) + (m == C2 - 1)
                last = copy(W2h[0:k, m, :], W2f[0:k, m, :])
            last.then_inc(s_wh, 1)
            copy(Wgh[:, :], Wgf[:, :]).then_inc(s_wh, 1)
            for t in range(NT):
                n = rows_of_tile(t)
                act.wait_ge(s_n0, 2 * t + 2)
                if t >= N0R:
                    act.wait_ge(s_tb[t % N0R], 16 * (t // N0R))
                copy(stB[0:n, t % N0R, :], bank[(2 * t + 1) % 8][0:n, 0:H0]).then_inc(s_n0b, 1)

            def tanh1(g, c):
                u, n = C1 * g + c, edges_of_group(g)
                act.wait_ge(s_T, u + 1)
                if g >= 1:
                    act.wait_ge(s_h1l, u - C1 + 1)
                act.activation(h1f[0:k1(c), c, 0:n], PT[u % 2][0:k1(c), 0:n], ACT.Tanh).then_inc(s_tanh1, 1)

            def h1_hi(g, c):
                u, n = C1 * g + c, edges_of_group(g)
                act.wait_ge(s_tanh1, u + 1)
                if g >= 2:
                    act.wait_ge(s_L1, C2 * (g - 1))
                if c < F1:
                    last = copy(h1h[:, g % 2, c, 0:n], h1f[:, c, 0:n])
                else:
                    for r in (S1[0], S1[2]):
                        last = copy(h1s[r:r + R1, g % 2, 0:n], h1f[0:R1, c, 0:n])
                last.then_inc(s_h1h, 1)

            def h1_chunks(g, chunks):
                for c in chunks:
                    tanh1(g, c)
                for c in chunks:
                    h1_hi(g, c)

            def tanh2(g, m):
                u, n = C2 * g + m, edges_of_group(g)
                act.wait_ge(s_L1, u + 1)
                if g >= 1:
                    act.wait_ge(s_h2l, u - C2 + 1)
                act.activation(h2f[0:k2(m), m, 0:n], PL1[u % 2][0:k2(m), 0:n], ACT.Tanh,
                               bias=b1c[0:k2(m), m:m + 1]).then_inc(s_tanh2, 1)
                act.wait_ge(s_tanh2, u + 1)
                if g >= 2:
                    act.wait_ge(s_L2, 2 * (g - 1))
                copy(h2h[0:k2(m), g % 2, m, 0:n], h2f[0:k2(m), m, 0:n]).then_inc(s_h2h, 1)

            def edge_hi(g):
                n = edges_of_group(g)
                act.wait_ge(s_e[g % 2], 16 * (g // 2 + 1))
                if g >= 2:
                    act.wait_ge(s_G, 2 * (g - 1))
                copy(eh[:, g % 2, 0:n], ef[:, g % 2, 0:n]).then_inc(s_eh, 1)

            def gate_copy(q):
                act.wait_ge(s_G, q + 1)
                if q >= 2:
                    act.wait_ge(s_mul, q - 1)
                k, n = len(blocks_of_pair(q)), rows_of_block(2 * q)
                copy(gate[0:n, q % 2, 0:k, :].rearrange("p i d -> p (i d)"), PG[0:n, 0:k * OUT]).then_inc(s_gate, 1)

            def gated_hi(q):
                act.wait_ge(s_mul, q + 1)
                if q >= 2:
                    act.wait_ge(s_Y, 2 * (q - 1))
                k, n = len(blocks_of_pair(q)), rows_of_block(2 * q)
                copy(mh[0:n, q % 2, 0:k, 0:OUT], mf[0:n, q % 2, 0:k, :]).then_inc(s_mh, 1)

            def sums_copy(b, banks, width, done, landed, tables, copied):
                n = rows_of_block(b)
                act.wait_ge(done, b + 1)
                if b >= Y_RING:
                    act.wait_ge(landed[b % tables], 16 * ((b - Y_RING) // tables + 1))
                copy(ystage[0:n, b % Y_RING, 0:width], banks[b % len(banks)][0:n, 0:width]).then_inc(copied, 1)

            wait_stage_n0(act)
            act.wait_ge(s_dc, DC["ones"])
            def pair_copies(g, i):
                for q in pairs(g)[i:i + 1]:
                    for b in blocks_of_pair(q):
                        sums_copy(b, PY, AW, s_Y, s_scA, TABLES, s_Yc)

            for s in range(-1, NG + 2):
                if 0 <= s - 1 < NG:
                    tanh2(s - 1, 2)
                if 0 <= s < NG:
                    tanh2(s, 0)
                    edge_hi(s)
                pair_copies(s - 2, 1)
                for q in pairs(s - 1)[0:1]:
                    gate_copy(q)
                    gated_hi(q)
                if s + 1 < NG:
                    h1_chunks(s + 1, (0, 1))
                if 0 <= s < NG:
                    tanh2(s, 1)
                for q in pairs(s - 1)[1:2]:
                    gate_copy(q)
                    gated_hi(q)
                pair_copies(s - 1, 0)
                if s + 1 < NG:
                    h1_chunks(s + 1, (2, 3))

            wait_stage_a(act)
            act.wait_ge(s_wa, 1)
            copy(Wc[:, :, OUT:OUT + 2 * HEADS],
                 bank[0][:, 0:DK * 8].rearrange("p (i c) -> p i c", c=8)).then_inc(s_wac, 1)
            act.wait_ge(s_dc, DC["node clear"])

            def deviations(c, u):
                tiles = tiles_of_chunk(c)
                v = slice(tiles[0], tiles[-1] + 1)
                act.wait_ge(s_mv, NT * (u // NC) + tiles[-1] + 1)
                act.activation(std[:, v], mv[:, v, 1], ACT.Sqrt, bias=eps[:, :]).then_inc(s_std, 1)

            def normalise(c, u):
                act.wait_ge(s_shift, u + 1)
                for t in tiles_of_chunk(c):
                    n = rows_of_tile(t)
                    act.activation(xn[0:n, t, :], xn[0:n, t, :], ACT.Identity, bias=shift[0:n, t:t + 1],
                                   scale=rstd[0:n, t:t + 1]).then_inc(s_x1, 1)

            deviations(0, 0)
            for t in range(NT):
                if t % TC == 0:
                    if t // TC + 1 < NC:
                        deviations(t // TC + 1, t // TC + 1)
                    normalise(t // TC, t // TC)
                n = rows_of_tile(t)
                act.wait_ge(s_x1t, t + 1)
                if t >= XTR:
                    act.wait_ge(s_H, t - XTR + 1)
                copy(x1T[:, t % XTR, :, 0:n],
                     bank[4 + t % 4][:, 0:DK * P].rearrange("p (k r) -> p k r", r=P)[:, :, 0:n]).then_inc(s_x1c, 1)
                if t >= 2:
                    rows_copy(act, copy, t - 2)
            rows_copy(act, copy, NT - 2)
            rows_copy(act, copy, NT - 1)

            act.wait_ge(s_b2, B2["neg"])
            act.activation(score[:, :, :], score[:, :, :], ACT.Exp, bias=neg_top[:, :]).then_inc(s_ex, 1)
            act.wait_ge(s_ex, 1)
            for g in range(NG + 2):
                if g < NG:
                    if g >= XBR:
                        act.wait_ge(s_YB, g - XBR + 1)
                    for run in same_rows(blocks_of_group(g)):
                        n, j, k = rows_of_block(run[0]), run[0] - g * BLOCKS_PER_GROUP, len(run)
                        last = copy(xb[0:n, g % XBR, j:j + k, OUT:BW], score[0:n, run[0]:run[0] + k, :])
                    last.then_inc(s_xe, 1)
                if g >= 2:
                    w = g - 2
                    act.wait_ge(s_YB, w + 1)
                    if w == 0:
                        for k in range(TABLES):
                            act.wait_ge(s_scA[k], ring_total(TABLES, k, NB))
                    if w >= Y_RING:
                        act.wait_ge(s_scB, 16 * (w - Y_RING + 1))
                    copy(ystage[:, w % Y_RING, :], bank[w % 8][:, 0:BW]).then_inc(s_YBc, 1)
            with if_outside(act):
                act.wait_ge(s_scB, 16 * NG)
                for b in range(NB):
                    n = rows_of_block(b)
                    act.wait_ge(s_up, b + 1)
                    if b >= 1:
                        act.wait_ge(s_us, 16 * b)
                    copy(ystage[0:n, 0, :], bank[0][0:n, 0:BW]).then_inc(s_uy, 1)
            for c in range(NC):
                deviations(c, NC + c)
                if c >= 1:
                    normalise(c - 1, NC + c - 1)
            normalise(NC - 1, 2 * NC - 1)


_INS = ["xT", "x", "src_cols", "dst_cols", "src_row", "dst_row", "eT", "w_cols", "W0", "b0", "W1", "b1",
        "W2", "b2", "Wg", "Wcat", "WcatT", "a_src", "a_dst"]


def kernel(x, src, dst, edge_attr_128, edge_weight, L0_gnn_W0, L0_gnn_b0, L0_gnn_W1, L0_gnn_b1, L0_gnn_W2,
           L0_gnn_b2, L0_gnn_Wg, L1_gnn_W, L1_gnn_a_src, L1_gnn_a_dst):
    import concourse.bacc as bacc
    from concourse.bass_utils import run_bass_kernel_spmd

    def columns(v):
        v = np.asarray(v)
        full = np.zeros(-(-v.shape[0] // P) * P, v.dtype)
        full[:v.shape[0]] = v
        return full.reshape(-1, P).T

    W = np.asarray(L1_gnn_W)
    Wcat = W.transpose(1, 0, 2).reshape(W.shape[1], -1)
    laid = dict(
        xT=np.asarray(x).T, x=x, src_cols=columns(src), dst_cols=columns(dst), src_row=src, dst_row=dst,
        eT=np.asarray(edge_attr_128).T, w_cols=columns(edge_weight), W0=L0_gnn_W0, b0=L0_gnn_b0,
        W1=L0_gnn_W1, b1=L0_gnn_b1, W2=L0_gnn_W2, b2=L0_gnn_b2, Wg=L0_gnn_Wg, Wcat=Wcat, WcatT=Wcat.T,
        a_src=L1_gnn_a_src, a_dst=L1_gnn_a_dst)
    nc = bacc.Bacc("TRN2", target_bir_lowering=False, num_devices=1)
    arrays, args = {}, []
    for name in _INS:
        a = np.ascontiguousarray(laid[name])
        arrays[f"in_{name}"] = a
        args.append(nc.dram_tensor(f"in_{name}", a.shape, mybir.dt.from_np(a.dtype), kind="ExternalInput").ap())
    args.append(nc.dram_tensor("out_0", np.asarray(x).shape, mybir.dt.float32, kind="ExternalOutput").ap())
    build_program(nc, *args)
    r = run_bass_kernel_spmd(nc, [arrays], core_ids=[0])
    return r.results[0]["out_0"]
```
